# Optimizing a Trainium2 kernel written in Bass

```python
import numpy as np
import jax
import jax.numpy as jnp

def _softmax(x, axis=-1):
    return jax.nn.softmax(x, axis=axis)

def _gelu(x):
    return jax.nn.gelu(x, approximate=True)

def _silu(x):
    return jax.nn.silu(x)

def _sigmoid(x):
    return jax.nn.sigmoid(x)

def _layernorm(x, axis=-1, eps=1e-05):
    m = jnp.mean(x, axis=axis, keepdims=True)
    v = jnp.var(x, axis=axis, keepdims=True)
    return (x - m) / jnp.sqrt(v + eps)

def _scatter_add(tgt, idx, src, axis=0):
    return tgt.at[idx].add(src)

def _segment_sum(src, seg, n):
    return jax.ops.segment_sum(src, seg, n)
kernel_name = 'mk_hybrid_d1_jaxref_r8_982b76'

def setup_inputs(seed: int=0):
    np.random.seed(seed)
    _w = jnp.asarray

    def _L0_attn_a_setup():
        import jax, jax.numpy as jnp
        import numpy as np
        EMBED_DIM = 128
        NUM_HEADS = 16
        HEAD_DIM = EMBED_DIM // NUM_HEADS
        ROPE_BASE = 10000.0

        def _rotary_emb(seq_len, dtype=jnp.float32):
            half = HEAD_DIM // 2
            inv_freq = 1.0 / ROPE_BASE ** (jnp.arange(half, dtype=dtype) / half)
            pos = jnp.arange(seq_len, dtype=dtype)
            sinusoid = pos[:, None] * inv_freq[None, :]
            sin = jnp.sin(sinusoid)
            cos = jnp.cos(sinusoid)
            sin = jnp.stack((sin, sin), axis=-1).reshape(seq_len, HEAD_DIM)
            cos = jnp.stack((cos, cos), axis=-1).reshape(seq_len, HEAD_DIM)
            return (sin, cos)

        def _rotate_half(x):
            x1 = x[..., ::2]
            x2 = x[..., 1::2]
            return jnp.stack((-x2, x1), axis=-1).reshape(x.shape)

        def _apply_rope(x, sin, cos):
            return x * cos[None, None] + _rotate_half(x) * sin[None, None]
        key = jax.random.key(seed)
        ks = jax.random.split(key, 9)
        B, S, E = (2, 256, EMBED_DIM)
        scale = 1.0 / np.sqrt(E)
        x = jax.random.normal(ks[0], (B, S, E), dtype=jnp.float32)
        Wq = jax.random.normal(ks[1], (E, E), dtype=jnp.float32) * scale
        bq = jnp.zeros((E,), dtype=jnp.float32)
        Wk = jax.random.normal(ks[2], (E, E), dtype=jnp.float32) * scale
        bk = jnp.zeros((E,), dtype=jnp.float32)
        Wv = jax.random.normal(ks[3], (E, E), dtype=jnp.float32) * scale
        bv = jnp.zeros((E,), dtype=jnp.float32)
        Wo = jax.random.normal(ks[4], (E, E), dtype=jnp.float32) * scale
        bo = jnp.zeros((E,), dtype=jnp.float32)
        return {'x': x, 'Wq': Wq, 'bq': bq, 'Wk': Wk, 'bk': bk, 'Wv': Wv, 'bv': bv, 'Wo': Wo, 'bo': bo}
    _L0_attn_a_in = _L0_attn_a_setup()

    def _L0_attn_b_setup():
        import jax, jax.numpy as jnp
        import numpy as np
        B, T, D = (4, 256, 128)
        NF = 64
        NB = 4
        FREQ_SCALE = 0.1

        def _w(k, shape, scale):
            return jax.random.normal(k, shape, jnp.float32) * scale

        def _ln(x, g, b):
            m = jnp.mean(x, axis=-1, keepdims=True)
            v = jnp.var(x, axis=-1, keepdims=True)
            return (x - m) * jax.lax.rsqrt(v + 1e-05) * g + b
        key = jax.random.key(seed)
        ks = jax.random.split(key, 16)
        d = D ** (-0.5)
        inp = {}
        inp['x'] = jax.random.normal(ks[0], (B, T, D), jnp.float32)
        inp['norm_g'] = jnp.ones((D,), jnp.float32)
        inp['norm_b'] = jnp.zeros((D,), jnp.float32)
        inp['Wconcept'] = _w(ks[1], (D, D), d)
        inp['bconcept'] = jnp.zeros((D,), jnp.float32)
        inp['Wcg'] = _w(ks[2], (D, D), d)
        inp['bcg'] = jnp.zeros((D,), jnp.float32)
        inp['Wfg'] = _w(ks[3], (NF, D), d)
        inp['bfg'] = jnp.zeros((NF,), jnp.float32)
        inp['Wtg'] = _w(ks[4], (1, D), d)
        inp['btg'] = jnp.zeros((1,), jnp.float32)
        inp['Wband'] = _w(ks[5], (NB, D), d)
        inp['bband'] = jnp.zeros((NB,), jnp.float32)
        inp['Wsp'] = _w(ks[6], (2 * NF, D), d)
        inp['freq_importance'] = jnp.ones((NF,), jnp.float32)
        inp['log_decay'] = (jnp.linspace(-3.0, -0.001, NF) + _w(ks[7], (NF,), 0.1)).astype(jnp.float32)
        inp['frequencies'] = (jnp.arange(NF, dtype=jnp.float32) / NF * 2.0 - 1.0) * 0.2
        inp['dt'] = jnp.ones((NF,), jnp.float32) * 0.5
        inp['Wgate'] = _w(ks[8], (D, D), d)
        inp['bgate'] = jnp.zeros((D,), jnp.float32)
        inp['Wfs'] = _w(ks[9], (D, 2 * NF), (2 * NF) ** (-0.5))
        inp['output_scale'] = jnp.ones((1,), jnp.float32) * 0.5
        inp['norm2_g'] = jnp.ones((D,), jnp.float32)
        inp['norm2_b'] = jnp.zeros((D,), jnp.float32)
        inp['W1'] = _w(ks[10], (4 * D, D), d)
        inp['b1'] = jnp.zeros((4 * D,), jnp.float32)
        inp['W2'] = _w(ks[11], (D, 4 * D), (4 * D) ** (-0.5))
        inp['b2'] = jnp.zeros((D,), jnp.float32)
        return inp
    _L0_attn_b_in = _L0_attn_b_setup()

    def _L0_ffn_setup():
        import jax, jax.numpy as jnp
        import numpy as np
        B, T, D = (2, 256, 128)
        E, DFF, TOPK = (8, 512, 2)
        TEMPERATURE = 1.0
        key = jax.random.key(seed)
        k_x, k_w1, k_w2, k_r = jax.random.split(key, 4)
        x = jax.random.normal(k_x, (B, T, D), dtype=jnp.float32)
        W1 = jax.random.normal(k_w1, (E, DFF, D), dtype=jnp.float32) * 0.02
        W2 = jax.random.normal(k_w2, (E, D, DFF), dtype=jnp.float32) * 0.02
        Wr = jax.random.normal(k_r, (E, D), dtype=jnp.float32) * 0.02
        return {'x': x, 'W1': W1, 'W2': W2, 'Wr': Wr}
    _L0_ffn_in = _L0_ffn_setup()
    _d = {'L0_attn_a_x': _L0_attn_a_in['x'], 'L0_attn_a_Wq': _L0_attn_a_in['Wq'], 'L0_attn_a_bq': _L0_attn_a_in['bq'], 'L0_attn_a_Wk': _L0_attn_a_in['Wk'], 'L0_attn_a_bk': _L0_attn_a_in['bk'], 'L0_attn_a_Wv': _L0_attn_a_in['Wv'], 'L0_attn_a_bv': _L0_attn_a_in['bv'], 'L0_attn_a_Wo': _L0_attn_a_in['Wo'], 'L0_attn_a_bo': _L0_attn_a_in['bo'], 'L0_attn_b_norm_g': _L0_attn_b_in['norm_g'], 'L0_attn_b_norm_b': _L0_attn_b_in['norm_b'], 'L0_attn_b_Wconcept': _L0_attn_b_in['Wconcept'], 'L0_attn_b_bconcept': _L0_attn_b_in['bconcept'], 'L0_attn_b_Wcg': _L0_attn_b_in['Wcg'], 'L0_attn_b_bcg': _L0_attn_b_in['bcg'], 'L0_attn_b_Wfg': _L0_attn_b_in['Wfg'], 'L0_attn_b_bfg': _L0_attn_b_in['bfg'], 'L0_attn_b_Wtg': _L0_attn_b_in['Wtg'], 'L0_attn_b_btg': _L0_attn_b_in['btg'], 'L0_attn_b_Wband': _L0_attn_b_in['Wband'], 'L0_attn_b_bband': _L0_attn_b_in['bband'], 'L0_attn_b_Wsp': _L0_attn_b_in['Wsp'], 'L0_attn_b_freq_importance': _L0_attn_b_in['freq_importance'], 'L0_attn_b_log_decay': _L0_attn_b_in['log_decay'], 'L0_attn_b_frequencies': _L0_attn_b_in['frequencies'], 'L0_attn_b_dt': _L0_attn_b_in['dt'], 'L0_attn_b_Wgate': _L0_attn_b_in['Wgate'], 'L0_attn_b_bgate': _L0_attn_b_in['bgate'], 'L0_attn_b_Wfs': _L0_attn_b_in['Wfs'], 'L0_attn_b_output_scale': _L0_attn_b_in['output_scale'], 'L0_attn_b_norm2_g': _L0_attn_b_in['norm2_g'], 'L0_attn_b_norm2_b': _L0_attn_b_in['norm2_b'], 'L0_attn_b_W1': _L0_attn_b_in['W1'], 'L0_attn_b_b1': _L0_attn_b_in['b1'], 'L0_attn_b_W2': _L0_attn_b_in['W2'], 'L0_attn_b_b2': _L0_attn_b_in['b2'], 'L0_ffn_W1': _L0_ffn_in['W1'], 'L0_ffn_W2': _L0_ffn_in['W2'], 'L0_ffn_Wr': _L0_ffn_in['Wr']}
    _x0 = _d['L0_attn_a_x']
    _d['L0_attn_a_x'] = jax.random.normal(jax.random.fold_in(jax.random.key(seed), 1), (4, 512, 128), dtype=_x0.dtype)
    del _x0
    return _d

def reference(L0_attn_a_x, L0_attn_a_Wq, L0_attn_a_bq, L0_attn_a_Wk, L0_attn_a_bk, L0_attn_a_Wv, L0_attn_a_bv, L0_attn_a_Wo, L0_attn_a_bo, L0_attn_b_norm_g, L0_attn_b_norm_b, L0_attn_b_Wconcept, L0_attn_b_bconcept, L0_attn_b_Wcg, L0_attn_b_bcg, L0_attn_b_Wfg, L0_attn_b_bfg, L0_attn_b_Wtg, L0_attn_b_btg, L0_attn_b_Wband, L0_attn_b_bband, L0_attn_b_Wsp, L0_attn_b_freq_importance, L0_attn_b_log_decay, L0_attn_b_frequencies, L0_attn_b_dt, L0_attn_b_Wgate, L0_attn_b_bgate, L0_attn_b_Wfs, L0_attn_b_output_scale, L0_attn_b_norm2_g, L0_attn_b_norm2_b, L0_attn_b_W1, L0_attn_b_b1, L0_attn_b_W2, L0_attn_b_b2, L0_ffn_W1, L0_ffn_W2, L0_ffn_Wr):

    def _L0_attn_a_ref(x, Wq, bq, Wk, bk, Wv, bv, Wo, bo):
        import jax, jax.numpy as jnp
        import numpy as np
        EMBED_DIM = 128
        NUM_HEADS = 16
        HEAD_DIM = EMBED_DIM // NUM_HEADS
        ROPE_BASE = 10000.0

        def _rotary_emb(seq_len, dtype=jnp.float32):
            half = HEAD_DIM // 2
            inv_freq = 1.0 / ROPE_BASE ** (jnp.arange(half, dtype=dtype) / half)
            pos = jnp.arange(seq_len, dtype=dtype)
            sinusoid = pos[:, None] * inv_freq[None, :]
            sin = jnp.sin(sinusoid)
            cos = jnp.cos(sinusoid)
            sin = jnp.stack((sin, sin), axis=-1).reshape(seq_len, HEAD_DIM)
            cos = jnp.stack((cos, cos), axis=-1).reshape(seq_len, HEAD_DIM)
            return (sin, cos)

        def _rotate_half(x):
            x1 = x[..., ::2]
            x2 = x[..., 1::2]
            return jnp.stack((-x2, x1), axis=-1).reshape(x.shape)

        def _apply_rope(x, sin, cos):
            return x * cos[None, None] + _rotate_half(x) * sin[None, None]
        B, S, E = x.shape
        H, D = (NUM_HEADS, HEAD_DIM)

        def proj(W, b):
            t = x @ W.T + b
            return t.reshape(B, S, H, D).transpose(0, 2, 1, 3)
        q = proj(Wq, bq)
        k = proj(Wk, bk)
        v = proj(Wv, bv)
        sin, cos = _rotary_emb(S, x.dtype)
        q = _apply_rope(q, sin, cos)
        k = _apply_rope(k, sin, cos)
        scores = jnp.einsum('bhqd,bhkd->bhqk', q, k) / jnp.sqrt(jnp.asarray(D, x.dtype))
        causal = jnp.tril(jnp.ones((S, S), dtype=bool))
        scores = jnp.where(causal[None, None], scores, -jnp.inf)
        weights = jax.nn.softmax(scores, axis=-1)
        out = jnp.einsum('bhqk,bhkd->bhqd', weights, v)
        out = out.transpose(0, 2, 1, 3).reshape(B, S, E)
        return out @ Wo.T + bo

    def _L0_attn_b_ref(x, norm_g, norm_b, Wconcept, bconcept, Wcg, bcg, Wfg, bfg, Wtg, btg, Wband, bband, Wsp, freq_importance, log_decay, frequencies, dt, Wgate, bgate, Wfs, output_scale, norm2_g, norm2_b, W1, b1, W2, b2):
        import jax, jax.numpy as jnp
        import numpy as np
        B, T, D = (4, 256, 128)
        NF = 64
        NB = 4
        FREQ_SCALE = 0.1

        def _w(k, shape, scale):
            return jax.random.normal(k, shape, jnp.float32) * scale

        def _ln(x, g, b):
            m = jnp.mean(x, axis=-1, keepdims=True)
            v = jnp.var(x, axis=-1, keepdims=True)
            return (x - m) * jax.lax.rsqrt(v + 1e-05) * g + b
        b_, t_, _ = x.shape
        nf = log_decay.shape[0]
        nb = Wband.shape[0]
        residual = x
        xn = _ln(x, norm_g, norm_b)
        concept = xn @ Wconcept.T + bconcept
        concept_preserved = concept * jax.nn.sigmoid(xn @ Wcg.T + bcg)
        forget_gates = jax.nn.sigmoid(xn @ Wfg.T + bfg)
        temporal_strength = jax.nn.sigmoid(xn @ Wtg.T + btg)
        band_strengths = jax.nn.sigmoid(xn @ Wband.T + bband)
        sp = xn @ Wsp.T
        u = jax.lax.complex(sp[..., :nf], sp[..., nf:]) * forget_gates
        decay = jax.nn.sigmoid(log_decay) * (jax.nn.softmax(freq_importance) * nf)
        omega = frequencies * FREQ_SCALE * (jax.nn.sigmoid(dt) * 2.0)
        rot = jax.lax.complex(jnp.cos(omega), jnp.sin(omega))
        A = decay * rot
        band_scale = jnp.repeat(band_strengths, nf // nb, axis=-1)
        A_exp = A * band_scale
        ones_first = jnp.ones((b_, 1, nf), A_exp.dtype)
        powers = jnp.cumprod(jnp.concatenate([ones_first, A_exp[:, :-1, :]], axis=1), axis=1)
        powers = powers * temporal_strength
        kernel = powers * rot
        n_fft = 2 * t_
        Uf = jnp.fft.fft(u, n=n_fft, axis=1)
        Kf = jnp.fft.fft(kernel, n=n_fft, axis=1)
        y = jnp.fft.ifft(Uf * Kf, n=n_fft, axis=1)[:, :t_, :]
        spectral_out = jnp.concatenate([y.real, y.imag], axis=-1)
        y_proj = spectral_out @ Wfs.T * output_scale
        gate_values = jax.nn.sigmoid(xn @ Wgate.T + bgate)
        y_gated = (y_proj * gate_values + concept_preserved) / 2.0
        x2 = residual + y_gated
        xn2 = _ln(x2, norm2_g, norm2_b)
        h = jax.nn.gelu(xn2 @ W1.T + b1, approximate=False)
        return x2 + h @ W2.T + b2

    def _L0_ffn_ref(x, W1, W2, Wr):
        import jax, jax.numpy as jnp
        import numpy as np
        B, T, D = (2, 256, 128)
        E, DFF, TOPK = (8, 512, 2)
        TEMPERATURE = 1.0
        logits = jnp.einsum('btd,ed->bte', x, Wr)
        probs = jax.nn.softmax(logits / TEMPERATURE, axis=-1)
        topk_vals, topk_idx = jax.lax.top_k(probs, TOPK)
        router_weights = topk_vals / topk_vals.sum(-1, keepdims=True)
        one_hot = jax.nn.one_hot(topk_idx, E, dtype=x.dtype)
        gate = jnp.einsum('btk,btke->bte', router_weights, one_hot)
        h = jax.nn.silu(jnp.einsum('btd,efd->btef', x, W1))
        y = jnp.einsum('btef,edf->bted', h, W2)
        out = jnp.einsum('bte,bted->btd', gate, y)
        return out
    x = L0_attn_a_x
    x = x + _L0_attn_a_ref(_layernorm(x, axis=-1), L0_attn_a_Wq, L0_attn_a_bq, L0_attn_a_Wk, L0_attn_a_bk, L0_attn_a_Wv, L0_attn_a_bv, L0_attn_a_Wo, L0_attn_a_bo)
    x = x + _L0_ffn_ref(_layernorm(x, axis=-1), L0_ffn_W1, L0_ffn_W2, L0_ffn_Wr)
    x = x + _L0_attn_b_ref(_layernorm(x, axis=-1), L0_attn_b_norm_g, L0_attn_b_norm_b, L0_attn_b_Wconcept, L0_attn_b_bconcept, L0_attn_b_Wcg, L0_attn_b_bcg, L0_attn_b_Wfg, L0_attn_b_bfg, L0_attn_b_Wtg, L0_attn_b_btg, L0_attn_b_Wband, L0_attn_b_bband, L0_attn_b_Wsp, L0_attn_b_freq_importance, L0_attn_b_log_decay, L0_attn_b_frequencies, L0_attn_b_dt, L0_attn_b_Wgate, L0_attn_b_bgate, L0_attn_b_Wfs, L0_attn_b_output_scale, L0_attn_b_norm2_g, L0_attn_b_norm2_b, L0_attn_b_W1, L0_attn_b_b1, L0_attn_b_W2, L0_attn_b_b2)
    x = x + _L0_ffn_ref(_layernorm(x, axis=-1), L0_ffn_W1, L0_ffn_W2, L0_ffn_Wr)
    return x

_drawn_inputs = setup_inputs


def setup_inputs(seed=0):
    import zlib

    import numpy as np

    out = dict(_drawn_inputs(seed))
    spreads = {'L0_attn_a_bq': (0.0, 0.505),
     'L0_attn_a_bk': (0.0, 0.679),
     'L0_attn_a_bv': (0.0, 0.1),
     'L0_attn_a_bo': (0.0, 0.1),
     'L0_attn_b_norm_g': (1.0, 0.2),
     'L0_attn_b_norm_b': (0.0, 0.463),
     'L0_attn_b_bconcept': (0.0, 0.557),
     'L0_attn_b_bcg': (0.0, 0.8),
     'L0_attn_b_bfg': (0.0, 0.8),
     'L0_attn_b_bband': (0.0, 2.0),
     'L0_attn_b_freq_importance': (1.0, 0.6),
     'L0_attn_b_dt': (0.5, 0.6),
     'L0_attn_b_bgate': (0.0, 0.8),
     'L0_attn_b_norm2_g': (1.0, 0.2),
     'L0_attn_b_norm2_b': (0.0, 0.272),
     'L0_attn_b_b1': (0.0, 0.287),
     'L0_attn_b_b2': (0.0, 0.1)}
    factors = {'L0_attn_b_Wfg': 5.175,
     'L0_attn_b_Wtg': 6.713,
     'L0_attn_b_Wband': 8.0,
     'L0_attn_b_log_decay': 8.0,
     'L0_attn_b_frequencies': 8.0,
     'L0_attn_b_Wgate': 5.319}
    for name, (base, spread) in spreads.items():
        noise = np.random.default_rng([zlib.crc32(name.encode()), seed]).standard_normal(out[name].shape)
        drawn = base * np.exp(spread * noise) if base else spread * noise
        out[name] = jnp.asarray(drawn.astype(out[name].dtype))
    for name, factor in factors.items():
        out[name] = (out[name] * factor).astype(out[name].dtype)
    return out
```

```python
from contextlib import ExitStack

import concourse.bass as bass
import numpy as np
from concourse import mybir

ALU = mybir.AluOpType
ACT = mybir.ActivationFunctionType
AX = mybir.AxisListType
F32 = mybir.dt.float32
BF16 = mybir.dt.bfloat16
I32 = mybir.dt.int32
U32 = mybir.dt.uint32

P = 128
B, S, D = 4, 512, 128
NT = B * S // P
TPB = S // P
EPS = 1e-5
ROUND = 12582912.0

NE, DFF = 8, 512
FT = DFF // P
NSLOT = (2 * NT * P + NE * (P - 1)) // P


class Chain:

    def __init__(self, engine, semaphore, base=0):
        self.engine, self.semaphore, self.count, self.base = engine, semaphore, 0, base

    def did(self, instruction):
        instruction.then_inc(self.semaphore, 1)
        self.count += 1
        return instruction

    def settle(self):
        self.engine.wait_ge(self.semaphore, self.base + self.count)

    def link(self, instruction):
        self.did(instruction)
        self.settle()


def phase_semaphores(nc, ctx, tag):
    made = []

    def clear():
        nc.clear_and_free_semaphores(made)
        nc.all_engine_barrier()

    def sem(name):
        made.append(nc.alloc_semaphore(f"{tag}_{name}"))
        return made[-1]

    ctx.callback(clear)
    return sem


def bc(ap, n, at):
    shape = list(ap.shape)
    return ap.unsqueeze(at).to_broadcast(shape[:at] + [n] + shape[at:])


def active(tile):
    return not isinstance(tile, int) or 0 <= tile < NSLOT


def later(tile, n):
    return not isinstance(tile, int) or tile >= n


def over_slot_tiles(engine, step, steps=NSLOT + 3):
    for i in range(8):
        step(i, i % 4)
    with engine.Fori(8, 36, 4) as i:
        for u in range(4):
            step(i + u, u)
    for i in range(36, steps):
        step(i, i % 4)


def moe(nc, tag, ps, x, c, w1t, w2t, wrt, xs_dram, ys_dram, s_weights):
    with ExitStack() as ctx:
        def sb(name, shape, dt=F32):
            return ctx.enter_context(nc.sbuf_tensor(f"{tag}_{name}", shape, dt))

        sem = phase_semaphores(nc, ctx, tag)

        stats = sb("stats", [P, NT, 6])
        mv = sb("mv", [P, NT, 2])
        std = sb("std", [P, NT])
        rstd = sb("rstd", [P, NT])
        xn = sb("xn", [P, NT, D])
        xnT = sb("xnT", [P, NT // 4, 4 * P])
        lg = sb("lg", [P, NT, NE])
        work = sb("work", [P, NT, NE])
        work2 = sb("work2", [P, NT, NE])
        oh1 = sb("oh1", [P, NT, NE])
        oh2 = sb("oh2", [P, NT, NE])
        top1 = sb("top1", [P, NT])
        top2 = sb("top2", [P, NT])
        pm = sb("pm", [P, NT])
        chosen = sb("chosen", [P, NE, NT], BF16)
        total = sb("total", [P, NE, NT])
        upto = sb("upto", [P, NE, NT])
        pos = sb("pos", [P, NE, NT])
        tiles = sb("tiles", [P, NE])
        tiles_upto = sb("tiles_upto", [P, NE])
        start = sb("start", [P, NE])
        slot = sb("slot", [P, 2, NT])
        sloti = sb("sloti", [P, 2, NT], U32)
        ecmp = sb("ecmp", [1, NSLOT, NE])
        eid = sb("eid", [1, NSLOT])
        eoff = sb("eoff", [1, NSLOT], I32)
        gap = sb("gap", [P, NT])
        egap = sb("egap", [P, NT])
        gate = sb("gate", [P, 2, NT])
        xg = sb("xg", [P, 4, D])
        xgT = sb("xgT", [P, 2, P])
        h = sb("h", [P, 2, DFF])
        hT = sb("hT", [P, 2, DFF])
        y = sb("y", [P, 4, D])
        ytok = sb("ytok", [P, 2, NT, D])

        s_chain = sem("dve_chain")
        s_mv = sem("moments")
        s_std = sem("std")
        s_xn = sem("xn")
        s_t = sem("xnT_psum")
        s_tc = sem("xnT_copied")
        s_lg = sem("logits")
        s_ch = sem("chosen_bf16")
        s_rank = sem("ranks")
        s_gap = sem("gap")
        s_egap = sem("exp_gap")
        s_slot = sem("slots")
        s_off = sem("expert_offsets")
        s_zero = sem("zeroed")
        s_scat = [sem(f"scattered{k}") for k in range(2)]
        s_xg = [sem(f"xg_loaded{i}") for i in range(4)]
        s_gate = sem("gates")
        s_x = sem("xgT_psum")
        s_xc = sem("xgT_copied")
        s_m1 = sem("hidden_psum")
        s_h = sem("hidden")
        s_ht = sem("hiddenT_psum")
        s_htc = sem("hiddenT_copied")
        s_m2 = sem("y_psum")
        s_y = sem("y_copied")
        s_st = [sem(f"y_stored{i}") for i in range(4)]
        s_gat = [[sem(f"gathered{k}_{g}") for g in range(NT // 4)] for k in range(2)]
        s_out = sem("combined")

        psX = lambda i: ps[:, i % 2, 0:P]
        psH = lambda i: ps[:, 2 + i % 2, :]
        psHT = lambda i: ps[:, 4 + i % 2, :]
        psY = lambda i: ps[:, 6 + i % 2, 0:D]

        block = ctx.enter_context(nc.Block())

        @block.vector
        def _(dve):
            ch = Chain(dve, s_chain)
            for t in range(NT):
                ch.did(dve.bn_stats(stats[:, t, :], x[:, t, :]))
            ch.settle()
            for t in range(NT):
                dve.bn_aggr(mv[:, t, :], stats[:, t, :]).then_inc(s_mv, 1)
            dve.wait_ge(s_std, 1)
            ch.link(dve.reciprocal(rstd[:, :], std[:, :]))
            for t in range(NT):
                dve.tensor_scalar(xn[:, t, :], x[:, t, :], mv[:, t, 0:1], rstd[:, t:t + 1],
                                  ALU.subtract, ALU.mult).then_inc(s_xn, 1)
            dve.wait_ge(s_lg, 1)
            ch.link(dve.tensor_copy(lg[:, :, :], ps[:, 2, 0:NT * NE].rearrange("p (t e) -> p t e", e=NE)))

            def first_max(src, top, oh):
                ch.link(dve.tensor_reduce(top[:, :], src[:, :, :], AX.X, ALU.max))
                ch.link(dve.tensor_tensor(work2[:, :, :], src[:, :, :], bc(top[:, :], NE, 2), ALU.is_equal))
                ch.link(dve.tensor_tensor(work2[:, :, :], work2[:, :, :], bc(c["falling"][:, :], NT, 1), ALU.mult))
                ch.link(dve.tensor_reduce(pm[:, :], work2[:, :, :], AX.X, ALU.max))
                ch.link(dve.tensor_tensor(oh[:, :, :], work2[:, :, :], bc(pm[:, :], NE, 2), ALU.is_equal))

            first_max(lg, top1, oh1)
            ch.link(dve.scalar_tensor_tensor(work[:, :, :], oh1[:, :, :], -3e38, lg[:, :, :], ALU.mult, ALU.add))
            first_max(work, top2, oh2)
            dve.tensor_tensor(chosen[:, :, :].rearrange("p e t -> p t e"), oh1[:, :, :], oh2[:, :, :],
                              ALU.add).then_inc(s_ch, 1)
            dve.tensor_tensor(gap[:, :], top2[:, :], top1[:, :], ALU.subtract).then_inc(s_gap, 1)
            dve.wait_ge(s_rank, 1)
            ranks = ps[:, 3, 0:NT * NE].rearrange("p (e t) -> p e t", t=NT)
            ch.link(dve.tensor_copy(total[:, :, :], ps[:, 4, 0:NT * NE].rearrange("p (e t) -> p e t", t=NT)))
            flat = lambda a: a[:, :, :].rearrange("p a b -> p (a b)")
            ch.link(dve.tensor_tensor_scan(flat(upto), c["restart"][:, :], flat(total), 0.0, ALU.mult, ALU.add))
            ch.link(dve.tensor_scalar(tiles[:, :], upto[:, :, NT - 1], 1.0 / P, 0.49609375, ALU.mult, ALU.add))
            ch.link(dve.tensor_scalar(tiles[:, :], tiles[:, :], ROUND, ROUND, ALU.add, ALU.subtract))
            ch.link(dve.tensor_tensor_scan(tiles_upto[:, :], c["one"][:, 0:NE], tiles[:, :], 0.0, ALU.mult, ALU.add))
            ch.link(dve.tensor_tensor(ecmp[:, :, :], bc(tiles_upto[0:1, :], NSLOT, 1),
                                      bc(c["slot_tile"][0:1, :], NE, 2), ALU.is_le))
            ch.link(dve.tensor_reduce(eid[:, :], ecmp[:, :, :], AX.X, ALU.add))
            dve.tensor_scalar(eoff[:, :], eid[:, :], float(NE - 1), float(DFF), ALU.min, ALU.mult).then_inc(s_off, 1)
            ch.link(dve.tensor_tensor(start[:, :], tiles_upto[:, :], tiles[:, :], ALU.subtract))
            ch.link(dve.tensor_tensor(pos[:, :, :], upto[:, :, :], total[:, :, :], ALU.subtract))
            ch.link(dve.tensor_tensor(pos[:, :, :], ranks, pos[:, :, :], ALU.add))
            ch.link(dve.scalar_tensor_tensor(pos[:, :, :], bc(start[:, :], NT, 2), float(P), pos[:, :, :],
                                             ALU.mult, ALU.add))
            for k, oh in enumerate((oh1, oh2)):
                ch.link(dve.tensor_tensor(work[:, :, :], oh[:, :, :], pos[:, :, :].rearrange("p e t -> p t e"), ALU.mult))
                ch.link(dve.tensor_reduce(slot[:, k, :], work[:, :, :], AX.X, ALU.add))
                dve.tensor_copy(sloti[:, k, :], slot[:, k, :]).then_inc(s_slot, 1)
            dve.wait_ge(s_egap, 1)
            ch.link(dve.tensor_scalar(gap[:, :], egap[:, :], 1.0, None, ALU.add))
            ch.link(dve.reciprocal(gate[:, 0, :], gap[:, :]))
            ch.link(dve.tensor_tensor(gate[:, 1, :], gate[:, 0, :], egap[:, :], ALU.mult))

            def step(i, u):
                j = i - 2
                if active(j):
                    dve.wait_ge(s_ht, j + 1)
                    if later(j, 2):
                        dve.wait_ge(s_m2, j - 1)
                    dve.tensor_copy(hT[:, u % 2, :], psHT(u)).then_inc(s_htc, 1)
                j = i - 3
                if active(j):
                    q = (u - 3) % 4
                    dve.wait_ge(s_m2, j + 1)
                    if later(j, 4):
                        dve.wait_ge(s_st[q], (j - q) * 4)
                    dve.tensor_copy(y[:, q, :], psY(u + 1)).then_inc(s_y, 1)

            over_slot_tiles(dve, step)
            for k in range(2):
                for t in range(NT):
                    dve.wait_ge(s_gat[k][t // 4], 64)
                    if k:
                        dve.wait_ge(s_out, t + 1)
                    dve.scalar_tensor_tensor(x[:, t, :], ytok[:, k, t, :], gate[:, k, t:t + 1], x[:, t, :],
                                             ALU.mult, ALU.add).then_inc(s_out, 1)

        @block.scalar
        def _(act):
            act.wait_ge(s_mv, NT)
            act.activation(std[:, :], mv[:, :, 1], ACT.Sqrt, bias=c["eps"][:, 0:1]).then_inc(s_std, 1)
            for g in range(NT // 4):
                act.wait_ge(s_t, g + 1)
                act.activation(xnT[:, g, :], ps[:, g % 2, :], ACT.Copy).then_inc(s_tc, 1)
            act.wait_ge(s_gap, 1)
            act.activation(egap[:, :], gap[:, :], ACT.Exp).then_inc(s_egap, 1)

            def step(i, u):
                j = i
                if active(j):
                    act.wait_ge(s_x, j + 1)
                    if later(j, 2):
                        act.wait_ge(s_m1, j - 1)
                    act.activation(xgT[:, u % 2, :], psX(u), ACT.Copy).then_inc(s_xc, 1)
                j = i - 1
                if active(j):
                    act.wait_ge(s_m1, j + 1)
                    if later(j, 2):
                        act.wait_ge(s_ht, j - 1)
                    act.activation(h[:, (u + 1) % 2, :], psH(u + 1), ACT.Silu).then_inc(s_h, 1)

            over_slot_tiles(act, step)

        @block.tensor
        def _(pe):
            pe.wait_ge(s_weights, 48)

            def transposed(g):
                pe.wait_ge(s_xn, 4 * g + 4)
                if g >= 2:
                    pe.wait_ge(s_tc, g - 1)
                for t in range(4):
                    mm = pe.transpose(ps[:, g % 2, t * P:(t + 1) * P], xn[:, 4 * g + t, :], c["ident"][:, :])
                mm.then_inc(s_t, 1)

            def logits(g):
                pe.wait_ge(s_tc, g + 1)
                for t in range(4 * g, 4 * g + 4):
                    mm = pe.matmul(ps[:, 2, t * NE:(t + 1) * NE], xnT[:, g, (t % 4) * P:(t % 4 + 1) * P],
                                   wrt[:, :], start=True, stop=True)
                if g == NT // 4 - 1:
                    mm.then_inc(s_lg, 1)

            transposed(0)
            for g in range(1, NT // 4):
                transposed(g)
                logits(g - 1)
            logits(NT // 4 - 1)
            pe.wait_ge(s_ch, 1)
            chosen_flat = chosen[:, :, :].rearrange("p e t -> p (e t)")
            pe.matmul(ps[:, 3, 0:NT * NE], c["before_bf"][:, :], chosen_flat, start=True, stop=True)
            pe.matmul(ps[:, 4, 0:NT * NE], c["ones_bf"][:, :], chosen_flat, start=True,
                      stop=True).then_inc(s_rank, 1)
            pe.wait_ge(s_off, 1)
            pe.wait_ge(s_slot, 2)

            def step(i, u):
                j = i
                if active(j):
                    pe.wait_ge(s_xg[u], (j - u) * 4 + 16)
                    if later(j, 2):
                        pe.wait_ge(s_xc, j - 1)
                    pe.transpose(psX(u), xg[:, u, :], c["ident"][:, :]).then_inc(s_x, 1)
                j = i - 1
                if active(j):
                    w = pe.value_load(eoff[0:1, bass.ds(j, 1)], min_val=0, max_val=(NE - 1) * DFF)
                    pe.wait_ge(s_xc, j + 1)
                    if later(j, 2):
                        pe.wait_ge(s_h, j - 1)
                    pe.matmul(psH(u + 1), xgT[:, (u + 1) % 2, :], w1t[:, bass.ds(w, DFF)],
                              start=True, stop=True).then_inc(s_m1, 1)
                j = i - 2
                if active(j):
                    pe.wait_ge(s_h, j + 1)
                    if later(j, 2):
                        pe.wait_ge(s_htc, j - 1)
                    for f in range(FT):
                        mm = pe.transpose(psHT(u)[:, f * P:(f + 1) * P], h[:, u % 2, f * P:(f + 1) * P],
                                          c["ident"][:, :])
                    mm.then_inc(s_ht, 1)
                j = i - 3
                if active(j):
                    w = pe.value_load(eoff[0:1, bass.ds(j, 1)], min_val=0, max_val=(NE - 1) * DFF)
                    pe.wait_ge(s_htc, j + 1)
                    if later(j, 2):
                        pe.wait_ge(s_y, j - 1)
                    for f in range(FT):
                        mm = pe.matmul(psY(u + 1), hT[:, (u + 1) % 2, f * P:(f + 1) * P],
                                       w2t[:, bass.ds(w + f * P, P)], start=(f == 0), stop=(f == FT - 1))
                    mm.then_inc(s_m2, 1)

            over_slot_tiles(pe, step)

        @block.sync
        def _(sp):
            sp.dma_start(xs_dram.rearrange("(n p) d -> p n d", p=P), bc(c["zero"][:, :], NSLOT, 1)).then_inc(s_zero, 16)
            sp.wait_ge(s_scat[0], 16 * NT)
            sp.wait_ge(s_scat[1], 16 * NT)

            def step(i, u):
                if not active(i):
                    return
                if later(i, 4):
                    sp.wait_ge(s_x, i - 3)
                sp.dma_start(xg[:, u, :], xs_dram[bass.ds(i * P, P), :]).then_inc(s_xg[u], 16)

            over_slot_tiles(sp, step)

        @block.gpsimd
        def _(pool):
            pool.wait_ge(s_zero, 16)
            pool.wait_ge(s_xn, NT)
            for k in range(2):
                pool.wait_ge(s_slot, k + 1)
                for t in range(NT):
                    pool.indirect_dma_start(xs_dram[:, :], bass.IndirectOffsetOnAxis(sloti[:, k, t:t + 1], 0),
                                            xn[:, t, :], None).then_inc(s_scat[k], 16)

            def step(i, u):
                j = i - 4
                if active(j):
                    pool.wait_ge(s_y, j + 1)
                    pool.dma_start(ys_dram[bass.ds(j * P, P), :], y[:, u, :]).then_inc(s_st[u], 16)

            over_slot_tiles(pool, step, NSLOT + 4)
            for q in range(4):
                pool.wait_ge(s_st[q], 16 * ((NSLOT - q + 3) // 4))
            for k in range(2):
                for t in range(NT):
                    pool.indirect_dma_start(ytok[:, k, t, :], None, ys_dram[:, :],
                                            bass.IndirectOffsetOnAxis(sloti[:, k, t:t + 1], 0)).then_inc(s_gat[k][t // 4], 16)


NH, DH = 16, 8
HG = 4
UNITS = B * NH // HG
GROUPS = NH // HG
KROWS = 128
MROW = 9 * DH
MASKED = -1e30
WIDTH = [S - P * k for k in range(TPB)]


def attention_prepare(nc, ps, x, c, w, parts_dram, hatq, hatk, vall, s_hat):
    with ExitStack() as ctx:
        def sb(name, shape, dt=F32):
            return ctx.enter_context(nc.sbuf_tensor(f"ap_{name}", shape, dt))

        sem = phase_semaphores(nc, ctx, "ap")

        stats = sb("stats", [P, NT, 6])
        mv = sb("mv", [P, NT, 2])
        std = sb("std", [P, NT])
        rstd = sb("rstd", [P, NT])
        xn = sb("xn", [P, 2, TPB, D])
        xnT = sb("xnT", [P, 2, S])
        rot = sb("rot", [P, 2, 2, S])
        full = sb("full", [P, 2, 2, S])
        rest = sb("rest", [P, 2, S])
        part = sb("part", [P, 2, 2, 3, S], BF16)
        s_chain = sem("dve_chain")
        s_mv, s_std, s_xn, s_t, s_tc = sem("moments"), sem("std"), sem("xn"), sem("xnT_psum"), sem("xnT_copied")
        s_pr, s_rot, s_v = sem("projected"), sem("rotated"), sem("values")
        s_full, s_p0, s_r1, s_p1, s_p2 = (sem(f"split{k}") for k in range(5))
        s_store = [sem("parts_stored0"), sem("parts_stored1")]
        s_bo = sem("bo_added")
        block = ctx.enter_context(nc.Block())

        @block.vector
        def _(dve):
            ch = Chain(dve, s_chain)
            for t in range(NT):
                ch.did(dve.bn_stats(stats[:, t, :], x[:, t, :]))
            ch.settle()
            for t in range(NT):
                dve.bn_aggr(mv[:, t, :], stats[:, t, :]).then_inc(s_mv, 1)
            dve.wait_ge(s_std, 1)
            ch.link(dve.reciprocal(rstd[:, :], std[:, :]))

            def normalize(b):
                if b >= 2:
                    dve.wait_ge(s_t, b - 1)
                for t in range(TPB):
                    n = b * TPB + t
                    dve.tensor_scalar(xn[:, b % 2, t, :], x[:, n, :], mv[:, n, 0:1], rstd[:, n:n + 1],
                                      ALU.subtract, ALU.mult).then_inc(s_xn, 1)

            normalize(0)
            for b in range(B):
                if b + 1 < B:
                    normalize(b + 1)
                for m in range(4):
                    dve.wait_ge(s_pr, 5 * b + m + 1)
                    if m % 2 == 0 and b:
                        dve.wait_ge(s_full, 2 * (b - 1) + m // 2 + 1)
                    dve.scalar_tensor_tensor(rot[:, m // 2, m % 2, :], ps[:, 2 + m, :], w["qk_bias"][:, m:m + 1],
                                             w["rotary"][:, m, :], ALU.add, ALU.mult).then_inc(s_rot, 1)
                dve.wait_ge(s_pr, 5 * b + 5)
                dve.tensor_tensor(vall[:, b * TPB:(b + 1) * TPB, :],
                                  ps[:, 6 + b % 2, :].rearrange("p (t d) -> p t d", d=D),
                                  bc(w["bv"][:, :], TPB, 1), ALU.add).then_inc(s_v, 1)
                for k in range(2):
                    dve.wait_ge(s_full, 2 * b + k + 1)
                    dve.wait_ge(s_p0, 2 * b + k + 1)
                    if b:
                        dve.wait_ge(s_p2, 2 * (b - 1) + k + 1)
                    dve.tensor_tensor(rest[:, k, :], full[:, b % 2, k, :], part[:, b % 2, k, 0, :],
                                      ALU.subtract).then_inc(s_r1, 1)

        @block.scalar
        def _(act):
            act.wait_ge(s_mv, NT)
            act.activation(std[:, :], mv[:, :, 1], ACT.Sqrt, bias=c["eps"][:, 0:1]).then_inc(s_std, 1)

            def copy_xnT(b):
                act.wait_ge(s_t, b + 1)
                if b >= 2:
                    act.wait_ge(s_pr, 5 * (b - 1))
                act.activation(xnT[:, b % 2, :], ps[:, b % 2, :], ACT.Copy).then_inc(s_tc, 1)

            copy_xnT(0)
            for b in range(B):
                if b + 1 < B:
                    copy_xnT(b + 1)
                if b >= 2:
                    act.wait_ge(s_store[b % 2], 32 * (b // 2))
                for k in range(2):
                    act.wait_ge(s_full, 2 * b + k + 1)
                    act.activation(part[:, b % 2, k, 0, :], full[:, b % 2, k, :], ACT.Copy).then_inc(s_p0, 1)
                for k in range(2):
                    act.wait_ge(s_r1, 2 * b + k + 1)
                    act.activation(part[:, b % 2, k, 1, :], rest[:, k, :], ACT.Copy).then_inc(s_p1, 1)

        @block.gpsimd
        def _(pool):
            for b in range(B):
                for k in range(2):
                    pool.wait_ge(s_rot, 4 * b + 2 * k + 2)
                    if b >= 2:
                        pool.wait_ge(s_p0, 2 * (b - 2) + k + 1)
                        pool.wait_ge(s_r1, 2 * (b - 2) + k + 1)
                    pool.tensor_tensor(full[:, b % 2, k, :], rot[:, k, 0, :], rot[:, k, 1, :], ALU.add).then_inc(s_full, 1)
                if b >= 2:
                    pool.wait_ge(s_store[b % 2], 32 * (b // 2))
                for k in range(2):
                    pool.wait_ge(s_p1, 2 * b + k + 1)
                    pool.wait_ge(s_r1, 2 * b + k + 1)
                    pool.tensor_tensor(part[:, b % 2, k, 2, :], rest[:, k, :], part[:, b % 2, k, 1, :],
                                       ALU.subtract).then_inc(s_p2, 1)
                pool.wait_ge(s_xn, TPB * (b + 1))
                pool.tensor_tensor(x[:, b * TPB:(b + 1) * TPB, :], x[:, b * TPB:(b + 1) * TPB, :],
                                   bc(w["bo"][:, :], TPB, 1), ALU.add).then_inc(s_bo, 1)

        @block.tensor
        def _(pe):
            def transposed(b):
                pe.wait_ge(s_xn, TPB * (b + 1))
                if b >= 2:
                    pe.wait_ge(s_tc, b - 1)
                for t in range(TPB):
                    mm = pe.transpose(ps[:, b % 2, t * P:(t + 1) * P], xn[:, b % 2, t, :], c["ident"][:, :])
                mm.then_inc(s_t, 1)

            transposed(0)
            for b in range(B):
                if b + 1 < B:
                    transposed(b + 1)
                pe.wait_ge(s_tc, b + 1)
                for m in range(4):
                    if b:
                        pe.wait_ge(s_rot, 4 * (b - 1) + m + 1)
                    pe.matmul(ps[:, 2 + m, :], w["wqk"][:, m * P:(m + 1) * P], xnT[:, b % 2, :],
                              start=True, stop=True).then_inc(s_pr, 1)
                if b >= 2:
                    pe.wait_ge(s_v, b - 1)
                for t in range(TPB):
                    mm = pe.matmul(ps[:, 6 + b % 2, t * P:(t + 1) * P], xnT[:, b % 2, t * P:(t + 1) * P],
                                   w["wv"][:, :], start=True, stop=True)
                mm.then_inc(s_pr, 1)

        @block.sync
        def _(sp):
            for par in range(2):
                for hat, name in ((hatq, "zero_rows"), (hatk, "one_rows")):
                    sp.dma_start(hat[MROW:KROWS, par, :, :], bc(c[name][:, :], NH, 1)).then_inc(s_hat["fill"], 16)
            for b in range(B):
                for k in range(2):
                    sp.wait_ge(s_p2, 2 * b + k + 1)
                    sp.dma_start(parts_dram[b, k].rearrange("i p t -> p i t"),
                                 part[:, b % 2, k, :, :]).then_inc(s_store[b % 2], 16)
                sp.wait_ge(s_store[b % 2], 32 * (b // 2 + 1))
                if b == 0:
                    load_hats(sp, b, parts_dram, hatq, hatk, s_hat)


def load_hats(sp, b, parts_dram, hatq, hatk, s_hat):
    for i in range(3):
        for j in range(3):
            rows = slice((3 * i + j) * DH, (3 * i + j + 1) * DH)
            for hat, k, p in ((hatq, 0, i), (hatk, 1, j)):
                sp.dma_start(hat[rows, b % 2, :, :],
                             parts_dram[b, k, p].rearrange("(h d) t -> d h t", d=DH)).then_inc(s_hat[b % 2], 16)


def attention(nc, ps, x, c, w, parts_dram, hatq, hatk, vall, s_hat):
    with ExitStack() as ctx:
        def sb(name, shape, dt=F32):
            return ctx.enter_context(nc.sbuf_tensor(f"at_{name}", shape, dt))

        sem = phase_semaphores(nc, ctx, "at")

        pt = sb("pt", [P, 2, 5, 2 * S])
        vext = sb("vext", [P, TPB, NH, 32])
        mx = sb("mx", [P, 2, TPB, HG])
        mh = sb("mh", [P, TPB, 2, HG], BF16)
        mT = sb("mT", [2 * HG, S], BF16)
        oT = sb("oT", [P, GROUPS, S])
        rden = sb("rden", [P, NH])
        on = sb("on", [P, TPB, D])
        onT = sb("onT", [P, S])
        s_a, s_ar, s_b, s_e = sem("a_psum"), sem("a_max"), sem("b_psum"), sem("b_exp")
        s_pv, s_oc, s_vx, s_fill = sem("pv"), sem("o_copied"), sem("values_placed"), sem("fill")
        s_mh, s_mt, s_mc, s_md = sem("max_negated"), sem("maxT_psum"), sem("maxT_copied"), sem("max_rows")
        s_tt, s_tc, s_rd = sem("tail_psum"), sem("tail_read"), sem("denominator")
        s_causal = sem("causal")
        s_zr = [sem("rows_zeroed0"), sem("rows_zeroed1")]
        bankA = lambda k: ps[:, k % 2, :]
        chunkB = lambda k: ps[:, 2 + 2 * (k % 2):4 + 2 * (k % 2), :]
        bankO, bankM = ps[:, 6, :], ps[:, 7, :]
        block = ctx.enter_context(nc.Block())

        A_CHUNKS = [[(h, 3, 0)] for h in range(4)] + [[(h, 2, 0), (h, 0, 384)] for h in range(4)] \
            + [[(h, 1, 0), (h + 1, 1, 256)] for h in (0, 2)]
        B_CHUNKS = [[(h, 0, 0, 0), (h, 1, 1, 0), (h, 3, 1, 384)] for h in range(4)] \
            + [[(h, 2, h // 2, 256 * (h % 2)) for h in range(4)]]
        PLACE = {(h, k): (n, S * bank + col) for n, ch in enumerate(B_CHUNKS) for h, k, bank, col in ch}

        def tail_rounds_before(u):
            b, g = (u - 1) // GROUPS, (u - 1) % GROUPS
            return max(0, 6 * (b - 1) + (0, 0, 4, 6)[g])

        TAIL = {(1, 1): 0, (1, 2): 1, (1, 3): 2, (1, 4): 3, (2, 1): 4, (2, 2): 5}

        @block.tensor
        def _(pe):
            def a_chunk(u, k):
                b, g, n = u // GROUPS, u % GROUPS, 10 * u + k
                if u % GROUPS == 0 and k == 0:
                    pe.wait_ge(s_hat[b % 2], 288 * (b // 2 + 1))
                    if b >= 2:
                        pe.wait_ge(s_zr[b % 2], 16 * (b // 2))
                if n >= 2:
                    pe.wait_ge(s_ar, n - 1)
                for h, t, col in A_CHUNKS[k]:
                    hh = HG * g + h
                    pe.matmul(bankA(n)[:, col:col + (t + 1) * P], hatq[0:KROWS, b % 2, hh, t * P:(t + 1) * P],
                              hatk[0:KROWS, b % 2, hh, 0:(t + 1) * P], start=True, stop=True)
                    mm = pe.matmul(bankA(n)[:, col + t * P:col + (t + 1) * P], c["ident_bf"][:, :],
                                   c["mask_q_bf"][:, :], start=False, stop=True, skip_group_check=True)
                mm.then_inc(s_a, 1)

            def b_chunk(u, k):
                b, g, n = u // GROUPS, u % GROUPS, 5 * u + k
                if k == 0:
                    pe.wait_ge(s_md, 32 * (u + 1))
                if n >= 2:
                    pe.wait_ge(s_e, n - 1)
                for h, t, bank, col in B_CHUNKS[k]:
                    hh = HG * g + h
                    mm = pe.matmul(chunkB(n)[:, bank, col:col + WIDTH[t]], hatk[0:KROWS, b % 2, hh, t * P:(t + 1) * P],
                              hatq[0:KROWS, b % 2, hh, t * P:S], start=True, stop=True)
                mm.then_inc(s_b, 1)

            def pv(u, t):
                b, g = u // GROUPS, u % GROUPS
                if t == 0:
                    pe.wait_ge(s_e, 5 * (u + 1))
                    pe.wait_ge(s_causal, 4 * (u + 1))
                    if u:
                        pe.wait_ge(s_oc, u)
                    if g == 0:
                        pe.wait_ge(s_vx, b + 1)
                for h in range(HG):
                    chunk, col = PLACE[h, t]
                    mm = pe.matmul(bankO[32 * h:32 * h + 32, t * P:S], vext[:, t, HG * g + h, :],
                                   pt[:, u % 2, chunk, col:col + WIDTH[t]],
                                   start=(t == 0), stop=(t == TPB - 1), skip_group_check=True)
                if t == TPB - 1:
                    mm.then_inc(s_pv, 1)

            def max_rows(u):
                pe.wait_ge(s_mh, 2 * (u + 1))
                if u:
                    pe.wait_ge(s_mc, u)
                if u > GROUPS + 1 and tail_rounds_before(u):
                    pe.wait_ge(s_tc, tail_rounds_before(u))
                out = bankM.bitcast(BF16)
                for t in range(TPB):
                    mm = pe.transpose(out[0:2 * HG, t * P:(t + 1) * P],
                                      mh[:, t, :, :].rearrange("p i h -> p (i h)"), c["ident_bf"][:, :])
                mm.then_inc(s_mt, 1)

            def tail(b, r):
                if r == 0:
                    pe.wait_ge(s_oc, GROUPS * (b + 1))
                if r in (0, 4):
                    pe.wait_ge(s_mc, min(GROUPS * (b + 1) + 3 + r // 4, UNITS))
                if b or r:
                    pe.wait_ge(s_tc, 6 * b + r)
                for t in range(TPB):
                    dst = bankM[:, t * P:(t + 1) * P]
                    if r < 4:
                        mm = pe.transpose(dst, oT[:, t, r * P:(r + 1) * P], c["ident"][:, :])
                    elif r == 4:
                        mm = pe.transpose(dst, on[:, t, :], c["ident"][:, :])
                    else:
                        mm = pe.matmul(dst, onT[:, t * P:(t + 1) * P], w["wo"][:, :], start=True, stop=True)
                mm.then_inc(s_tt, 1)

            pe.wait_ge(s_fill, 2)
            pe.wait_ge(s_hat["fill"], 64)
            for u in range(2):
                for k in range(10):
                    a_chunk(u, k)
                    if (u, k) == (1, 1):
                        max_rows(0)
            for u in range(UNITS):
                b, g = u // GROUPS, u % GROUPS
                for k in range(5):
                    if u + 2 < UNITS:
                        a_chunk(u + 2, 2 * k)
                    b_chunk(u, k)
                    if u + 2 < UNITS:
                        a_chunk(u + 2, 2 * k + 1)
                    if u and k < TPB:
                        pv(u - 1, k)
                    if k == 0 and u + 1 < UNITS:
                        max_rows(u + 1)
                    if b and (g, k) in TAIL:
                        tail(b - 1, TAIL[g, k])
            for t in range(TPB):
                pv(UNITS - 1, t)
            for r in range(6):
                tail(B - 1, r)

        @block.vector
        def _(dve):
            def a_max(u, k):
                n = 10 * u + k
                dve.wait_ge(s_a, n + 1)
                if k == 0 and u >= 2:
                    dve.wait_ge(s_mh, 2 * (u - 1))
                chunk = A_CHUNKS[k]
                if len(chunk) == 2 and chunk[0][1] == chunk[1][1]:
                    h, t, _ = chunk[0]
                    m = dve.tensor_reduce(mx[:, u % 2, t, h:h + 2], bankA(n).rearrange("p (h c) -> p h c", h=2),
                                          AX.X, ALU.max)
                else:
                    for h, t, col in chunk:
                        m = dve.tensor_reduce(mx[:, u % 2, t, h:h + 1], bankA(n)[:, col:col + (t + 1) * P],
                                              AX.X, ALU.max)
                m.then_inc(s_ar, 1)

            def negate(u):
                dve.wait_ge(s_ar, 10 * (u + 1))
                if u:
                    dve.wait_ge(s_mt, u)
                dve.tensor_scalar(mh[:, :, 0, :], mx[:, u % 2, :, :], -1.0, None, ALU.mult).then_inc(s_mh, 1)
                dve.wait_ge(s_mh, 2 * u + 1)
                dve.scalar_tensor_tensor(mh[:, :, 1, :], mx[:, u % 2, :, :], -1.0, mh[:, :, 0, :],
                                         ALU.mult, ALU.subtract).then_inc(s_mh, 1)

            def rows_copy(u):
                dve.wait_ge(s_mt, u + 1)
                if u:
                    dve.wait_ge(s_md, 32 * u)
                dve.tensor_copy(mT[:, :], bankM.bitcast(BF16)[0:2 * HG, 0:S]).then_inc(s_mc, 1)

            def place_values(b):
                if b:
                    dve.wait_ge(s_pv, GROUPS * b)
                src = vall[:, b * TPB:(b + 1) * TPB, :].rearrange("p t (h d) -> p (t h) d", d=DH)
                dve.tensor_copy(vext[:, :, :, 0:DH].rearrange("p t h d -> p (t h) d"), src).then_inc(s_vx, 1)

            def tail(b, r):
                dve.wait_ge(s_tt, 6 * b + r + 1)
                if r < 4:
                    o = bankM.rearrange("p (h c) -> p h c", c=32)
                    if b or r:
                        dve.wait_ge(s_tc, 6 * b + r)
                    dve.reciprocal(rden[:, :], o[:, :, DH]).then_inc(s_rd, 1)
                    dve.wait_ge(s_rd, 4 * b + r + 1)
                    dve.tensor_tensor(on[:, r, :].rearrange("p (h d) -> p h d", d=DH), o[:, :, 0:DH],
                                      bc(rden[:, :], DH, 2), ALU.mult).then_inc(s_tc, 1)
                elif r == 4:
                    dve.tensor_copy(onT[:, :], bankM).then_inc(s_tc, 1)
                else:
                    xb = x[:, b * TPB:(b + 1) * TPB, :]
                    dve.tensor_tensor(xb, bankM.rearrange("p (t d) -> p t d", d=D), xb, ALU.add).then_inc(s_tc, 1)

            dve.memset(vext[:, :, :, :], 0.0).then_inc(s_fill, 1)
            dve.wait_ge(s_fill, 1)
            dve.memset(vext[:, :, :, DH:DH + 1], 1.0).then_inc(s_fill, 1)
            place_values(0)
            for u in range(2):
                for k in range(10):
                    a_max(u, k)
                negate(u)
                if u == 0:
                    rows_copy(u)
            for u in range(UNITS):
                b, g = u // GROUPS, u % GROUPS
                for k in range(5):
                    if u + 2 < UNITS:
                        a_max(u + 2, 2 * k)
                        a_max(u + 2, 2 * k + 1)
                    if k == 0 and u + 1 < UNITS:
                        rows_copy(u + 1)
                    if g == 0 and b and k == 3:
                        place_values(b)
                    if b and (g, k) in TAIL:
                        tail(b - 1, TAIL[g, k])
                if u + 2 < UNITS:
                    negate(u + 2)
            for r in range(6):
                tail(B - 1, r)

        @block.scalar
        def _(act):
            def o_copy(u):
                b, g = u // GROUPS, u % GROUPS
                act.wait_ge(s_pv, u + 1)
                if g == 0 and b:
                    act.wait_ge(s_tt, 6 * (b - 1) + 4)
                act.activation(oT[:, g, :], bankO, ACT.Copy).then_inc(s_oc, 1)

            for u in range(UNITS):
                for k in range(5):
                    n = 5 * u + k
                    act.wait_ge(s_b, n + 1)
                    if k == 0 and u >= 2:
                        act.wait_ge(s_pv, u - 1)
                    act.activation(pt[:, u % 2, k, :], chunkB(n).rearrange("p a b -> p (a b)"), ACT.Exp).then_inc(s_e, 1)
                    if k == 4 and u:
                        o_copy(u - 1)
            o_copy(UNITS - 1)

        @block.gpsimd
        def _(pool):
            for u in range(UNITS):
                pool.wait_ge(s_e, 5 * (u + 1))
                for t in range(TPB):
                    chunk, col = PLACE[0, t]
                    if t == 2:
                        own = pt[:, u % 2, chunk, :].rearrange("p (h q) -> p h q", h=HG)[:, :, 0:P]
                    else:
                        own = pt[:, u % 2, 0:HG, col:col + P]
                    pool.affine_select(out=own, in_=own, compare_op=ALU.is_ge, fill=0.0, base=0,
                                       pattern=[[0, HG], [1, P]], channel_multiplier=-1).then_inc(s_causal, 1)

        @block.sync
        def _(sp):
            load_hats(sp, 1, parts_dram, hatq, hatk, s_hat)
            for u in range(UNITS):
                b, g = u // GROUPS, u % GROUPS
                if g == 2 and b + 1 in range(2, B):
                    sp.wait_ge(s_b, 5 * GROUPS * b)
                    sp.dma_start(hatq[MROW:MROW + 2, (b + 1) % 2, :, :], bc(c["zero_rows"][0:2, :], NH, 1)).then_inc(s_zr[(b + 1) % 2], 16)
                    load_hats(sp, b + 1, parts_dram, hatq, hatk, s_hat)
                sp.wait_ge(s_mc, u + 1)
                for i in range(2):
                    sp.dma_start(hatq[MROW + i:MROW + i + 1, b % 2, HG * g:HG * (g + 1), :],
                                 mT[HG * i:HG * (i + 1), :]).then_inc(s_md, 16)


NF, NB = 64, 4
NFFT = 2 * S
R4 = 4
HALF = S // 2
KT = HALF // P
COLS = 2 * B * NF
TWO_PI = 2 * np.pi
TWO_PI_HI = 6.28125
PI_BELOW = 3.1415925


class Moments:

    def __init__(self, sb, sem, tag):
        self.stats = sb(f"{tag}_stats", [P, NT, 6])
        self.mv = sb(f"{tag}_mv", [P, NT, 2])
        self.std = sb(f"{tag}_std", [P, NT])
        self.rstd = sb(f"{tag}_rstd", [P, NT])
        self.s_st, self.s_mv, self.s_std = sem(f"{tag}_stats"), sem(f"{tag}_moments"), sem(f"{tag}_std")
        self.s_rstd, self.s_done = sem(f"{tag}_rstd"), sem(f"{tag}_normalized")

    def moments(self, dve, src):
        for t in range(NT):
            dve.bn_stats(self.stats[:, t, :], src[:, t, :]).then_inc(self.s_st, 1)
        dve.wait_ge(self.s_st, NT)
        for t in range(NT):
            dve.bn_aggr(self.mv[:, t, :], self.stats[:, t, :]).then_inc(self.s_mv, 1)

    def root(self, act, eps):
        act.wait_ge(self.s_mv, NT)
        act.activation(self.std[:, :], self.mv[:, :, 1], ACT.Sqrt, bias=eps[:, 0:1]).then_inc(self.s_std, 1)

    def normalize(self, dve, dst, src):
        dve.wait_ge(self.s_std, 1)
        dve.reciprocal(self.rstd[:, :], self.std[:, :]).then_inc(self.s_rstd, 1)
        dve.wait_ge(self.s_rstd, 1)
        for t in range(NT):
            dve.tensor_scalar(dst[:, t, :], src[:, t, :], self.mv[:, t, 0:1], self.rstd[:, t:t + 1],
                              ALU.subtract, ALU.mult).then_inc(self.s_done, 1)


def ssm_project(nc, ps, x, c, w, xi, xh, cp, gate, U, K):
    with ExitStack() as ctx:
        def sb(name, shape, dt=F32):
            return ctx.enter_context(nc.sbuf_tensor(f"sp_{name}", shape, dt))

        sem = phase_semaphores(nc, ctx, "sp")

        outer, inner = Moments(sb, sem, "outer"), Moments(sb, sem, "inner")
        xnT = sb("xnT", [P, 2, S])
        sig = sb("sig", [P, 4, S])
        uT = sb("uT", [P, 2, S])
        pw = sb("pw", [P, S + 1])
        k1 = sb("k1", [P, S])
        kT = sb("kT", [P, 2, S])
        turn = sb("turn", [P, S])
        angle = sb("angle", [P, S])
        wave = sb("wave", [P, S])
        col = sb("col", [P, 12])
        erow = sb("erow", [P, NF])
        s_ch, s_a = sem("dve_chain"), sem("act_setup")
        s_dv, s_red, s_wave = sem("dve_setup"), sem("angles"), sem("wave")
        s_t, s_tc = sem("xnT_psum"), sem("xnT_copied")
        s_pr = sem("projected")
        s_sig = sem("sigmoids")
        s_u, s_cp, s_k1, s_k = sem("inputs"), sem("concept"), sem("kernel_size"), sem("kernel")
        s_ut, s_kt, s_uc, s_kc = sem("inputs_psum"), sem("kernel_psum"), sem("inputs_copied"), sem("kernel_copied")
        PROJ = [("fg", 2), ("band", 3), ("tg", 4), ("sp", 5), ("concept", 6), ("cg", 7), ("gate", 2)]
        block = ctx.enter_context(nc.Block())

        @block.vector
        def _(dve):
            ch = Chain(dve, s_ch)
            outer.moments(dve, x)
            ch.link(dve.tensor_reduce(col[:, 0:1], w["fi_row"][:, :], AX.X, ALU.max))
            dve.tensor_scalar(col[:, 1:2], col[:, 0:1], -1.0, None, ALU.mult).then_inc(s_dv, 1)
            outer.normalize(dve, xi, x)
            dve.wait_ge(outer.s_done, NT)
            inner.moments(dve, xi)
            dve.wait_ge(s_a, 4)
            ch.link(dve.reciprocal(col[:, 6:7], col[:, 2:3]))
            ch.link(dve.tensor_scalar(col[:, 7:8], col[:, 3:4], col[:, 6:7], float(NF), ALU.mult, ALU.mult))
            ch.link(dve.tensor_tensor(col[:, 8:9], col[:, 7:8], col[:, 4:5], ALU.mult))
            ch.link(dve.tensor_scalar(col[:, 9:10], w["freq"][:, 0:1], 0.1, None, ALU.mult))
            ch.link(dve.tensor_scalar(col[:, 10:11], col[:, 5:6], col[:, 9:10], 2.0, ALU.mult, ALU.mult))
            ch.link(dve.tensor_scalar(angle[:, :], w["steps"][:, :], col[:, 10:11], w["quarter"][:, 0:1],
                                      ALU.mult, ALU.add))
            ch.link(dve.tensor_scalar(turn[:, :], angle[:, :], 1 / TWO_PI, ROUND, ALU.mult, ALU.add))
            ch.link(dve.tensor_scalar(turn[:, :], turn[:, :], ROUND, None, ALU.subtract))
            ch.link(dve.scalar_tensor_tensor(angle[:, :], turn[:, :], -TWO_PI_HI, angle[:, :], ALU.mult, ALU.add))
            ch.link(dve.scalar_tensor_tensor(angle[:, :], turn[:, :], -(TWO_PI - TWO_PI_HI), angle[:, :],
                                             ALU.mult, ALU.add))
            dve.tensor_scalar(angle[:, :], angle[:, :], PI_BELOW, -PI_BELOW, ALU.min, ALU.max).then_inc(s_red, 1)
            inner.normalize(dve, xh, xi)
            ch.link(dve.memset(pw[:, 0:1], 1.0))

            def affine(b):
                dve.wait_ge(s_t, b + 1)
                if b >= 2:
                    dve.wait_ge(s_pr, 7 * (b - 1))
                dve.tensor_scalar(xnT[:, b % 2, :], ps[:, b % 2, :], w["norm_gb"][:, 0:1], w["norm_gb"][:, 1:2],
                                  ALU.mult, ALU.add).then_inc(s_tc, 1)

            def copies(b):
                for bank, s, done, dst in ((3, s_ut, s_uc, U), (4, s_kt, s_kc, K)):
                    dve.wait_ge(s, b + 1)
                    for cc in range(2):
                        m = dve.tensor_copy(dst[:, :, cc, b, :],
                                            ps[:, bank, :].rearrange("p (t c n) -> p t c n", c=2, n=NF)[:, :, cc, :])
                    m.then_inc(done, 1)

            affine(0)
            for b in range(B):
                if b + 1 < B:
                    affine(b + 1)
                if b:
                    copies(b - 1)
                dve.wait_ge(s_pr, 7 * b + 4)
                dve.wait_ge(s_sig, 5 * b + 1)
                dve.tensor_tensor(uT[:, b % 2, :], ps[:, 5, :], sig[:, 0, :], ALU.mult).then_inc(s_u, 1)
                dve.wait_ge(s_sig, 5 * b + 2)
                if b:
                    dve.wait_ge(s_k1, b)
                ch.link(dve.tensor_tensor_scan(pw[:, 1:S + 1], sig[:, 1, :], col[:, 8:9].to_broadcast([P, S]), 1.0,
                                               ALU.mult, ALU.mult))
                dve.wait_ge(s_sig, 5 * b + 3)
                if b:
                    dve.wait_ge(s_k, b)
                dve.tensor_tensor(k1[:, :], pw[:, 0:S], sig[:, 2, :], ALU.mult).then_inc(s_k1, 1)
                dve.wait_ge(s_pr, 7 * b + 5)
                dve.wait_ge(s_sig, 5 * b + 4)
                dve.scalar_tensor_tensor(cp[:, b, :], ps[:, 6, :], w["bias"][:, 4:5], sig[:, 3, :],
                                         ALU.add, ALU.mult).then_inc(s_cp, 1)
            copies(B - 1)

        @block.scalar
        def _(act):
            outer.root(act, c["eps"])
            act.wait_ge(s_dv, 1)
            act.activation(erow[:, :], w["fi_row"][:, :], ACT.Exp, bias=col[:, 1:2], accum_out=col[:, 2:3]).then_inc(s_a, 1)
            act.activation(col[:, 3:4], w["fi_col"][:, 0:1], ACT.Exp, bias=col[:, 1:2]).then_inc(s_a, 1)
            act.activation(col[:, 4:5], w["log_decay"][:, 0:1], ACT.Sigmoid).then_inc(s_a, 1)
            act.activation(col[:, 5:6], w["dt"][:, 0:1], ACT.Sigmoid).then_inc(s_a, 1)
            inner.root(act, c["eps"])
            act.wait_ge(s_red, 1)
            act.activation(wave[:, :], angle[:, :], ACT.Sin).then_inc(s_wave, 1)
            for b in range(B):
                for k, (m, bias) in enumerate(((1, 0), (2, 1), (3, 2), (6, 3), (7, 5))):
                    act.wait_ge(s_pr, 7 * b + m)
                    if b:
                        if k == 0:
                            act.wait_ge(s_u, b)
                        elif k == 1:
                            act.wait_ge(s_k1, b)
                        elif k == 3:
                            act.wait_ge(s_cp, b)
                    dst = sig[:, k, :] if k < 4 else gate[:, b, :]
                    act.activation(dst, ps[:, PROJ[m - 1][1], :], ACT.Sigmoid,
                                   bias=w["bias"][:, bias:bias + 1]).then_inc(s_sig, 1)

        @block.gpsimd
        def _(pool):
            pool.wait_ge(s_wave, 1)
            for b in range(B):
                pool.wait_ge(s_k1, b + 1)
                if b >= 2:
                    pool.wait_ge(s_kt, b - 1)
                pool.tensor_tensor(kT[:, b % 2, :], k1[:, :], wave[:, :], ALU.mult).then_inc(s_k, 1)

        @block.tensor
        def _(pe):
            def transposed(b):
                pe.wait_ge(inner.s_done, TPB * (b + 1))
                if b >= 2:
                    pe.wait_ge(s_tc, b - 1)
                for t in range(TPB):
                    mm = pe.transpose(ps[:, b % 2, t * P:(t + 1) * P], xh[:, b * TPB + t, :], c["ident"][:, :])
                mm.then_inc(s_t, 1)

            def by_token(b):
                for bank, s, ready, src in ((3, s_ut, s_u, uT), (4, s_kt, s_k, kT)):
                    pe.wait_ge(ready, b + 1)
                    pe.wait_ge(s_sig, 5 * b + 3)
                    for t in range(TPB):
                        mm = pe.transpose(ps[:, bank, t * P:(t + 1) * P], src[:, b % 2, t * P:(t + 1) * P],
                                          c["ident"][:, :])
                    mm.then_inc(s, 1)

            transposed(0)
            for b in range(B):
                if b + 1 < B:
                    transposed(b + 1)
                pe.wait_ge(s_tc, b + 1)
                for m, (_, bank) in enumerate(PROJ):
                    if b and m == 0:
                        pe.wait_ge(s_sig, 5 * b)
                    elif b and m == 1:
                        pe.wait_ge(s_uc, b)
                    elif b and m == 2:
                        pe.wait_ge(s_kc, b)
                    elif b and m == 3:
                        pe.wait_ge(s_u, b)
                    elif b and m == 4:
                        pe.wait_ge(s_cp, b)
                    elif m == 6:
                        pe.wait_ge(s_sig, 5 * b + 1)
                    pe.matmul(ps[:, bank, :], w["wproj"][:, m * P:(m + 1) * P], xnT[:, b % 2, :],
                              start=True, stop=True).then_inc(s_pr, 1)
                by_token(b)


def ssm_convolve(nc, ps, w, U, K, spec, tables_loaded):
    with ExitStack() as ctx:
        def sb(name, shape, dt=F32):
            return ctx.enter_context(nc.sbuf_tensor(f"cv_{name}", shape, dt))

        sem = phase_semaphores(nc, ctx, "cv")

        H = COLS // 2
        fold = [sb(f"fold{k}", [P, KT, 2, COLS]) for k in range(2)]
        uf = sb("uf", [P, 2, COLS])
        prod = sb("prod", [P, 2, 2, COLS])
        Y = sb("Y", [P, 4, COLS])
        even = sb("even", [P, KT, COLS])
        odd = sb("odd", [P, KT, COLS])
        sums = sb("sums", [P, 2, KT, COLS])
        s_fold = [sem("folded0"), sem("folded1")]
        s_f = sem("transformed")
        s_uf, s_pr, s_y = sem("uf_copied"), sem("products"), sem("Y")
        s_z, s_zc, s_cb, s_sp = sem("inverse"), sem("inverse_copied"), sem("combined"), sem("spectral")
        ORDER = (0, 2, 1, 3)
        flat = lambda a, t: a[:, t, :, :, :].rearrange("p c b n -> p (c b n)")
        bankU = lambda n: ps[:, n % 2, :]
        bankK = lambda n: ps[:, 2 + n % 2, :]
        bankZ = lambda q, mt: ps[:, 4 + 2 * (q % 2) + mt, :]
        block = ctx.enter_context(nc.Block())

        def folds(eng, k, src):
            for q, r in enumerate(ORDER):
                if q >= 2:
                    eng.wait_ge(s_f, 4 * (q - 1))
                for kt in range(KT):
                    a, z, o = flat(src, kt), flat(src, KT + kt), fold[k][:, kt, q % 2, :]
                    if r % 2 == 0:
                        m = eng.tensor_tensor(o, a, z, ALU.subtract if r else ALU.add)
                    else:
                        ops = (ALU.add, ALU.subtract) if r == 1 else (ALU.subtract, ALU.add)
                        eng.tensor_tensor(o[:, 0:H], a[:, 0:H], z[:, H:COLS], ops[0])
                        m = eng.tensor_tensor(o[:, H:COLS], a[:, H:COLS], z[:, 0:H], ops[1])
                m.then_inc(s_fold[k], 1)
                yield

        @block.vector
        def _(dve):
            step = folds(dve, 0, U)
            next(step)
            next(step)

            def multiply(n):
                dve.wait_ge(s_f, 2 * n + 2)
                dve.wait_ge(s_uf, n + 1)
                if n >= 2:
                    dve.wait_ge(s_y, 2 * (n - 1))
                u, k, p = uf[:, n % 2, :], bankK(n), prod[:, n % 2, :, :]
                for half in range(2):
                    dve.tensor_tensor(p[:, 0, half * H:(half + 1) * H], u[:, half * H:(half + 1) * H], k[:, 0:H], ALU.mult)
                    m = dve.tensor_tensor(p[:, 1, half * H:(half + 1) * H], u[:, (1 - half) * H:(2 - half) * H],
                                          k[:, H:COLS], ALU.mult)
                m.then_inc(s_pr, 1)

            def combine(q):
                for mt in range(KT):
                    dve.wait_ge(s_z, KT * q + mt + 1)
                    if mt == 0:
                        dve.wait_ge(s_zc, KT * (q // 2 + 1))
                    z, e = bankZ(q, mt), (even if q == 1 else odd)[:, mt, :]
                    dve.tensor_tensor(sums[:, q // 2, mt, :], e, z, ALU.add).then_inc(s_cb, 1)
                    dve.tensor_tensor(e, e, z, ALU.subtract).then_inc(s_cb, 1)

            for q in range(R4):
                for gt in range(KT):
                    multiply(KT * q + gt)
                if q < 2:
                    next(step)
                if q == 2:
                    combine(1)
            combine(3)

        @block.gpsimd
        def _(pool):
            step = folds(pool, 1, K)
            next(step)
            next(step)
            for n in range(R4 * KT):
                pool.wait_ge(s_pr, n + 1)
                if n >= 4:
                    pool.wait_ge(s_z, KT * ((n - 4) // KT + 1))
                p, y = prod[:, n % 2, :, :], Y[:, n % 4, :]
                pool.tensor_tensor(y[:, 0:H], p[:, 0, 0:H], p[:, 1, 0:H], ALU.subtract).then_inc(s_y, 1)
                pool.tensor_tensor(y[:, H:COLS], p[:, 0, H:COLS], p[:, 1, H:COLS], ALU.add).then_inc(s_y, 1)
                if n in (1, 3):
                    next(step)
            pool.wait_ge(s_cb, 8)
            for mt in range(KT):
                part = lambda a, cc: a[:, mt, cc * H:(cc + 1) * H].rearrange("p (b n) -> p b n", n=NF)
                to = lambda t, cc: spec[:, t, :, cc, :]
                for cc in range(2):
                    pool.tensor_tensor(to(mt, cc), part(sums[:, 0], cc), part(sums[:, 1], cc), ALU.add)
                pool.tensor_tensor(to(KT + mt, 0), part(even, 0), part(odd, 1), ALU.subtract)
                pool.tensor_tensor(to(KT + mt, 1), part(even, 1), part(odd, 0), ALU.add).then_inc(s_sp, 1)

        @block.scalar
        def _(act):
            def z_copy(q, dst):
                for mt in range(KT):
                    act.wait_ge(s_z, KT * q + mt + 1)
                    act.activation(dst[:, mt, :], bankZ(q, mt), ACT.Copy).then_inc(s_zc, 1)

            for n in range(R4 * KT):
                act.wait_ge(s_f, 2 * n + 1)
                if n >= 2:
                    act.wait_ge(s_pr, n - 1)
                act.activation(uf[:, n % 2, :], bankU(n), ACT.Copy).then_inc(s_uf, 1)
                if n == 3:
                    z_copy(0, even)
                if n == 7:
                    z_copy(2, odd)

        @block.tensor
        def _(pe):
            pe.wait_ge(tables_loaded, 32)

            def transform(q, gt, k):
                r, n = ORDER[q], KT * q + gt
                bank = (bankU if k == 0 else bankK)(n)
                pe.wait_ge(s_fold[k], q + 1)
                if n >= 2:
                    if k == 0:
                        pe.wait_ge(s_uf, n - 1)
                    else:
                        pe.wait_ge(s_pr, n - 1)
                v = fold[k][:, :, q % 2, :]
                tab = lambda kt, j: w["forward"][:, kt, r, gt, j, :]
                pe.matmul(bank, tab(0, 0), v[:, 0, :], start=True, stop=False)
                for kt in range(KT):
                    pe.matmul(bank[:, 0:H], tab(kt, 1), v[:, kt, H:COLS], start=False, stop=False,
                              skip_group_check=True)
                    pe.matmul(bank[:, H:COLS], tab(kt, 2), v[:, kt, 0:H], start=False, stop=False,
                              skip_group_check=True)
                pe.matmul(bank, tab(1, 0), v[:, 1, :], start=False, stop=True).then_inc(s_f, 1)

            def inverse(q):
                r = ORDER[q]
                pe.wait_ge(s_y, 2 * KT * (q + 1))
                if q == 2:
                    pe.wait_ge(s_zc, KT)
                if q == 3:
                    pe.wait_ge(s_cb, 4)
                for mt in range(KT):
                    bank = bankZ(q, mt)
                    tab = lambda gt, j: w["inverse"][:, gt, r, mt, j, :]
                    y = lambda gt: Y[:, (KT * q + gt) % 4, :]
                    pe.matmul(bank, tab(0, 0), y(0), start=True, stop=False)
                    for gt in range(KT):
                        pe.matmul(bank[:, 0:H], tab(gt, 2), y(gt)[:, H:COLS], start=False, stop=False,
                                  skip_group_check=True)
                        pe.matmul(bank[:, H:COLS], tab(gt, 1), y(gt)[:, 0:H], start=False, stop=False,
                                  skip_group_check=True)
                    pe.matmul(bank, tab(1, 0), y(1), start=False, stop=True).then_inc(s_z, 1)

            for q in range(R4):
                for gt in range(KT):
                    transform(q, gt, 0)
                    transform(q, gt, 1)
                if q:
                    inverse(q - 1)
            inverse(R4 - 1)


def ssm_output(nc, ps, x, c, w, xi, xh, cp, gate, spec):
    with ExitStack() as ctx:
        def sb(name, shape, dt=F32):
            return ctx.enter_context(nc.sbuf_tensor(f"so_{name}", shape, dt))

        sem = phase_semaphores(nc, ctx, "so")

        ln = Moments(sb, sem, "ln")
        specT = sb("specT", [P, 2, S])
        gated = sb("gated", [P, 2, S])
        scale = sb("scale", [P, 1])
        xnT = sb("xnT", [P, 2, S])
        hid = sb("hid", [P, 2, FT, S])
        s_ch = sem("dve_chain")
        s_st, s_sc, s_yp, s_ga, s_gt, s_xi = (sem(k) for k in ("specT_psum", "specT_copied", "y_psum", "gated", "gated_psum", "xi"))
        s_t, s_tc, s_h, s_hg, s_o, s_x, s_xs = (sem(k) for k in ("xnT_psum", "xnT", "hidden_psum", "hidden", "out_psum", "x", "x_xi"))
        block = ctx.enter_context(nc.Block())

        @block.vector
        def _(dve):
            ch = Chain(dve, s_ch)
            ch.link(dve.tensor_scalar(scale[:, :], w["output_scale"][:, 0:1], 0.5, None, ALU.mult))
            for b in range(B):
                dve.wait_ge(s_yp, b + 1)
                if b >= 2:
                    dve.wait_ge(s_gt, b - 1)
                ch.link(dve.scalar_tensor_tensor(gated[:, b % 2, :], ps[:, 2 + b % 2, :], scale[:, 0:1], gate[:, b, :],
                                                 ALU.mult, ALU.mult))
                dve.scalar_tensor_tensor(gated[:, b % 2, :], cp[:, b, :], 0.5, gated[:, b % 2, :],
                                         ALU.mult, ALU.add).then_inc(s_ga, 1)
                dve.wait_ge(s_gt, b + 1)
                xb = xi[:, b * TPB:(b + 1) * TPB, :]
                dve.tensor_tensor(xb, ps[:, 4 + b % 2, :].rearrange("p (t d) -> p t d", d=D), xb, ALU.add).then_inc(s_xi, 1)
            dve.wait_ge(s_xi, B)
            ln.moments(dve, xi)
            ln.normalize(dve, xh, xi)

            def affine(b):
                dve.wait_ge(s_t, b + 1)
                if b >= 2:
                    dve.wait_ge(s_h, FT * (b - 1))
                dve.tensor_scalar(xnT[:, b % 2, :], ps[:, b % 2, :], w["norm2_gb"][:, 0:1], w["norm2_gb"][:, 1:2],
                                  ALU.mult, ALU.add).then_inc(s_tc, 1)

            affine(0)
            for b in range(B):
                if b + 1 < B:
                    affine(b + 1)
                dve.wait_ge(s_o, b + 1)
                dve.wait_ge(s_xs, 2 * (b + 1))
                xb = x[:, b * TPB:(b + 1) * TPB, :]
                dve.tensor_tensor(xb, ps[:, 6 + b % 2, :].rearrange("p (t d) -> p t d", d=D), xb, ALU.add).then_inc(s_x, 1)

        @block.gpsimd
        def _(pool):
            for b in range(B):
                xb = x[:, b * TPB:(b + 1) * TPB, :]
                pool.wait_ge(s_xi, b + 1)
                pool.tensor_tensor(xb, xb, xi[:, b * TPB:(b + 1) * TPB, :], ALU.add).then_inc(s_xs, 1)
                pool.wait_ge(s_xs, 2 * b + 1)
                pool.tensor_tensor(xb, xb, bc(w["b2"][:, :], TPB, 1), ALU.add).then_inc(s_xs, 1)

        @block.scalar
        def _(act):
            for b in range(B):
                act.wait_ge(s_st, b + 1)
                if b >= 2:
                    act.wait_ge(s_yp, b - 1)
                act.activation(specT[:, b % 2, :], ps[:, b % 2, :], ACT.Copy).then_inc(s_sc, 1)
            ln.root(act, c["eps"])
            for b in range(B):
                for f in range(FT):
                    act.wait_ge(s_h, FT * b + f + 1)
                    if b >= 2 and f == 0:
                        act.wait_ge(s_o, b - 1)
                    act.activation(hid[:, b % 2, f, :], ps[:, 2 + f, :], ACT.Gelu, bias=w["b1"][:, f:f + 1]).then_inc(s_hg, 1)

        @block.tensor
        def _(pe):
            def spectral(b):
                if b >= 2:
                    pe.wait_ge(s_sc, b - 1)
                for t in range(TPB):
                    mm = pe.transpose(ps[:, b % 2, t * P:(t + 1) * P], spec[:, t, b, :, :].rearrange("p c n -> p (c n)"), c["ident"][:, :])
                mm.then_inc(s_st, 1)

            def project(b):
                pe.wait_ge(s_sc, b + 1)
                if b >= 2:
                    pe.wait_ge(s_ga, b - 1)
                pe.matmul(ps[:, 2 + b % 2, :], w["wfs"][:, :], specT[:, b % 2, :], start=True, stop=True).then_inc(s_yp, 1)

            def by_token(b):
                pe.wait_ge(s_ga, b + 1)
                if b >= 2:
                    pe.wait_ge(s_xi, b - 1)
                for t in range(TPB):
                    mm = pe.transpose(ps[:, 4 + b % 2, t * P:(t + 1) * P], gated[:, b % 2, t * P:(t + 1) * P],
                                      c["ident"][:, :])
                mm.then_inc(s_gt, 1)

            spectral(0)
            for b in range(B):
                if b + 1 < B:
                    spectral(b + 1)
                project(b)
                by_token(b)

            def transposed(b):
                pe.wait_ge(ln.s_done, TPB * (b + 1))
                if b >= 2:
                    pe.wait_ge(s_tc, b - 1)
                for t in range(TPB):
                    mm = pe.transpose(ps[:, b % 2, t * P:(t + 1) * P], xh[:, b * TPB + t, :], c["ident"][:, :])
                mm.then_inc(s_t, 1)

            def hidden(b):
                pe.wait_ge(s_tc, b + 1)
                for f in range(FT):
                    if b:
                        pe.wait_ge(s_hg, FT * (b - 1) + f + 1)
                    pe.matmul(ps[:, 2 + f, :], w["w1"][:, f * P:(f + 1) * P], xnT[:, b % 2, :],
                              start=True, stop=True).then_inc(s_h, 1)

            def out(b):
                pe.wait_ge(s_hg, FT * (b + 1))
                if b >= 2:
                    pe.wait_ge(s_x, b - 1)
                for t in range(TPB):
                    for f in range(FT):
                        mm = pe.matmul(ps[:, 6 + b % 2, t * P:(t + 1) * P], hid[:, b % 2, f, t * P:(t + 1) * P],
                                       w["w2"][:, f, :], start=(f == 0), stop=(f == FT - 1))
                mm.then_inc(s_o, 1)

            transposed(0)
            for b in range(B):
                if b + 1 < B:
                    transposed(b + 1)
                hidden(b)
                if b:
                    out(b - 1)
            out(B - 1)


def constants():
    f = np.float32
    k = np.arange(P)
    restart = np.ones((NE, NT), f)
    restart[:, 0] = 0
    rows = lambda a: np.ascontiguousarray(np.broadcast_to(np.asarray(a, f).reshape(1, -1), (P, np.size(a))))
    return {
        "ident": np.eye(P, dtype=f),
        "before": (k[:, None] < k[None, :]).astype(f),
        "falling": rows(np.arange(NE, 0, -1)),
        "restart": rows(restart),
        "slot_tile": rows(np.arange(NSLOT)),
        "mask_q": np.where(k[None, :] > k[:, None], MASKED, 0).astype(f),
    }


def place_constants(nc, ctx, dram):
    c = {k: ctx.enter_context(nc.sbuf_tensor(f"c_{k}", list(v.shape), F32)) for k, v in dram.items()}
    for name, shape, dt in (("eps", [P, 1], F32), ("one", [P, NE], F32), ("zero", [P, D], F32),
                            ("ones_bf", [P, P], BF16), ("before_bf", [P, P], BF16), ("ident_bf", [P, P], BF16),
                            ("mask_q_bf", [P, P], BF16), ("zero_rows", [KROWS - MROW, S], BF16), ("one_rows", [KROWS - MROW, S], BF16)):
        c[name] = ctx.enter_context(nc.sbuf_tensor(f"c_{name}", shape, dt))
    s_const = ctx.enter_context(nc.semaphore("constants_loaded"))

    def load(block):
        @block.scalar
        def _(act):
            for k, v in dram.items():
                act.dma_start(c[k][:, :], v).then_inc(s_const, 16)

        @block.vector
        def _(dve):
            dve.memset(c["eps"][:, :], EPS)
            dve.memset(c["one"][:, :], 1.0)
            dve.memset(c["zero"][:, :], 0.0)
            dve.memset(c["ones_bf"][:, :], 1.0)
            dve.wait_ge(s_const, 16 * len(dram))
            dve.tensor_copy(c["before_bf"][:, :], c["before"][:, :])
            dve.memset(c["zero_rows"][:, :], 0.0)
            dve.memset(c["one_rows"][:, :], 1.0)
            for k in ("ident", "mask_q"):
                dve.tensor_copy(c[k + "_bf"][:, :], c[k][:, :])

    return c, load


def rotary():
    f = np.float32
    half = DH // 2
    inv = (1.0 / f(10000.0) ** (np.arange(half, dtype=f) / half)).astype(f)
    angle = (np.arange(S, dtype=f)[:, None] * inv[None, :]).astype(f)
    row = np.arange(P) % DH
    cos, sin = np.cos(angle)[:, row // 2].T, np.sin(angle)[:, row // 2].T
    sin = sin * np.where(row % 2, 1, -1)[:, None]
    r = 1 / np.sqrt(f(DH))
    return np.ascontiguousarray(np.stack([cos * r, sin * r, cos, sin], 1).astype(f))


def transform_tables():
    k = np.arange(HALF)
    out = []
    for inverse in range(2):
        tab = np.empty((P, KT, R4, KT, 3, P), np.float64)
        for r in range(R4):
            turns = np.outer(k, R4 * k + r)
            turns = (turns.T if inverse else turns) % NFFT
            a = turns * (TWO_PI / NFFT)
            for j, m in enumerate((np.cos(a), np.sin(a), -np.sin(a))):
                tab[:, :, r, :, j, :] = m.reshape(KT, P, KT, P).transpose(1, 0, 2, 3)
        out.append((tab / (NFFT if inverse else 1)).astype(np.float32))
    return out


def ssm_weights(inputs):
    g = lambda name: np.asarray(inputs[f"L0_attn_b_{name}"])
    twice = lambda a: np.concatenate([a, a], 0)
    col = lambda a: np.ascontiguousarray(a.reshape(-1, 1))
    band = lambda a: twice(np.repeat(a, NF // NB, 0))
    every = lambda a: np.repeat(a, P, 0)
    f = np.float32
    proj = [twice(g("Wfg")), band(g("Wband")), every(g("Wtg")), g("Wsp"), g("Wconcept"), g("Wcg"), g("Wgate")]
    bias = [twice(g("bfg")), band(g("bband")), every(g("btg")), g("bcg"), g("bconcept"), g("bgate")]
    return {
        "wproj": np.ascontiguousarray(np.concatenate(proj, 0).T),
        "bias": np.ascontiguousarray(np.stack(bias, 1)),
        "norm_gb": np.ascontiguousarray(np.stack([g("norm_g"), g("norm_b")], 1)),
        "norm2_gb": np.ascontiguousarray(np.stack([g("norm2_g"), g("norm2_b")], 1)),
        "fi_row": np.ascontiguousarray(np.broadcast_to(g("freq_importance")[None, :], (P, NF))),
        "fi_col": col(twice(g("freq_importance"))),
        "log_decay": col(twice(g("log_decay"))),
        "dt": col(twice(g("dt"))),
        "freq": col(twice(g("frequencies"))),
        "steps": np.ascontiguousarray(np.broadcast_to(np.arange(1, S + 1, dtype=f)[None, :], (P, S))),
        "quarter": col(np.repeat(np.array([np.pi / 2, 0], f), NF)),
        "output_scale": col(every(g("output_scale"))),
        "wfs": np.ascontiguousarray(g("Wfs").T),
        "w1": np.ascontiguousarray(g("W1").T),
        "b1": np.ascontiguousarray(g("b1").reshape(FT, P).T),
        "w2": np.ascontiguousarray(g("W2").reshape(D, FT, P).transpose(2, 1, 0)),
        "b2": np.ascontiguousarray(np.broadcast_to(g("b2")[None, :], (P, D))),
        "forward": transform_tables()[0],
        "inverse": transform_tables()[1],
    }


def ssm(nc, ps, x, c, dram):
    with ExitStack() as ctx:
        def sb(name, shape, dt=F32):
            return ctx.enter_context(nc.sbuf_tensor(f"sm_{name}", shape, dt))

        w = {k: sb(k, list(v.shape)) for k, v in dram.items()}
        xi, xh = sb("xi", [P, NT, D]), sb("xh", [P, NT, D])
        cp, gate = sb("cp", [P, B, S]), sb("gate", [P, B, S])
        s_tab = ctx.enter_context(nc.semaphore("sm_tables_loaded"))
        s_w = ctx.enter_context(nc.semaphore("sm_weights_loaded"))
        U, K = sb("U", [P, TPB, 2, B, NF]), sb("K", [P, TPB, 2, B, NF])
        spec = xh[:, :, :].rearrange("p (t b) (c n) -> p t b c n", b=B, n=NF)
        with nc.Block() as block:
            @block.sync
            def _(sp):
                small = [k for k in dram if k not in ("forward", "inverse")]
                for k in small:
                    sp.dma_start(w[k][tuple([slice(None)] * len(dram[k].shape))], dram[k]).then_inc(s_w, 16)
                sp.wait_ge(s_w, 16 * len(small))
                for k in ("forward", "inverse"):
                    sp.dma_start(w[k][tuple([slice(None)] * len(dram[k].shape))], dram[k]).then_inc(s_tab, 16)
        ssm_project(nc, ps, x, c, w, xi, xh, cp, gate, U, K)
        ssm_convolve(nc, ps, w, U, K, spec, s_tab)
        ssm_output(nc, ps, x, c, w, xi, xh, cp, gate, spec)


def attention_weights(inputs):
    g = lambda name: np.asarray(inputs[f"L0_attn_a_{name}"])
    swap = np.arange(P) ^ 1
    rows = lambda a: np.ascontiguousarray(np.broadcast_to(a[None, :], (P, P)))
    wq, wk, bq, bk = g("Wq"), g("Wk"), g("bq"), g("bk")
    return {
        "wqk": np.ascontiguousarray(np.concatenate([wq, wq[swap], wk, wk[swap]], 0).T),
        "qk_bias": np.ascontiguousarray(np.stack([bq, bq[swap], bk, bk[swap]], 1)),
        "rotary": rotary(),
        "wv": np.ascontiguousarray(g("Wv").T),
        "wo": np.ascontiguousarray(g("Wo").T),
        "bv": rows(g("bv")),
        "bo": rows(g("bo")),
    }


def moe_weights(inputs):
    g = lambda name: np.asarray(inputs[f"L0_ffn_{name}"])
    return {
        "w1": np.ascontiguousarray(g("W1").transpose(2, 0, 1).reshape(P, NE * DFF)),
        "w2": np.ascontiguousarray(g("W2").reshape(NE, D, FT, P).transpose(3, 0, 2, 1).reshape(P, NE * DFF)),
        "wr": np.ascontiguousarray(g("Wr").T),
    }


def whole(nc, x_dram, out_dram, consts, att, ssm_w, moe_w):
    whole_of = lambda t: t[tuple([slice(None)] * len(t.shape))]
    with ExitStack() as ctx:
        ps = ctx.enter_context(nc.psum_tensor("ps", [P, 8, S], F32))
        x = ctx.enter_context(nc.sbuf_tensor("x", [P, NT, D], F32))
        mw = {k: ctx.enter_context(nc.sbuf_tensor(f"moe_{k}", list(v.shape), F32)) for k, v in moe_w.items()}
        c, load = place_constants(nc, ctx, consts)
        s_x = ctx.enter_context(nc.semaphore("x_loaded"))
        s_mw = ctx.enter_context(nc.semaphore("moe_weights_loaded"))
        s_out = ctx.enter_context(nc.semaphore("out_stored"))
        xs = nc.dram_tensor("expert_rows", [NSLOT * P, D], F32, kind="Internal").ap()
        ys = nc.dram_tensor("expert_results", [NSLOT * P, D], F32, kind="Internal").ap()
        parts = nc.dram_tensor("parts", [B, 2, 3, P, S], BF16, kind="Internal").ap()
        x_rows = x_dram.rearrange("b (t p) d -> p (b t) d", p=P)
        out_rows = out_dram.rearrange("b (t p) d -> p (b t) d", p=P)

        with ExitStack() as actx:
            w = {k: actx.enter_context(nc.sbuf_tensor(f"w_{k}", list(v.shape), F32)) for k, v in att.items()}
            hatq = actx.enter_context(nc.sbuf_tensor("hatq", [KROWS, 2, NH, S], BF16))
            hatk = actx.enter_context(nc.sbuf_tensor("hatk", [KROWS, 2, NH, S], BF16))
            vall = actx.enter_context(nc.sbuf_tensor("vall", [P, NT, D], F32))
            s_hat = {k: actx.enter_context(nc.semaphore(f"hat_{k}")) for k in (0, 1, "fill")}
            with nc.Block() as block:
                @block.sync
                def _(sp):
                    sp.dma_start(x[:, :, :], x_rows).then_inc(s_x, 16)
                    for k, v in w.items():
                        sp.dma_start(whole_of(v), att[k]).then_inc(s_x, 16)
                    for k, v in mw.items():
                        sp.dma_start(whole_of(v), moe_w[k]).then_inc(s_mw, 16)
                    sp.wait_ge(s_x, 16 * (1 + len(w)))

                load(block)
            attention_prepare(nc, ps, x, c, w, parts, hatq, hatk, vall, s_hat)
            attention(nc, ps, x, c, w, parts, hatq, hatk, vall, s_hat)
        moe(nc, "moe0", ps, x, c, mw["w1"], mw["w2"], mw["wr"], xs, ys, s_mw)
        ssm(nc, ps, x, c, ssm_w)
        moe(nc, "moe1", ps, x, c, mw["w1"], mw["w2"], mw["wr"], xs, ys, s_mw)
        with nc.Block() as block:
            @block.sync
            def _(sp):
                sp.dma_start(out_rows, x[:, :, :]).then_inc(s_out, 16)
                sp.wait_ge(s_out, 16)


def kernel(**inputs):
    import concourse.bacc as bacc
    from concourse.bass_utils import run_bass_kernel_spmd

    nc = bacc.Bacc("TRN2", target_bir_lowering=False, num_devices=1)
    groups = {"c": constants(), "att": attention_weights(inputs), "ssm": ssm_weights(inputs), "moe": moe_weights(inputs)}
    arrays, aps = {}, {}
    for g, members in groups.items():
        aps[g] = {}
        for k, a in members.items():
            arrays[f"{g}_{k}_dram"] = a
            aps[g][k] = nc.dram_tensor(f"{g}_{k}_dram", a.shape, F32, kind="ExternalInput").ap()
    arrays["x_dram"] = np.ascontiguousarray(inputs["L0_attn_a_x"])
    x = nc.dram_tensor("x_dram", [B, S, D], F32, kind="ExternalInput").ap()
    out = nc.dram_tensor("out_dram", [B, S, D], F32, kind="ExternalOutput").ap()
    whole(nc, x, out, aps["c"], aps["att"], aps["ssm"], aps["moe"])
    r = run_bass_kernel_spmd(nc, [arrays], core_ids=[0])
    return r.results[0]["out_dram"]
```

```python
from contextlib import ExitStack

import concourse.bass as bass
import numpy as np
from concourse import mybir

ALU = mybir.AluOpType
ACT = mybir.ActivationFunctionType
AX = mybir.AxisListType
F32 = mybir.dt.float32
BF16 = mybir.dt.bfloat16
I32 = mybir.dt.int32
U32 = mybir.dt.uint32

P = 128
B, S, D = 4, 512, 128
NT = B * S // P
TPB = S // P
EPS = 1e-5
ROUND = 12582912.0

NE, DFF = 8, 512
FT = DFF // P
NSLOT = (2 * NT * P + NE * (P - 1)) // P
GT = TPB
NG = NT // GT
REGION = B * S + P
ROW = D + 1


class Chain:

    def __init__(self, engine, semaphore, base=0):
        self.engine, self.semaphore, self.count, self.base = engine, semaphore, 0, base

    def did(self, instruction):
        instruction.then_inc(self.semaphore, 1)
        self.count += 1
        return instruction

    def settle(self):
        self.engine.wait_ge(self.semaphore, self.base + self.count)

    def link(self, instruction):
        self.did(instruction)
        self.settle()


def phase_semaphores(nc, ctx, tag):
    made = []

    def clear():
        nc.clear_and_free_semaphores(made)
        nc.all_engine_barrier()

    def sem(name):
        made.append(nc.alloc_semaphore(f"{tag}_{name}"))
        return made[-1]

    ctx.callback(clear)
    return sem


def bc(ap, n, at):
    shape = list(ap.shape)
    return ap.unsqueeze(at).to_broadcast(shape[:at] + [n] + shape[at:])


def active(tile):
    return not isinstance(tile, int) or 0 <= tile < NSLOT


def later(tile, n):
    return not isinstance(tile, int) or tile >= n


def over_slot_tiles(engine, step, steps=NSLOT + 3):
    for i in range(8):
        step(i, i % 4)
    with engine.Fori(8, 36, 4) as i:
        for u in range(4):
            step(i + u, u)
    for i in range(36, steps):
        step(i, i % 4)


def moe(nc, tag, ps, x, c, mw, pads, xs_dram, ys_dram, s_weights):
    w1t, w2t, wrt = mw["w1"], mw["w2"], mw["wr"]
    with ExitStack() as ctx:
        def sb(name, shape, dt=F32):
            return ctx.enter_context(nc.sbuf_tensor(f"{tag}_{name}", shape, dt))

        sem = phase_semaphores(nc, ctx, tag)

        stats = sb("stats", [P, NT, 6])
        mv = sb("mv", [P, NT, 2])
        std = sb("std", [P, NT])
        rstd = sb("rstd", [P, NT])
        rows = sb("rows", [P, 2, NT, ROW])
        xnT = sb("xnT", [P, 2, GT * P])
        lg = sb("lg", [P, NT, NE])
        work = sb("work", [P, NT, NE])
        work2 = sb("work2", [P, NT, NE])
        first = sb("first", [P, NT])
        oh = sb("oh", [P, 2, NT, NE])
        top = sb("top", [P, 2, NT])
        chosen = sb("chosen", [P, NT, NE], BF16)
        before = sb("before", [P, NT + 1, NE], BF16)
        pos = sb("pos", [P, NT, NE])
        mine = sb("mine", [P, NT, 2, NE])
        slot = sb("slot", [P, NT, 2])
        sloti = sb("sloti", [P, NT, 2], U32)
        tiles = sb("tiles", [1, NE])
        tiles_upto = sb("tiles_upto", [1, NE])
        pad_start = sb("pad_start", [1, NE], I32)
        passed = sb("passed", [1, NSLOT, NE])
        passed_tiles = sb("passed_tiles", [1, NSLOT, NE])
        eid = sb("eid", [1, NSLOT])
        first_tile = sb("first_tile", [1, NSLOT])
        eoff = sb("eoff", [1, NSLOT], I32)
        roff = sb("roff", [1, NSLOT], I32)
        gap = sb("gap", [P, NT])
        egap = sb("egap", [P, NT])
        gate = sb("gate", [P, 2, NT])
        xg = sb("xg", [P, 4, ROW])
        xgT = sb("xgT", [P, 2, P])
        w1 = sb("w1", [P, 2, DFF])
        hT = sb("hT", [P, 2, DFF])
        y = sb("y", [P, 4, D])
        target = sb("target", [P, 4])
        targeti = sb("targeti", [P, 4], U32)
        ytok = sb("ytok", [P, 2, NT, D])

        s_chain = sem("dve_chain")
        s_mv = sem("moments")
        s_std = sem("std")
        s_number = sem("row_numbers")
        s_xn = sem("xn")
        s_copy = sem("second_rows")
        s_t = sem("xnT_psum")
        s_tc = sem("xnT_copied")
        s_lg = sem("logits")
        s_ch = sem("chosen")
        s_rank = sem("ranks")
        s_total = sem("totals")
        s_gap = sem("gap")
        s_egap = sem("exp_gap")
        s_slot = sem("slots")
        s_off = sem("expert_offsets")
        s_pad = sem("pad_rows_written")
        s_scat = sem("scattered")
        s_xg = [sem(f"xg_loaded{i}") for i in range(4)]
        s_tgt = sem("targets_copied")
        s_x = sem("xgT_psum")
        s_xc = sem("xgT_copied")
        s_m1 = sem("hidden_psum")
        s_h = sem("hidden")
        s_w1 = sem("w1_of_tile")
        s_m2 = sem("y_psum")
        s_y = sem("y_copied")
        s_st = [sem(f"y_scattered{i}") for i in range(4)]
        s_go = sem("scatter_may_start")
        s_res = [[sem(f"results_loaded{k}_{g}") for g in range(NG)] for k in range(2)]
        s_out = sem("combined")

        psX = lambda i: ps[:, i % 2, 0:P]
        psH = lambda i: ps[:, 2 + i % 2, :]
        psY = lambda i: ps[:, 6 + i % 2, 0:D]
        flat = lambda a: a.rearrange("p a b -> p (a b)")

        block = ctx.enter_context(nc.Block())

        @block.vector
        def _(dve):
            ch = Chain(dve, s_chain)

            def moments(g):
                for t in range(g * GT, (g + 1) * GT):
                    ch.did(dve.bn_stats(stats[:, t, :], x[:, t, :]))
                ch.settle()
                for t in range(g * GT, (g + 1) * GT):
                    dve.bn_aggr(mv[:, t, :], stats[:, t, :]).then_inc(s_mv, 1)

            def normalize(g):
                dve.wait_ge(s_std, g + 1)
                ch.link(dve.reciprocal(rstd[:, g * GT:(g + 1) * GT], std[:, g * GT:(g + 1) * GT]))
                for t in range(g * GT, (g + 1) * GT):
                    dve.tensor_scalar(rows[:, 0, t, 0:D], x[:, t, :], mv[:, t, 0:1], rstd[:, t:t + 1],
                                      ALU.subtract, ALU.mult).then_inc(s_xn, 1)

            def first_max(g, src, k):
                ts = slice(g * GT, (g + 1) * GT)
                ch.link(dve.tensor_reduce(top[:, k, ts], src[:, ts, :], AX.X, ALU.max))
                ch.link(dve.tensor_tensor(work2[:, ts, :], src[:, ts, :], bc(top[:, k, ts], NE, 2), ALU.is_equal))
                ch.link(dve.tensor_tensor(work2[:, ts, :], work2[:, ts, :], bc(c["falling"][:, :], GT, 1), ALU.mult))
                ch.link(dve.tensor_reduce(first[:, ts], work2[:, ts, :], AX.X, ALU.max))
                ch.link(dve.tensor_tensor(oh[:, k, ts, :], work2[:, ts, :], bc(first[:, ts], NE, 2), ALU.is_equal))

            def choose(g):
                ts = slice(g * GT, (g + 1) * GT)
                if g:
                    dve.wait_ge(s_ch, g)
                dve.wait_ge(s_lg, g + 1)
                ch.link(dve.tensor_copy(lg[:, ts, :], ps[:, 2 + g % 2, 0:GT * NE].rearrange("p (t e) -> p t e", e=NE)))
                first_max(g, lg, 0)
                ch.link(dve.scalar_tensor_tensor(work[:, ts, :], oh[:, 0, ts, :], -3e38, lg[:, ts, :],
                                                 ALU.mult, ALU.add))
                first_max(g, work, 1)
                ch.link(dve.tensor_tensor(chosen[:, ts, :], oh[:, 0, ts, :], oh[:, 1, ts, :], ALU.add))
                for t in range(g * GT, (g + 1) * GT - 1):
                    ch.link(dve.tensor_tensor(before[:, t + 1, :], before[:, t, :], chosen[:, t, :], ALU.add))
                t = (g + 1) * GT - 1
                dve.tensor_tensor(before[:, t + 1, :], before[:, t, :], chosen[:, t, :], ALU.add).then_inc(s_ch, 1)

            def slots(g):
                ts = slice(g * GT, (g + 1) * GT)
                dve.wait_ge(s_rank, g + 1)
                ch.link(dve.tensor_tensor(pos[:, ts, :], ps[:, 4 + g % 2, 0:GT * NE].rearrange("p (t e) -> p t e", e=NE),
                                          bc(c["region"][:, :], GT, 1), ALU.add))
                for k in range(2):
                    ch.did(dve.tensor_tensor(mine[:, ts, k, :], oh[:, k, ts, :], pos[:, ts, :], ALU.mult))
                ch.settle()
                ch.link(dve.tensor_reduce(slot[:, ts, :], mine[:, ts, :, :], AX.X, ALU.add))
                dve.tensor_copy(sloti[:, ts, :], slot[:, ts, :]).then_inc(s_slot, 1)

            ch.link(dve.memset(before[:, 0, :], 0.0))
            moments(0)
            moments(1)
            normalize(0)
            for g in range(NG):
                if g + 1 < NG:
                    normalize(g + 1)
                choose(g)
                if g + 2 < NG:
                    moments(g + 2)
                slots(g)
            dve.wait_ge(s_total, 1)
            total = ps[0:1, 6, 0:NE]
            dve.tensor_tensor(pad_start[:, :], total, c["region"][0:1, :], ALU.add).then_inc(s_off, 1)
            ch.link(dve.tensor_scalar(tiles[:, :], total, 1.0 / P, 0.49609375, ALU.mult, ALU.add))
            ch.link(dve.tensor_scalar(tiles[:, :], tiles[:, :], ROUND, ROUND, ALU.add, ALU.subtract))
            ch.link(dve.tensor_tensor_scan(tiles_upto[:, :], c["one"][0:1, 0:NE], tiles[:, :], 0.0, ALU.mult, ALU.add))
            ch.link(dve.tensor_tensor(passed[:, :, :], bc(tiles_upto[:, :], NSLOT, 1),
                                      bc(c["slot_tile"][0:1, :], NE, 2), ALU.is_le))
            ch.did(dve.tensor_reduce(eid[:, :], passed[:, :, :], AX.X, ALU.add))
            ch.link(dve.tensor_tensor(passed_tiles[:, :, :], passed[:, :, :], bc(tiles[:, :], NSLOT, 1), ALU.mult))
            dve.tensor_scalar(eoff[:, :], eid[:, :], float(NE - 1), float(DFF), ALU.min, ALU.mult).then_inc(s_off, 1)
            ch.link(dve.tensor_reduce(first_tile[:, :], passed_tiles[:, :, :], AX.X, ALU.add))
            ch.link(dve.tensor_tensor(first_tile[:, :], c["slot_tile"][0:1, :], first_tile[:, :], ALU.subtract))
            ch.link(dve.tensor_scalar(eid[:, :], eid[:, :], float(REGION), None, ALU.mult))
            dve.scalar_tensor_tensor(roff[:, :], first_tile[:, :], float(P), eid[:, :],
                                     ALU.mult, ALU.add).then_inc(s_off, 1)
            dve.tensor_tensor(gap[:, :], top[:, 1, :], top[:, 0, :], ALU.subtract).then_inc(s_gap, 1)
            dve.wait_ge(s_egap, 1)
            ch.link(dve.tensor_scalar(gap[:, :], egap[:, :], 1.0, None, ALU.add))
            ch.link(dve.reciprocal(gate[:, 0, :], gap[:, :]))
            ch.link(dve.tensor_tensor(gate[:, 1, :], gate[:, 0, :], egap[:, :], ALU.mult))

            def step(i, u):
                j = i
                if active(j):
                    w = dve.value_load(eoff[0:1, bass.ds(j, 1)], min_val=0, max_val=(NE - 1) * DFF)
                    if later(j, 2):
                        dve.wait_ge(s_m1, j - 1)
                    dve.tensor_copy(w1[:, u % 2, :], w1t[:, bass.ds(w, DFF)]).then_inc(s_w1, 1)
                j = i - 1
                if active(j):
                    q = (u - 1) % 4
                    if later(j, 4):
                        dve.wait_ge(s_y, (j - 3) * 2)
                    dve.wait_ge(s_x, j + 1)
                    dve.tensor_copy(target[:, q:q + 1], xg[:, q, D:ROW]).then_inc(s_tgt, 1)
                j = i - 3
                if active(j):
                    q = (u - 3) % 4
                    if later(j, 4):
                        dve.wait_ge(s_st[q], (j - q) * 4)
                    dve.wait_ge(s_tgt, j + 1)
                    dve.tensor_copy(targeti[:, q:q + 1], target[:, q:q + 1]).then_inc(s_y, 1)
                    dve.wait_ge(s_m2, j + 1)
                    dve.tensor_copy(y[:, q, :], psY(u + 1)).then_inc(s_y, 1)

            over_slot_tiles(dve, step)
            for k in range(2):
                for t in range(NT):
                    dve.wait_ge(s_res[k][t // GT], 16)
                    if k:
                        dve.wait_ge(s_out, t + 1)
                    dve.scalar_tensor_tensor(x[:, t, :], ytok[:, k, t, :], gate[:, k, t:t + 1], x[:, t, :],
                                             ALU.mult, ALU.add).then_inc(s_out, 1)

        @block.scalar
        def _(act):
            def deviation(g):
                act.wait_ge(s_mv, (g + 1) * GT)
                act.activation(std[:, g * GT:(g + 1) * GT], mv[:, g * GT:(g + 1) * GT, 1], ACT.Sqrt,
                               bias=c["eps"][:, 0:1]).then_inc(s_std, 1)

            deviation(0)
            deviation(1)
            for g in range(NG):
                act.wait_ge(s_t, g + 1)
                act.activation(xnT[:, g % 2, :], ps[:, g % 2, :], ACT.Copy).then_inc(s_tc, 1)
                act.activation(rows[:, 1, g * GT:(g + 1) * GT, 0:D], rows[:, 0, g * GT:(g + 1) * GT, 0:D],
                               ACT.Copy).then_inc(s_copy, 1)
                if g + 2 < NG:
                    deviation(g + 2)
            act.wait_ge(s_gap, 1)
            act.activation(egap[:, :], gap[:, :], ACT.Exp).then_inc(s_egap, 1)

            def step(i, u):
                j = i
                if active(j):
                    act.wait_ge(s_x, j + 1)
                    if later(j, 2):
                        act.wait_ge(s_m1, j - 1)
                    act.activation(xgT[:, u % 2, :], psX(u), ACT.Copy).then_inc(s_xc, 1)
                j = i - 1
                if active(j):
                    act.wait_ge(s_m1, j + 1)
                    if later(j, 2):
                        act.wait_ge(s_m2, j - 1)
                    act.activation(hT[:, (u + 1) % 2, :], psH(u + 1), ACT.Silu).then_inc(s_h, 1)

            over_slot_tiles(act, step)

        @block.tensor
        def _(pe):
            pe.wait_ge(s_weights, 48)

            def transposed(g):
                pe.wait_ge(s_xn, GT * g + GT)
                if g >= 2:
                    pe.wait_ge(s_tc, g - 1)
                for t in range(GT):
                    mm = pe.transpose(ps[:, g % 2, t * P:(t + 1) * P], rows[:, 0, GT * g + t, 0:D], c["ident"][:, :])
                mm.then_inc(s_t, 1)

            def logits(g):
                pe.wait_ge(s_tc, g + 1)
                for t in range(GT):
                    mm = pe.matmul(ps[:, 2 + g % 2, t * NE:(t + 1) * NE], xnT[:, g % 2, t * P:(t + 1) * P],
                                   wrt[:, :], start=True, stop=True)
                mm.then_inc(s_lg, 1)

            def ranks(g):
                pe.wait_ge(s_ch, g + 1)
                out = ps[:, 4 + g % 2, 0:GT * NE]
                pe.matmul(out, c["before_bf"][:, :], flat(chosen[:, g * GT:(g + 1) * GT, :]), start=True, stop=False)
                pe.matmul(out, c["ones_bf"][:, :], flat(before[:, g * GT:(g + 1) * GT, :]), start=False,
                          stop=True).then_inc(s_rank, 1)

            transposed(0)
            logits(0)
            transposed(1)
            for g in range(NG):
                if g + 1 < NG:
                    logits(g + 1)
                ranks(g)
                if g + 2 < NG:
                    transposed(g + 2)
            pe.matmul(ps[:, 6, 0:NE], c["ones_bf"][:, :], before[:, NT, :], start=True, stop=True).then_inc(s_total, 1)
            pe.wait_ge(s_off, 3)
            pe.wait_ge(s_slot, NG)

            def step(i, u):
                j = i
                if active(j):
                    pe.wait_ge(s_xg[u], (j - u) * 4 + 16)
                    if later(j, 2):
                        pe.wait_ge(s_xc, j - 1)
                    pe.transpose(psX(u), xg[:, u, 0:D], c["ident"][:, :]).then_inc(s_x, 1)
                j = i - 1
                if active(j):
                    pe.wait_ge(s_xc, j + 1)
                    pe.wait_ge(s_w1, j + 1)
                    if later(j, 2):
                        pe.wait_ge(s_h, j - 1)
                    for f in range(FT):
                        mm = pe.matmul(psH(u + 1)[:, f * P:(f + 1) * P], w1[:, (u + 1) % 2, f * P:(f + 1) * P],
                                       xgT[:, (u + 1) % 2, :], start=True, stop=True)
                    mm.then_inc(s_m1, 1)
                j = i - 2
                if active(j):
                    w = pe.value_load(eoff[0:1, bass.ds(j, 1)], min_val=0, max_val=(NE - 1) * DFF)
                    pe.wait_ge(s_h, j + 1)
                    if later(j, 2):
                        pe.wait_ge(s_y, (j - 1) * 2)
                    for f in range(FT):
                        mm = pe.matmul(psY(u), hT[:, u % 2, f * P:(f + 1) * P],
                                       w2t[:, bass.ds(w + f * P, P)], start=(f == 0), stop=(f == FT - 1))
                    mm.then_inc(s_m2, 1)

            over_slot_tiles(pe, step)

        @block.sync
        def _(sp):
            sp.dma_start(xs_dram[NE * REGION:NE * REGION + NE * P, :], pads[NE * P:2 * NE * P, :]).then_inc(s_pad, 16)
            sp.wait_ge(s_off, 1)
            for e in range(NE):
                r = sp.value_load(pad_start[0:1, e:e + 1], min_val=e * REGION, max_val=(e + 1) * REGION - P)
                sp.dma_start(xs_dram[bass.ds(r, P), :], pads[e * P:(e + 1) * P, :]).then_inc(s_pad, 16)
            sp.wait_ge(s_off, 3)
            sp.wait_ge(s_pad, 16 * (NE + 1))
            sp.wait_ge(s_scat, 16 * 2 * NT)

            def step(i, u):
                if not active(i):
                    return
                r = sp.value_load(roff[0:1, bass.ds(i, 1)], min_val=0, max_val=NE * REGION + (NE - 1) * P)
                if later(i, 4):
                    sp.wait_ge(s_tgt, i - 3)
                sp.dma_start(xg[:, u, :], xs_dram[bass.ds(r, P), :]).then_inc(s_xg[u], 16)

            over_slot_tiles(sp, step)
            for q in range(4):
                sp.wait_ge(s_st[q], 16 * ((NSLOT - q + 3) // 4))
            for k in range(2):
                for g in range(NG):
                    r0 = k * NT * P + g * GT * P
                    sp.dma_start(ytok[:, k, g * GT:(g + 1) * GT, :],
                                 ys_dram[r0:r0 + GT * P, :].rearrange("(t p) d -> p t d", p=P)).then_inc(s_res[k][g], 16)

        @block.gpsimd
        def _(pool):
            pool.tensor_copy(rows[:, :, :, D:ROW].rearrange("p k t o -> p (k t o)"), c["row_number"][:, :]).then_inc(s_number, 1)
            pool.wait_ge(s_number, 1)
            for g in range(NG):
                pool.wait_ge(s_slot, g + 1)
                for k in range(2):
                    if k:
                        pool.wait_ge(s_copy, g + 1)
                    else:
                        pool.wait_ge(s_xn, (g + 1) * GT)
                    for t in range(g * GT, (g + 1) * GT):
                        pool.indirect_dma_start(xs_dram[:, :], bass.IndirectOffsetOnAxis(sloti[:, t, k:k + 1], 0),
                                                rows[:, k, t, :], None).then_inc(s_scat, 16)

            def step(i, u):
                j = i - 4
                if active(j):
                    pool.wait_ge(s_y, (j + 1) * 2)
                    pool.sem_inc(s_go, 1)
                    pool.indirect_dma_start(ys_dram[:, :], bass.IndirectOffsetOnAxis(targeti[:, u:u + 1], 0),
                                            y[:, u, :], None).then_inc(s_st[u], 16)

            over_slot_tiles(pool, step, NSLOT + 4)


NH, DH = 16, 8
HG = 4
UNITS = B * NH // HG
GROUPS = NH // HG
KROWS = 128
MROW = 9 * DH
MASKED = -1e30
WIDTH = [S - P * k for k in range(TPB)]


def attention_prepare(nc, ps, x, c, w, parts_dram, hatq, hatk, vall, s_hat):
    with ExitStack() as ctx:
        def sb(name, shape, dt=F32):
            return ctx.enter_context(nc.sbuf_tensor(f"ap_{name}", shape, dt))

        sem = phase_semaphores(nc, ctx, "ap")

        stats = sb("stats", [P, NT, 6])
        mv = sb("mv", [P, NT, 2])
        std = sb("std", [P, NT])
        rstd = sb("rstd", [P, NT])
        xn = sb("xn", [P, 2, TPB, D])
        xnT = sb("xnT", [P, 2, S])
        rot = sb("rot", [P, 2, 2, S])
        full = sb("full", [P, 2, 2, S])
        rest = sb("rest", [P, 2, S])
        part = sb("part", [P, 2, 2, 3, S], BF16)
        s_chain = sem("dve_chain")
        s_mv, s_std, s_xn, s_t, s_tc = sem("moments"), sem("std"), sem("xn"), sem("xnT_psum"), sem("xnT_copied")
        s_pr, s_rot, s_v = sem("projected"), sem("rotated"), sem("values")
        s_full, s_p0, s_r1, s_p1, s_p2 = (sem(f"split{k}") for k in range(5))
        s_store = [sem("parts_stored0"), sem("parts_stored1")]
        s_bo = sem("bo_added")
        block = ctx.enter_context(nc.Block())

        @block.vector
        def _(dve):
            ch = Chain(dve, s_chain)
            for t in range(NT):
                ch.did(dve.bn_stats(stats[:, t, :], x[:, t, :]))
            ch.settle()
            for t in range(NT):
                dve.bn_aggr(mv[:, t, :], stats[:, t, :]).then_inc(s_mv, 1)
            dve.wait_ge(s_std, 1)
            ch.link(dve.reciprocal(rstd[:, :], std[:, :]))

            def normalize(b):
                if b >= 2:
                    dve.wait_ge(s_t, b - 1)
                for t in range(TPB):
                    n = b * TPB + t
                    dve.tensor_scalar(xn[:, b % 2, t, :], x[:, n, :], mv[:, n, 0:1], rstd[:, n:n + 1],
                                      ALU.subtract, ALU.mult).then_inc(s_xn, 1)

            normalize(0)
            for b in range(B):
                if b + 1 < B:
                    normalize(b + 1)
                for m in range(4):
                    dve.wait_ge(s_pr, 5 * b + m + 1)
                    if m % 2 == 0 and b:
                        dve.wait_ge(s_full, 2 * (b - 1) + m // 2 + 1)
                    dve.scalar_tensor_tensor(rot[:, m // 2, m % 2, :], ps[:, 2 + m, :], w["qk_bias"][:, m:m + 1],
                                             w["rotary"][:, m, :], ALU.add, ALU.mult).then_inc(s_rot, 1)
                dve.wait_ge(s_pr, 5 * b + 5)
                dve.tensor_tensor(vall[:, b * TPB:(b + 1) * TPB, :],
                                  ps[:, 6 + b % 2, :].rearrange("p (t d) -> p t d", d=D),
                                  bc(w["bv"][:, :], TPB, 1), ALU.add).then_inc(s_v, 1)
                for k in range(2):
                    dve.wait_ge(s_full, 2 * b + k + 1)
                    dve.wait_ge(s_p0, 2 * b + k + 1)
                    if b:
                        dve.wait_ge(s_p2, 2 * (b - 1) + k + 1)
                    dve.tensor_tensor(rest[:, k, :], full[:, b % 2, k, :], part[:, b % 2, k, 0, :],
                                      ALU.subtract).then_inc(s_r1, 1)

        @block.scalar
        def _(act):
            act.wait_ge(s_mv, NT)
            act.activation(std[:, :], mv[:, :, 1], ACT.Sqrt, bias=c["eps"][:, 0:1]).then_inc(s_std, 1)

            def copy_xnT(b):
                act.wait_ge(s_t, b + 1)
                if b >= 2:
                    act.wait_ge(s_pr, 5 * (b - 1))
                act.activation(xnT[:, b % 2, :], ps[:, b % 2, :], ACT.Copy).then_inc(s_tc, 1)

            copy_xnT(0)
            for b in range(B):
                if b + 1 < B:
                    copy_xnT(b + 1)
                if b >= 2:
                    act.wait_ge(s_store[b % 2], 32 * (b // 2))
                for k in range(2):
                    act.wait_ge(s_full, 2 * b + k + 1)
                    act.activation(part[:, b % 2, k, 0, :], full[:, b % 2, k, :], ACT.Copy).then_inc(s_p0, 1)
                for k in range(2):
                    act.wait_ge(s_r1, 2 * b + k + 1)
                    act.activation(part[:, b % 2, k, 1, :], rest[:, k, :], ACT.Copy).then_inc(s_p1, 1)

        @block.gpsimd
        def _(pool):
            for b in range(B):
                for k in range(2):
                    pool.wait_ge(s_rot, 4 * b + 2 * k + 2)
                    if b >= 2:
                        pool.wait_ge(s_p0, 2 * (b - 2) + k + 1)
                        pool.wait_ge(s_r1, 2 * (b - 2) + k + 1)
                    pool.tensor_tensor(full[:, b % 2, k, :], rot[:, k, 0, :], rot[:, k, 1, :], ALU.add).then_inc(s_full, 1)
                if b >= 2:
                    pool.wait_ge(s_store[b % 2], 32 * (b // 2))
                for k in range(2):
                    pool.wait_ge(s_p1, 2 * b + k + 1)
                    pool.wait_ge(s_r1, 2 * b + k + 1)
                    pool.tensor_tensor(part[:, b % 2, k, 2, :], rest[:, k, :], part[:, b % 2, k, 1, :],
                                       ALU.subtract).then_inc(s_p2, 1)
                pool.wait_ge(s_xn, TPB * (b + 1))
                pool.tensor_tensor(x[:, b * TPB:(b + 1) * TPB, :], x[:, b * TPB:(b + 1) * TPB, :],
                                   bc(w["bo"][:, :], TPB, 1), ALU.add).then_inc(s_bo, 1)

        @block.tensor
        def _(pe):
            def transposed(b):
                pe.wait_ge(s_xn, TPB * (b + 1))
                if b >= 2:
                    pe.wait_ge(s_tc, b - 1)
                for t in range(TPB):
                    mm = pe.transpose(ps[:, b % 2, t * P:(t + 1) * P], xn[:, b % 2, t, :], c["ident"][:, :])
                mm.then_inc(s_t, 1)

            transposed(0)
            for b in range(B):
                if b + 1 < B:
                    transposed(b + 1)
                pe.wait_ge(s_tc, b + 1)
                for m in range(4):
                    if b:
                        pe.wait_ge(s_rot, 4 * (b - 1) + m + 1)
                    pe.matmul(ps[:, 2 + m, :], w["wqk"][:, m * P:(m + 1) * P], xnT[:, b % 2, :],
                              start=True, stop=True).then_inc(s_pr, 1)
                if b >= 2:
                    pe.wait_ge(s_v, b - 1)
                for t in range(TPB):
                    mm = pe.matmul(ps[:, 6 + b % 2, t * P:(t + 1) * P], xnT[:, b % 2, t * P:(t + 1) * P],
                                   w["wv"][:, :], start=True, stop=True)
                mm.then_inc(s_pr, 1)

        @block.sync
        def _(sp):
            for par in range(2):
                for hat, name in ((hatq, "zero_rows"), (hatk, "one_rows")):
                    sp.dma_start(hat[MROW:KROWS, par, :, :], bc(c[name][:, :], NH, 1)).then_inc(s_hat["fill"], 16)
            for b in range(B):
                for k in range(2):
                    sp.wait_ge(s_p2, 2 * b + k + 1)
                    sp.dma_start(parts_dram[b, k].rearrange("i p t -> p i t"),
                                 part[:, b % 2, k, :, :]).then_inc(s_store[b % 2], 16)
                sp.wait_ge(s_store[b % 2], 32 * (b // 2 + 1))
                if b == 0:
                    load_hats(sp, b, parts_dram, hatq, hatk, s_hat)


def load_hats(sp, b, parts_dram, hatq, hatk, s_hat):
    for i in range(3):
        for j in range(3):
            rows = slice((3 * i + j) * DH, (3 * i + j + 1) * DH)
            for hat, k, p in ((hatq, 0, i), (hatk, 1, j)):
                sp.dma_start(hat[rows, b % 2, :, :],
                             parts_dram[b, k, p].rearrange("(h d) t -> d h t", d=DH)).then_inc(s_hat[b % 2], 16)


def attention(nc, ps, x, c, w, parts_dram, hatq, hatk, vall, s_hat):
    with ExitStack() as ctx:
        def sb(name, shape, dt=F32):
            return ctx.enter_context(nc.sbuf_tensor(f"at_{name}", shape, dt))

        sem = phase_semaphores(nc, ctx, "at")

        pt = sb("pt", [P, 2, 5, 2 * S])
        vext = sb("vext", [P, TPB, NH, 32])
        mx = sb("mx", [P, 2, TPB, HG])
        mh = sb("mh", [P, TPB, 2, HG], BF16)
        mT = sb("mT", [2 * HG, S], BF16)
        oT = sb("oT", [P, GROUPS, S])
        rden = sb("rden", [P, NH])
        on = sb("on", [P, TPB, D])
        onT = sb("onT", [P, S])
        s_a, s_ar, s_b, s_e = sem("a_psum"), sem("a_max"), sem("b_psum"), sem("b_exp")
        s_pv, s_oc, s_vx, s_fill = sem("pv"), sem("o_copied"), sem("values_placed"), sem("fill")
        s_mh, s_mt, s_mc, s_md = sem("max_negated"), sem("maxT_psum"), sem("maxT_copied"), sem("max_rows")
        s_tt, s_tc, s_rd = sem("tail_psum"), sem("tail_read"), sem("denominator")
        s_causal = sem("causal")
        s_zr = [sem("rows_zeroed0"), sem("rows_zeroed1")]
        bankA = lambda k: ps[:, k % 2, :]
        chunkB = lambda k: ps[:, 2 + 2 * (k % 2):4 + 2 * (k % 2), :]
        bankO, bankM = ps[:, 6, :], ps[:, 7, :]
        block = ctx.enter_context(nc.Block())

        A_CHUNKS = [[(h, 3, 0)] for h in range(4)] + [[(h, 2, 0), (h, 0, 384)] for h in range(4)] \
            + [[(h, 1, 0), (h + 1, 1, 256)] for h in (0, 2)]
        B_CHUNKS = [[(h, 0, 0, 0), (h, 1, 1, 0), (h, 3, 1, 384)] for h in range(4)] \
            + [[(h, 2, h // 2, 256 * (h % 2)) for h in range(4)]]
        PLACE = {(h, k): (n, S * bank + col) for n, ch in enumerate(B_CHUNKS) for h, k, bank, col in ch}

        def tail_rounds_before(u):
            b, g = (u - 1) // GROUPS, (u - 1) % GROUPS
            return max(0, 6 * (b - 1) + (0, 0, 4, 6)[g])

        TAIL = {(1, 1): 0, (1, 2): 1, (1, 3): 2, (1, 4): 3, (2, 1): 4, (2, 2): 5}

        @block.tensor
        def _(pe):
            def a_chunk(u, k):
                b, g, n = u // GROUPS, u % GROUPS, 10 * u + k
                if u % GROUPS == 0 and k == 0:
                    pe.wait_ge(s_hat[b % 2], 288 * (b // 2 + 1))
                    if b >= 2:
                        pe.wait_ge(s_zr[b % 2], 16 * (b // 2))
                if n >= 2:
                    pe.wait_ge(s_ar, n - 1)
                for h, t, col in A_CHUNKS[k]:
                    hh = HG * g + h
                    pe.matmul(bankA(n)[:, col:col + (t + 1) * P], hatq[0:KROWS, b % 2, hh, t * P:(t + 1) * P],
                              hatk[0:KROWS, b % 2, hh, 0:(t + 1) * P], start=True, stop=True)
                    mm = pe.matmul(bankA(n)[:, col + t * P:col + (t + 1) * P], c["ident_bf"][:, :],
                                   c["mask_q_bf"][:, :], start=False, stop=True, skip_group_check=True)
                mm.then_inc(s_a, 1)

            def b_chunk(u, k):
                b, g, n = u // GROUPS, u % GROUPS, 5 * u + k
                if k == 0:
                    pe.wait_ge(s_md, 32 * (u + 1))
                if n >= 2:
                    pe.wait_ge(s_e, n - 1)
                for h, t, bank, col in B_CHUNKS[k]:
                    hh = HG * g + h
                    mm = pe.matmul(chunkB(n)[:, bank, col:col + WIDTH[t]], hatk[0:KROWS, b % 2, hh, t * P:(t + 1) * P],
                              hatq[0:KROWS, b % 2, hh, t * P:S], start=True, stop=True)
                mm.then_inc(s_b, 1)

            def pv(u, t):
                b, g = u // GROUPS, u % GROUPS
                if t == 0:
                    pe.wait_ge(s_e, 5 * (u + 1))
                    pe.wait_ge(s_causal, 4 * (u + 1))
                    if u:
                        pe.wait_ge(s_oc, u)
                    if g == 0:
                        pe.wait_ge(s_vx, b + 1)
                for h in range(HG):
                    chunk, col = PLACE[h, t]
                    mm = pe.matmul(bankO[32 * h:32 * h + 32, t * P:S], vext[:, t, HG * g + h, :],
                                   pt[:, u % 2, chunk, col:col + WIDTH[t]],
                                   start=(t == 0), stop=(t == TPB - 1), skip_group_check=True)
                if t == TPB - 1:
                    mm.then_inc(s_pv, 1)

            def max_rows(u):
                pe.wait_ge(s_mh, 2 * (u + 1))
                if u:
                    pe.wait_ge(s_mc, u)
                if u > GROUPS + 1 and tail_rounds_before(u):
                    pe.wait_ge(s_tc, tail_rounds_before(u))
                out = bankM.bitcast(BF16)
                for t in range(TPB):
                    mm = pe.transpose(out[0:2 * HG, t * P:(t + 1) * P],
                                      mh[:, t, :, :].rearrange("p i h -> p (i h)"), c["ident_bf"][:, :])
                mm.then_inc(s_mt, 1)

            def tail(b, r):
                if r == 0:
                    pe.wait_ge(s_oc, GROUPS * (b + 1))
                if r in (0, 4):
                    pe.wait_ge(s_mc, min(GROUPS * (b + 1) + 3 + r // 4, UNITS))
                if b or r:
                    pe.wait_ge(s_tc, 6 * b + r)
                for t in range(TPB):
                    dst = bankM[:, t * P:(t + 1) * P]
                    if r < 4:
                        mm = pe.transpose(dst, oT[:, t, r * P:(r + 1) * P], c["ident"][:, :])
                    elif r == 4:
                        mm = pe.transpose(dst, on[:, t, :], c["ident"][:, :])
                    else:
                        mm = pe.matmul(dst, onT[:, t * P:(t + 1) * P], w["wo"][:, :], start=True, stop=True)
                mm.then_inc(s_tt, 1)

            pe.wait_ge(s_fill, 2)
            pe.wait_ge(s_hat["fill"], 64)
            for u in range(2):
                for k in range(10):
                    a_chunk(u, k)
                    if (u, k) == (1, 1):
                        max_rows(0)
            for u in range(UNITS):
                b, g = u // GROUPS, u % GROUPS
                for k in range(5):
                    if u + 2 < UNITS:
                        a_chunk(u + 2, 2 * k)
                    b_chunk(u, k)
                    if u + 2 < UNITS:
                        a_chunk(u + 2, 2 * k + 1)
                    if u and k < TPB:
                        pv(u - 1, k)
                    if k == 0 and u + 1 < UNITS:
                        max_rows(u + 1)
                    if b and (g, k) in TAIL:
                        tail(b - 1, TAIL[g, k])
            for t in range(TPB):
                pv(UNITS - 1, t)
            for r in range(6):
                tail(B - 1, r)

        @block.vector
        def _(dve):
            def a_max(u, k):
                n = 10 * u + k
                dve.wait_ge(s_a, n + 1)
                if k == 0 and u >= 2:
                    dve.wait_ge(s_mh, 2 * (u - 1))
                chunk = A_CHUNKS[k]
                if len(chunk) == 2 and chunk[0][1] == chunk[1][1]:
                    h, t, _ = chunk[0]
                    m = dve.tensor_reduce(mx[:, u % 2, t, h:h + 2], bankA(n).rearrange("p (h c) -> p h c", h=2),
                                          AX.X, ALU.max)
                else:
                    for h, t, col in chunk:
                        m = dve.tensor_reduce(mx[:, u % 2, t, h:h + 1], bankA(n)[:, col:col + (t + 1) * P],
                                              AX.X, ALU.max)
                m.then_inc(s_ar, 1)

            def negate(u):
                dve.wait_ge(s_ar, 10 * (u + 1))
                if u:
                    dve.wait_ge(s_mt, u)
                dve.tensor_scalar(mh[:, :, 0, :], mx[:, u % 2, :, :], -1.0, None, ALU.mult).then_inc(s_mh, 1)
                dve.wait_ge(s_mh, 2 * u + 1)
                dve.scalar_tensor_tensor(mh[:, :, 1, :], mx[:, u % 2, :, :], -1.0, mh[:, :, 0, :],
                                         ALU.mult, ALU.subtract).then_inc(s_mh, 1)

            def rows_copy(u):
                dve.wait_ge(s_mt, u + 1)
                if u:
                    dve.wait_ge(s_md, 32 * u)
                dve.tensor_copy(mT[:, :], bankM.bitcast(BF16)[0:2 * HG, 0:S]).then_inc(s_mc, 1)

            def place_values(b):
                if b:
                    dve.wait_ge(s_pv, GROUPS * b)
                src = vall[:, b * TPB:(b + 1) * TPB, :].rearrange("p t (h d) -> p (t h) d", d=DH)
                dve.tensor_copy(vext[:, :, :, 0:DH].rearrange("p t h d -> p (t h) d"), src).then_inc(s_vx, 1)

            def tail(b, r):
                dve.wait_ge(s_tt, 6 * b + r + 1)
                if r < 4:
                    o = bankM.rearrange("p (h c) -> p h c", c=32)
                    if b or r:
                        dve.wait_ge(s_tc, 6 * b + r)
                    dve.reciprocal(rden[:, :], o[:, :, DH]).then_inc(s_rd, 1)
                    dve.wait_ge(s_rd, 4 * b + r + 1)
                    dve.tensor_tensor(on[:, r, :].rearrange("p (h d) -> p h d", d=DH), o[:, :, 0:DH],
                                      bc(rden[:, :], DH, 2), ALU.mult).then_inc(s_tc, 1)
                elif r == 4:
                    dve.tensor_copy(onT[:, :], bankM).then_inc(s_tc, 1)
                else:
                    xb = x[:, b * TPB:(b + 1) * TPB, :]
                    dve.tensor_tensor(xb, bankM.rearrange("p (t d) -> p t d", d=D), xb, ALU.add).then_inc(s_tc, 1)

            dve.memset(vext[:, :, :, :], 0.0).then_inc(s_fill, 1)
            dve.wait_ge(s_fill, 1)
            dve.memset(vext[:, :, :, DH:DH + 1], 1.0).then_inc(s_fill, 1)
            place_values(0)
            for u in range(2):
                for k in range(10):
                    a_max(u, k)
                negate(u)
                if u == 0:
                    rows_copy(u)
            for u in range(UNITS):
                b, g = u // GROUPS, u % GROUPS
                for k in range(5):
                    if u + 2 < UNITS:
                        a_max(u + 2, 2 * k)
                        a_max(u + 2, 2 * k + 1)
                    if k == 0 and u + 1 < UNITS:
                        rows_copy(u + 1)
                    if g == 0 and b and k == 3:
                        place_values(b)
                    if b and (g, k) in TAIL:
                        tail(b - 1, TAIL[g, k])
                if u + 2 < UNITS:
                    negate(u + 2)
            for r in range(6):
                tail(B - 1, r)

        @block.scalar
        def _(act):
            def o_copy(u):
                b, g = u // GROUPS, u % GROUPS
                act.wait_ge(s_pv, u + 1)
                if g == 0 and b:
                    act.wait_ge(s_tt, 6 * (b - 1) + 4)
                act.activation(oT[:, g, :], bankO, ACT.Copy).then_inc(s_oc, 1)

            for u in range(UNITS):
                for k in range(5):
                    n = 5 * u + k
                    act.wait_ge(s_b, n + 1)
                    if k == 0 and u >= 2:
                        act.wait_ge(s_pv, u - 1)
                    act.activation(pt[:, u % 2, k, :], chunkB(n).rearrange("p a b -> p (a b)"), ACT.Exp).then_inc(s_e, 1)
                    if k == 4 and u:
                        o_copy(u - 1)
            o_copy(UNITS - 1)

        @block.gpsimd
        def _(pool):
            for u in range(UNITS):
                pool.wait_ge(s_e, 5 * (u + 1))
                for t in range(TPB):
                    chunk, col = PLACE[0, t]
                    if t == 2:
                        own = pt[:, u % 2, chunk, :].rearrange("p (h q) -> p h q", h=HG)[:, :, 0:P]
                    else:
                        own = pt[:, u % 2, 0:HG, col:col + P]
                    pool.affine_select(out=own, in_=own, compare_op=ALU.is_ge, fill=0.0, base=0,
                                       pattern=[[0, HG], [1, P]], channel_multiplier=-1).then_inc(s_causal, 1)

        @block.sync
        def _(sp):
            load_hats(sp, 1, parts_dram, hatq, hatk, s_hat)
            for u in range(UNITS):
                b, g = u // GROUPS, u % GROUPS
                if g == 2 and b + 1 in range(2, B):
                    sp.wait_ge(s_b, 5 * GROUPS * b)
                    sp.dma_start(hatq[MROW:MROW + 2, (b + 1) % 2, :, :], bc(c["zero_rows"][0:2, :], NH, 1)).then_inc(s_zr[(b + 1) % 2], 16)
                    load_hats(sp, b + 1, parts_dram, hatq, hatk, s_hat)
                sp.wait_ge(s_mc, u + 1)
                for i in range(2):
                    sp.dma_start(hatq[MROW + i:MROW + i + 1, b % 2, HG * g:HG * (g + 1), :],
                                 mT[HG * i:HG * (i + 1), :]).then_inc(s_md, 16)


NF, NB = 64, 4
NFFT = 2 * S
R4 = 4
HALF = S // 2
KT = HALF // P
COLS = 2 * B * NF
TWO_PI = 2 * np.pi
TWO_PI_HI = 6.28125
PI_BELOW = 3.1415925


class Moments:

    def __init__(self, sb, sem, tag):
        self.stats = sb(f"{tag}_stats", [P, NT, 6])
        self.mv = sb(f"{tag}_mv", [P, NT, 2])
        self.std = sb(f"{tag}_std", [P, NT])
        self.rstd = sb(f"{tag}_rstd", [P, NT])
        self.s_st, self.s_mv, self.s_std = sem(f"{tag}_stats"), sem(f"{tag}_moments"), sem(f"{tag}_std")
        self.s_rstd, self.s_done = sem(f"{tag}_rstd"), sem(f"{tag}_normalized")

    def moments(self, dve, src):
        for t in range(NT):
            dve.bn_stats(self.stats[:, t, :], src[:, t, :]).then_inc(self.s_st, 1)
        dve.wait_ge(self.s_st, NT)
        for t in range(NT):
            dve.bn_aggr(self.mv[:, t, :], self.stats[:, t, :]).then_inc(self.s_mv, 1)

    def root(self, act, eps):
        act.wait_ge(self.s_mv, NT)
        act.activation(self.std[:, :], self.mv[:, :, 1], ACT.Sqrt, bias=eps[:, 0:1]).then_inc(self.s_std, 1)

    def normalize(self, dve, dst, src):
        dve.wait_ge(self.s_std, 1)
        dve.reciprocal(self.rstd[:, :], self.std[:, :]).then_inc(self.s_rstd, 1)
        dve.wait_ge(self.s_rstd, 1)
        for t in range(NT):
            dve.tensor_scalar(dst[:, t, :], src[:, t, :], self.mv[:, t, 0:1], self.rstd[:, t:t + 1],
                              ALU.subtract, ALU.mult).then_inc(self.s_done, 1)


def ssm_project(nc, ps, x, c, w, xi, xh, cp, gate, U, K):
    with ExitStack() as ctx:
        def sb(name, shape, dt=F32):
            return ctx.enter_context(nc.sbuf_tensor(f"sp_{name}", shape, dt))

        sem = phase_semaphores(nc, ctx, "sp")

        outer, inner = Moments(sb, sem, "outer"), Moments(sb, sem, "inner")
        xnT = sb("xnT", [P, 2, S])
        sig = sb("sig", [P, 4, S])
        uT = sb("uT", [P, 2, S])
        pw = sb("pw", [P, S + 1])
        k1 = sb("k1", [P, S])
        kT = sb("kT", [P, 2, S])
        turn = sb("turn", [P, S])
        angle = sb("angle", [P, S])
        wave = sb("wave", [P, S])
        col = sb("col", [P, 12])
        erow = sb("erow", [P, NF])
        s_ch, s_a = sem("dve_chain"), sem("act_setup")
        s_dv, s_red, s_wave = sem("dve_setup"), sem("angles"), sem("wave")
        s_t, s_tc = sem("xnT_psum"), sem("xnT_copied")
        s_pr = sem("projected")
        s_sig = sem("sigmoids")
        s_u, s_cp, s_k1, s_k = sem("inputs"), sem("concept"), sem("kernel_size"), sem("kernel")
        s_ut, s_kt, s_uc, s_kc = sem("inputs_psum"), sem("kernel_psum"), sem("inputs_copied"), sem("kernel_copied")
        PROJ = [("fg", 2), ("band", 3), ("tg", 4), ("sp", 5), ("concept", 6), ("cg", 7), ("gate", 2)]
        block = ctx.enter_context(nc.Block())

        @block.vector
        def _(dve):
            ch = Chain(dve, s_ch)
            outer.moments(dve, x)
            ch.link(dve.tensor_reduce(col[:, 0:1], w["fi_row"][:, :], AX.X, ALU.max))
            dve.tensor_scalar(col[:, 1:2], col[:, 0:1], -1.0, None, ALU.mult).then_inc(s_dv, 1)
            outer.normalize(dve, xi, x)
            dve.wait_ge(outer.s_done, NT)
            inner.moments(dve, xi)
            dve.wait_ge(s_a, 4)
            ch.link(dve.reciprocal(col[:, 6:7], col[:, 2:3]))
            ch.link(dve.tensor_scalar(col[:, 7:8], col[:, 3:4], col[:, 6:7], float(NF), ALU.mult, ALU.mult))
            ch.link(dve.tensor_tensor(col[:, 8:9], col[:, 7:8], col[:, 4:5], ALU.mult))
            ch.link(dve.tensor_scalar(col[:, 9:10], w["freq"][:, 0:1], 0.1, None, ALU.mult))
            ch.link(dve.tensor_scalar(col[:, 10:11], col[:, 5:6], col[:, 9:10], 2.0, ALU.mult, ALU.mult))
            ch.link(dve.tensor_scalar(angle[:, :], w["steps"][:, :], col[:, 10:11], w["quarter"][:, 0:1],
                                      ALU.mult, ALU.add))
            ch.link(dve.tensor_scalar(turn[:, :], angle[:, :], 1 / TWO_PI, ROUND, ALU.mult, ALU.add))
            ch.link(dve.tensor_scalar(turn[:, :], turn[:, :], ROUND, None, ALU.subtract))
            ch.link(dve.scalar_tensor_tensor(angle[:, :], turn[:, :], -TWO_PI_HI, angle[:, :], ALU.mult, ALU.add))
            ch.link(dve.scalar_tensor_tensor(angle[:, :], turn[:, :], -(TWO_PI - TWO_PI_HI), angle[:, :],
                                             ALU.mult, ALU.add))
            dve.tensor_scalar(angle[:, :], angle[:, :], PI_BELOW, -PI_BELOW, ALU.min, ALU.max).then_inc(s_red, 1)
            inner.normalize(dve, xh, xi)
            ch.link(dve.memset(pw[:, 0:1], 1.0))

            def affine(b):
                dve.wait_ge(s_t, b + 1)
                if b >= 2:
                    dve.wait_ge(s_pr, 7 * (b - 1))
                dve.tensor_scalar(xnT[:, b % 2, :], ps[:, b % 2, :], w["norm_gb"][:, 0:1], w["norm_gb"][:, 1:2],
                                  ALU.mult, ALU.add).then_inc(s_tc, 1)

            def copies(b):
                for bank, s, done, dst in ((3, s_ut, s_uc, U), (4, s_kt, s_kc, K)):
                    dve.wait_ge(s, b + 1)
                    for cc in range(2):
                        m = dve.tensor_copy(dst[:, :, cc, b, :],
                                            ps[:, bank, :].rearrange("p (t c n) -> p t c n", c=2, n=NF)[:, :, cc, :])
                    m.then_inc(done, 1)

            affine(0)
            for b in range(B):
                if b + 1 < B:
                    affine(b + 1)
                if b:
                    copies(b - 1)
                dve.wait_ge(s_pr, 7 * b + 4)
                dve.wait_ge(s_sig, 5 * b + 1)
                dve.tensor_tensor(uT[:, b % 2, :], ps[:, 5, :], sig[:, 0, :], ALU.mult).then_inc(s_u, 1)
                dve.wait_ge(s_sig, 5 * b + 2)
                if b:
                    dve.wait_ge(s_k1, b)
                ch.link(dve.tensor_tensor_scan(pw[:, 1:S + 1], sig[:, 1, :], col[:, 8:9].to_broadcast([P, S]), 1.0,
                                               ALU.mult, ALU.mult))
                dve.wait_ge(s_sig, 5 * b + 3)
                if b:
                    dve.wait_ge(s_k, b)
                dve.tensor_tensor(k1[:, :], pw[:, 0:S], sig[:, 2, :], ALU.mult).then_inc(s_k1, 1)
                dve.wait_ge(s_pr, 7 * b + 5)
                dve.wait_ge(s_sig, 5 * b + 4)
                dve.scalar_tensor_tensor(cp[:, b, :], ps[:, 6, :], w["bias"][:, 4:5], sig[:, 3, :],
                                         ALU.add, ALU.mult).then_inc(s_cp, 1)
            copies(B - 1)

        @block.scalar
        def _(act):
            outer.root(act, c["eps"])
            act.wait_ge(s_dv, 1)
            act.activation(erow[:, :], w["fi_row"][:, :], ACT.Exp, bias=col[:, 1:2], accum_out=col[:, 2:3]).then_inc(s_a, 1)
            act.activation(col[:, 3:4], w["fi_col"][:, 0:1], ACT.Exp, bias=col[:, 1:2]).then_inc(s_a, 1)
            act.activation(col[:, 4:5], w["log_decay"][:, 0:1], ACT.Sigmoid).then_inc(s_a, 1)
            act.activation(col[:, 5:6], w["dt"][:, 0:1], ACT.Sigmoid).then_inc(s_a, 1)
            inner.root(act, c["eps"])
            act.wait_ge(s_red, 1)
            act.activation(wave[:, :], angle[:, :], ACT.Sin).then_inc(s_wave, 1)
            for b in range(B):
                for k, (m, bias) in enumerate(((1, 0), (2, 1), (3, 2), (6, 3), (7, 5))):
                    act.wait_ge(s_pr, 7 * b + m)
                    if b:
                        if k == 0:
                            act.wait_ge(s_u, b)
                        elif k == 1:
                            act.wait_ge(s_k1, b)
                        elif k == 3:
                            act.wait_ge(s_cp, b)
                    dst = sig[:, k, :] if k < 4 else gate[:, b, :]
                    act.activation(dst, ps[:, PROJ[m - 1][1], :], ACT.Sigmoid,
                                   bias=w["bias"][:, bias:bias + 1]).then_inc(s_sig, 1)

        @block.gpsimd
        def _(pool):
            pool.wait_ge(s_wave, 1)
            for b in range(B):
                pool.wait_ge(s_k1, b + 1)
                if b >= 2:
                    pool.wait_ge(s_kt, b - 1)
                pool.tensor_tensor(kT[:, b % 2, :], k1[:, :], wave[:, :], ALU.mult).then_inc(s_k, 1)

        @block.tensor
        def _(pe):
            def transposed(b):
                pe.wait_ge(inner.s_done, TPB * (b + 1))
                if b >= 2:
                    pe.wait_ge(s_tc, b - 1)
                for t in range(TPB):
                    mm = pe.transpose(ps[:, b % 2, t * P:(t + 1) * P], xh[:, b * TPB + t, :], c["ident"][:, :])
                mm.then_inc(s_t, 1)

            def by_token(b):
                for bank, s, ready, src in ((3, s_ut, s_u, uT), (4, s_kt, s_k, kT)):
                    pe.wait_ge(ready, b + 1)
                    pe.wait_ge(s_sig, 5 * b + 3)
                    for t in range(TPB):
                        mm = pe.transpose(ps[:, bank, t * P:(t + 1) * P], src[:, b % 2, t * P:(t + 1) * P],
                                          c["ident"][:, :])
                    mm.then_inc(s, 1)

            transposed(0)
            for b in range(B):
                if b + 1 < B:
                    transposed(b + 1)
                pe.wait_ge(s_tc, b + 1)
                for m, (_, bank) in enumerate(PROJ):
                    if b and m == 0:
                        pe.wait_ge(s_sig, 5 * b)
                    elif b and m == 1:
                        pe.wait_ge(s_uc, b)
                    elif b and m == 2:
                        pe.wait_ge(s_kc, b)
                    elif b and m == 3:
                        pe.wait_ge(s_u, b)
                    elif b and m == 4:
                        pe.wait_ge(s_cp, b)
                    elif m == 6:
                        pe.wait_ge(s_sig, 5 * b + 1)
                    pe.matmul(ps[:, bank, :], w["wproj"][:, m * P:(m + 1) * P], xnT[:, b % 2, :],
                              start=True, stop=True).then_inc(s_pr, 1)
                by_token(b)


def ssm_convolve(nc, ps, w, U, K, spec, tables_loaded):
    with ExitStack() as ctx:
        def sb(name, shape, dt=F32):
            return ctx.enter_context(nc.sbuf_tensor(f"cv_{name}", shape, dt))

        sem = phase_semaphores(nc, ctx, "cv")

        H = COLS // 2
        fold = [sb(f"fold{k}", [P, KT, 2, COLS]) for k in range(2)]
        uf = sb("uf", [P, 2, COLS])
        prod = sb("prod", [P, 2, 2, COLS])
        Y = sb("Y", [P, 4, COLS])
        even = sb("even", [P, KT, COLS])
        odd = sb("odd", [P, KT, COLS])
        sums = sb("sums", [P, 2, KT, COLS])
        s_fold = [sem("folded0"), sem("folded1")]
        s_f = sem("transformed")
        s_uf, s_pr, s_y = sem("uf_copied"), sem("products"), sem("Y")
        s_z, s_zc, s_cb, s_sp = sem("inverse"), sem("inverse_copied"), sem("combined"), sem("spectral")
        ORDER = (0, 2, 1, 3)
        flat = lambda a, t: a[:, t, :, :, :].rearrange("p c b n -> p (c b n)")
        bankU = lambda n: ps[:, n % 2, :]
        bankK = lambda n: ps[:, 2 + n % 2, :]
        bankZ = lambda q, mt: ps[:, 4 + 2 * (q % 2) + mt, :]
        block = ctx.enter_context(nc.Block())

        def folds(eng, k, src):
            for q, r in enumerate(ORDER):
                if q >= 2:
                    eng.wait_ge(s_f, 4 * (q - 1))
                for kt in range(KT):
                    a, z, o = flat(src, kt), flat(src, KT + kt), fold[k][:, kt, q % 2, :]
                    if r % 2 == 0:
                        m = eng.tensor_tensor(o, a, z, ALU.subtract if r else ALU.add)
                    else:
                        ops = (ALU.add, ALU.subtract) if r == 1 else (ALU.subtract, ALU.add)
                        eng.tensor_tensor(o[:, 0:H], a[:, 0:H], z[:, H:COLS], ops[0])
                        m = eng.tensor_tensor(o[:, H:COLS], a[:, H:COLS], z[:, 0:H], ops[1])
                m.then_inc(s_fold[k], 1)
                yield

        @block.vector
        def _(dve):
            step = folds(dve, 0, U)
            next(step)
            next(step)

            def multiply(n):
                dve.wait_ge(s_f, 2 * n + 2)
                dve.wait_ge(s_uf, n + 1)
                if n >= 2:
                    dve.wait_ge(s_y, 2 * (n - 1))
                u, k, p = uf[:, n % 2, :], bankK(n), prod[:, n % 2, :, :]
                for half in range(2):
                    dve.tensor_tensor(p[:, 0, half * H:(half + 1) * H], u[:, half * H:(half + 1) * H], k[:, 0:H], ALU.mult)
                    m = dve.tensor_tensor(p[:, 1, half * H:(half + 1) * H], u[:, (1 - half) * H:(2 - half) * H],
                                          k[:, H:COLS], ALU.mult)
                m.then_inc(s_pr, 1)

            def combine(q):
                for mt in range(KT):
                    dve.wait_ge(s_z, KT * q + mt + 1)
                    if mt == 0:
                        dve.wait_ge(s_zc, KT * (q // 2 + 1))
                    z, e = bankZ(q, mt), (even if q == 1 else odd)[:, mt, :]
                    dve.tensor_tensor(sums[:, q // 2, mt, :], e, z, ALU.add).then_inc(s_cb, 1)
                    dve.tensor_tensor(e, e, z, ALU.subtract).then_inc(s_cb, 1)

            for q in range(R4):
                for gt in range(KT):
                    multiply(KT * q + gt)
                if q < 2:
                    next(step)
                if q == 2:
                    combine(1)
            combine(3)

        @block.gpsimd
        def _(pool):
            step = folds(pool, 1, K)
            next(step)
            next(step)
            for n in range(R4 * KT):
                pool.wait_ge(s_pr, n + 1)
                if n >= 4:
                    pool.wait_ge(s_z, KT * ((n - 4) // KT + 1))
                p, y = prod[:, n % 2, :, :], Y[:, n % 4, :]
                pool.tensor_tensor(y[:, 0:H], p[:, 0, 0:H], p[:, 1, 0:H], ALU.subtract).then_inc(s_y, 1)
                pool.tensor_tensor(y[:, H:COLS], p[:, 0, H:COLS], p[:, 1, H:COLS], ALU.add).then_inc(s_y, 1)
                if n in (1, 3):
                    next(step)
            pool.wait_ge(s_cb, 8)
            for mt in range(KT):
                part = lambda a, cc: a[:, mt, cc * H:(cc + 1) * H].rearrange("p (b n) -> p b n", n=NF)
                to = lambda t, cc: spec[:, t, :, cc, :]
                for cc in range(2):
                    pool.tensor_tensor(to(mt, cc), part(sums[:, 0], cc), part(sums[:, 1], cc), ALU.add)
                pool.tensor_tensor(to(KT + mt, 0), part(even, 0), part(odd, 1), ALU.subtract)
                pool.tensor_tensor(to(KT + mt, 1), part(even, 1), part(odd, 0), ALU.add).then_inc(s_sp, 1)

        @block.scalar
        def _(act):
            def z_copy(q, dst):
                for mt in range(KT):
                    act.wait_ge(s_z, KT * q + mt + 1)
                    act.activation(dst[:, mt, :], bankZ(q, mt), ACT.Copy).then_inc(s_zc, 1)

            for n in range(R4 * KT):
                act.wait_ge(s_f, 2 * n + 1)
                if n >= 2:
                    act.wait_ge(s_pr, n - 1)
                act.activation(uf[:, n % 2, :], bankU(n), ACT.Copy).then_inc(s_uf, 1)
                if n == 3:
                    z_copy(0, even)
                if n == 7:
                    z_copy(2, odd)

        @block.tensor
        def _(pe):
            pe.wait_ge(tables_loaded, 32)

            def transform(q, gt, k):
                r, n = ORDER[q], KT * q + gt
                bank = (bankU if k == 0 else bankK)(n)
                pe.wait_ge(s_fold[k], q + 1)
                if n >= 2:
                    if k == 0:
                        pe.wait_ge(s_uf, n - 1)
                    else:
                        pe.wait_ge(s_pr, n - 1)
                v = fold[k][:, :, q % 2, :]
                tab = lambda kt, j: w["forward"][:, kt, r, gt, j, :]
                pe.matmul(bank, tab(0, 0), v[:, 0, :], start=True, stop=False)
                for kt in range(KT):
                    pe.matmul(bank[:, 0:H], tab(kt, 1), v[:, kt, H:COLS], start=False, stop=False,
                              skip_group_check=True)
                    pe.matmul(bank[:, H:COLS], tab(kt, 2), v[:, kt, 0:H], start=False, stop=False,
                              skip_group_check=True)
                pe.matmul(bank, tab(1, 0), v[:, 1, :], start=False, stop=True).then_inc(s_f, 1)

            def inverse(q):
                r = ORDER[q]
                pe.wait_ge(s_y, 2 * KT * (q + 1))
                if q == 2:
                    pe.wait_ge(s_zc, KT)
                if q == 3:
                    pe.wait_ge(s_cb, 4)
                for mt in range(KT):
                    bank = bankZ(q, mt)
                    tab = lambda gt, j: w["inverse"][:, gt, r, mt, j, :]
                    y = lambda gt: Y[:, (KT * q + gt) % 4, :]
                    pe.matmul(bank, tab(0, 0), y(0), start=True, stop=False)
                    for gt in range(KT):
                        pe.matmul(bank[:, 0:H], tab(gt, 2), y(gt)[:, H:COLS], start=False, stop=False,
                                  skip_group_check=True)
                        pe.matmul(bank[:, H:COLS], tab(gt, 1), y(gt)[:, 0:H], start=False, stop=False,
                                  skip_group_check=True)
                    pe.matmul(bank, tab(1, 0), y(1), start=False, stop=True).then_inc(s_z, 1)

            for q in range(R4):
                for gt in range(KT):
                    transform(q, gt, 0)
                    transform(q, gt, 1)
                if q:
                    inverse(q - 1)
            inverse(R4 - 1)


def ssm_output(nc, ps, x, c, w, xi, xh, cp, gate, spec):
    with ExitStack() as ctx:
        def sb(name, shape, dt=F32):
            return ctx.enter_context(nc.sbuf_tensor(f"so_{name}", shape, dt))

        sem = phase_semaphores(nc, ctx, "so")

        ln = Moments(sb, sem, "ln")
        specT = sb("specT", [P, 2, S])
        gated = sb("gated", [P, 2, S])
        scale = sb("scale", [P, 1])
        xnT = sb("xnT", [P, 2, S])
        hid = sb("hid", [P, 2, FT, S])
        s_ch = sem("dve_chain")
        s_st, s_sc, s_yp, s_ga, s_gt, s_xi = (sem(k) for k in ("specT_psum", "specT_copied", "y_psum", "gated", "gated_psum", "xi"))
        s_t, s_tc, s_h, s_hg, s_o, s_x, s_xs = (sem(k) for k in ("xnT_psum", "xnT", "hidden_psum", "hidden", "out_psum", "x", "x_xi"))
        block = ctx.enter_context(nc.Block())

        @block.vector
        def _(dve):
            ch = Chain(dve, s_ch)
            ch.link(dve.tensor_scalar(scale[:, :], w["output_scale"][:, 0:1], 0.5, None, ALU.mult))
            for b in range(B):
                dve.wait_ge(s_yp, b + 1)
                if b >= 2:
                    dve.wait_ge(s_gt, b - 1)
                ch.link(dve.scalar_tensor_tensor(gated[:, b % 2, :], ps[:, 2 + b % 2, :], scale[:, 0:1], gate[:, b, :],
                                                 ALU.mult, ALU.mult))
                dve.scalar_tensor_tensor(gated[:, b % 2, :], cp[:, b, :], 0.5, gated[:, b % 2, :],
                                         ALU.mult, ALU.add).then_inc(s_ga, 1)
                dve.wait_ge(s_gt, b + 1)
                xb = xi[:, b * TPB:(b + 1) * TPB, :]
                dve.tensor_tensor(xb, ps[:, 4 + b % 2, :].rearrange("p (t d) -> p t d", d=D), xb, ALU.add).then_inc(s_xi, 1)
            dve.wait_ge(s_xi, B)
            ln.moments(dve, xi)
            ln.normalize(dve, xh, xi)

            def affine(b):
                dve.wait_ge(s_t, b + 1)
                if b >= 2:
                    dve.wait_ge(s_h, FT * (b - 1))
                dve.tensor_scalar(xnT[:, b % 2, :], ps[:, b % 2, :], w["norm2_gb"][:, 0:1], w["norm2_gb"][:, 1:2],
                                  ALU.mult, ALU.add).then_inc(s_tc, 1)

            affine(0)
            for b in range(B):
                if b + 1 < B:
                    affine(b + 1)
                dve.wait_ge(s_o, b + 1)
                dve.wait_ge(s_xs, 2 * (b + 1))
                xb = x[:, b * TPB:(b + 1) * TPB, :]
                dve.tensor_tensor(xb, ps[:, 6 + b % 2, :].rearrange("p (t d) -> p t d", d=D), xb, ALU.add).then_inc(s_x, 1)

        @block.gpsimd
        def _(pool):
            for b in range(B):
                xb = x[:, b * TPB:(b + 1) * TPB, :]
                pool.wait_ge(s_xi, b + 1)
                pool.tensor_tensor(xb, xb, xi[:, b * TPB:(b + 1) * TPB, :], ALU.add).then_inc(s_xs, 1)
                pool.wait_ge(s_xs, 2 * b + 1)
                pool.tensor_tensor(xb, xb, bc(w["b2"][:, :], TPB, 1), ALU.add).then_inc(s_xs, 1)

        @block.scalar
        def _(act):
            for b in range(B):
                act.wait_ge(s_st, b + 1)
                if b >= 2:
                    act.wait_ge(s_yp, b - 1)
                act.activation(specT[:, b % 2, :], ps[:, b % 2, :], ACT.Copy).then_inc(s_sc, 1)
            ln.root(act, c["eps"])
            for b in range(B):
                for f in range(FT):
                    act.wait_ge(s_h, FT * b + f + 1)
                    if b >= 2 and f == 0:
                        act.wait_ge(s_o, b - 1)
                    act.activation(hid[:, b % 2, f, :], ps[:, 2 + f, :], ACT.Gelu, bias=w["b1"][:, f:f + 1]).then_inc(s_hg, 1)

        @block.tensor
        def _(pe):
            def spectral(b):
                if b >= 2:
                    pe.wait_ge(s_sc, b - 1)
                for t in range(TPB):
                    mm = pe.transpose(ps[:, b % 2, t * P:(t + 1) * P], spec[:, t, b, :, :].rearrange("p c n -> p (c n)"), c["ident"][:, :])
                mm.then_inc(s_st, 1)

            def project(b):
                pe.wait_ge(s_sc, b + 1)
                if b >= 2:
                    pe.wait_ge(s_ga, b - 1)
                pe.matmul(ps[:, 2 + b % 2, :], w["wfs"][:, :], specT[:, b % 2, :], start=True, stop=True).then_inc(s_yp, 1)

            def by_token(b):
                pe.wait_ge(s_ga, b + 1)
                if b >= 2:
                    pe.wait_ge(s_xi, b - 1)
                for t in range(TPB):
                    mm = pe.transpose(ps[:, 4 + b % 2, t * P:(t + 1) * P], gated[:, b % 2, t * P:(t + 1) * P],
                                      c["ident"][:, :])
                mm.then_inc(s_gt, 1)

            spectral(0)
            for b in range(B):
                if b + 1 < B:
                    spectral(b + 1)
                project(b)
                by_token(b)

            def transposed(b):
                pe.wait_ge(ln.s_done, TPB * (b + 1))
                if b >= 2:
                    pe.wait_ge(s_tc, b - 1)
                for t in range(TPB):
                    mm = pe.transpose(ps[:, b % 2, t * P:(t + 1) * P], xh[:, b * TPB + t, :], c["ident"][:, :])
                mm.then_inc(s_t, 1)

            def hidden(b):
                pe.wait_ge(s_tc, b + 1)
                for f in range(FT):
                    if b:
                        pe.wait_ge(s_hg, FT * (b - 1) + f + 1)
                    pe.matmul(ps[:, 2 + f, :], w["w1"][:, f * P:(f + 1) * P], xnT[:, b % 2, :],
                              start=True, stop=True).then_inc(s_h, 1)

            def out(b):
                pe.wait_ge(s_hg, FT * (b + 1))
                if b >= 2:
                    pe.wait_ge(s_x, b - 1)
                for t in range(TPB):
                    for f in range(FT):
                        mm = pe.matmul(ps[:, 6 + b % 2, t * P:(t + 1) * P], hid[:, b % 2, f, t * P:(t + 1) * P],
                                       w["w2"][:, f, :], start=(f == 0), stop=(f == FT - 1))
                mm.then_inc(s_o, 1)

            transposed(0)
            for b in range(B):
                if b + 1 < B:
                    transposed(b + 1)
                hidden(b)
                if b:
                    out(b - 1)
            out(B - 1)


def constants():
    f = np.float32
    k = np.arange(P)
    rows = lambda a: np.ascontiguousarray(np.broadcast_to(np.asarray(a, f).reshape(1, -1), (P, np.size(a))))
    return {
        "ident": np.eye(P, dtype=f),
        "before": (k[:, None] < k[None, :]).astype(f),
        "falling": rows(np.arange(NE, 0, -1)),
        "region": rows(np.arange(NE) * REGION),
        "row_number": np.ascontiguousarray((np.arange(2 * NT)[None, :] * P + k[:, None]).astype(f)),
        "slot_tile": rows(np.arange(NSLOT)),
        "mask_q": np.where(k[None, :] > k[:, None], MASKED, 0).astype(f),
    }


def pad_rows():
    rows = np.zeros((2 * NE * P, ROW), np.float32)
    rows[:, D] = 2 * NT * P + np.arange(len(rows))
    return rows


def place_constants(nc, ctx, dram):
    c = {k: ctx.enter_context(nc.sbuf_tensor(f"c_{k}", list(v.shape), F32)) for k, v in dram.items()}
    for name, shape, dt in (("eps", [P, 1], F32), ("one", [P, NE], F32), ("zero", [P, D], F32),
                            ("ones_bf", [P, P], BF16), ("before_bf", [P, P], BF16), ("ident_bf", [P, P], BF16),
                            ("mask_q_bf", [P, P], BF16), ("zero_rows", [KROWS - MROW, S], BF16), ("one_rows", [KROWS - MROW, S], BF16)):
        c[name] = ctx.enter_context(nc.sbuf_tensor(f"c_{name}", shape, dt))
    s_const = ctx.enter_context(nc.semaphore("constants_loaded"))

    def load(block):
        @block.scalar
        def _(act):
            for k, v in dram.items():
                act.dma_start(c[k][:, :], v).then_inc(s_const, 16)

        @block.vector
        def _(dve):
            dve.memset(c["eps"][:, :], EPS)
            dve.memset(c["one"][:, :], 1.0)
            dve.memset(c["zero"][:, :], 0.0)
            dve.memset(c["ones_bf"][:, :], 1.0)
            dve.wait_ge(s_const, 16 * len(dram))
            dve.tensor_copy(c["before_bf"][:, :], c["before"][:, :])
            dve.memset(c["zero_rows"][:, :], 0.0)
            dve.memset(c["one_rows"][:, :], 1.0)
            for k in ("ident", "mask_q"):
                dve.tensor_copy(c[k + "_bf"][:, :], c[k][:, :])

    return c, load


def rotary():
    f = np.float32
    half = DH // 2
    inv = (1.0 / f(10000.0) ** (np.arange(half, dtype=f) / half)).astype(f)
    angle = (np.arange(S, dtype=f)[:, None] * inv[None, :]).astype(f)
    row = np.arange(P) % DH
    cos, sin = np.cos(angle)[:, row // 2].T, np.sin(angle)[:, row // 2].T
    sin = sin * np.where(row % 2, 1, -1)[:, None]
    r = 1 / np.sqrt(f(DH))
    return np.ascontiguousarray(np.stack([cos * r, sin * r, cos, sin], 1).astype(f))


def transform_tables():
    k = np.arange(HALF)
    out = []
    for inverse in range(2):
        tab = np.empty((P, KT, R4, KT, 3, P), np.float64)
        for r in range(R4):
            turns = np.outer(k, R4 * k + r)
            turns = (turns.T if inverse else turns) % NFFT
            a = turns * (TWO_PI / NFFT)
            for j, m in enumerate((np.cos(a), np.sin(a), -np.sin(a))):
                tab[:, :, r, :, j, :] = m.reshape(KT, P, KT, P).transpose(1, 0, 2, 3)
        out.append((tab / (NFFT if inverse else 1)).astype(np.float32))
    return out


def ssm_weights(inputs):
    g = lambda name: np.asarray(inputs[f"L0_attn_b_{name}"])
    twice = lambda a: np.concatenate([a, a], 0)
    col = lambda a: np.ascontiguousarray(a.reshape(-1, 1))
    band = lambda a: twice(np.repeat(a, NF // NB, 0))
    every = lambda a: np.repeat(a, P, 0)
    f = np.float32
    proj = [twice(g("Wfg")), band(g("Wband")), every(g("Wtg")), g("Wsp"), g("Wconcept"), g("Wcg"), g("Wgate")]
    bias = [twice(g("bfg")), band(g("bband")), every(g("btg")), g("bcg"), g("bconcept"), g("bgate")]
    return {
        "wproj": np.ascontiguousarray(np.concatenate(proj, 0).T),
        "bias": np.ascontiguousarray(np.stack(bias, 1)),
        "norm_gb": np.ascontiguousarray(np.stack([g("norm_g"), g("norm_b")], 1)),
        "norm2_gb": np.ascontiguousarray(np.stack([g("norm2_g"), g("norm2_b")], 1)),
        "fi_row": np.ascontiguousarray(np.broadcast_to(g("freq_importance")[None, :], (P, NF))),
        "fi_col": col(twice(g("freq_importance"))),
        "log_decay": col(twice(g("log_decay"))),
        "dt": col(twice(g("dt"))),
        "freq": col(twice(g("frequencies"))),
        "steps": np.ascontiguousarray(np.broadcast_to(np.arange(1, S + 1, dtype=f)[None, :], (P, S))),
        "quarter": col(np.repeat(np.array([np.pi / 2, 0], f), NF)),
        "output_scale": col(every(g("output_scale"))),
        "wfs": np.ascontiguousarray(g("Wfs").T),
        "w1": np.ascontiguousarray(g("W1").T),
        "b1": np.ascontiguousarray(g("b1").reshape(FT, P).T),
        "w2": np.ascontiguousarray(g("W2").reshape(D, FT, P).transpose(2, 1, 0)),
        "b2": np.ascontiguousarray(np.broadcast_to(g("b2")[None, :], (P, D))),
        "forward": transform_tables()[0],
        "inverse": transform_tables()[1],
    }


def ssm(nc, ps, x, c, dram):
    with ExitStack() as ctx:
        def sb(name, shape, dt=F32):
            return ctx.enter_context(nc.sbuf_tensor(f"sm_{name}", shape, dt))

        w = {k: sb(k, list(v.shape)) for k, v in dram.items()}
        xi, xh = sb("xi", [P, NT, D]), sb("xh", [P, NT, D])
        cp, gate = sb("cp", [P, B, S]), sb("gate", [P, B, S])
        s_tab = ctx.enter_context(nc.semaphore("sm_tables_loaded"))
        s_w = ctx.enter_context(nc.semaphore("sm_weights_loaded"))
        U, K = sb("U", [P, TPB, 2, B, NF]), sb("K", [P, TPB, 2, B, NF])
        spec = xh[:, :, :].rearrange("p (t b) (c n) -> p t b c n", b=B, n=NF)
        with nc.Block() as block:
            @block.sync
            def _(sp):
                small = [k for k in dram if k not in ("forward", "inverse")]
                for k in small:
                    sp.dma_start(w[k][tuple([slice(None)] * len(dram[k].shape))], dram[k]).then_inc(s_w, 16)
                sp.wait_ge(s_w, 16 * len(small))
                for k in ("forward", "inverse"):
                    sp.dma_start(w[k][tuple([slice(None)] * len(dram[k].shape))], dram[k]).then_inc(s_tab, 16)
        ssm_project(nc, ps, x, c, w, xi, xh, cp, gate, U, K)
        ssm_convolve(nc, ps, w, U, K, spec, s_tab)
        ssm_output(nc, ps, x, c, w, xi, xh, cp, gate, spec)


def attention_weights(inputs):
    g = lambda name: np.asarray(inputs[f"L0_attn_a_{name}"])
    swap = np.arange(P) ^ 1
    rows = lambda a: np.ascontiguousarray(np.broadcast_to(a[None, :], (P, P)))
    wq, wk, bq, bk = g("Wq"), g("Wk"), g("bq"), g("bk")
    return {
        "wqk": np.ascontiguousarray(np.concatenate([wq, wq[swap], wk, wk[swap]], 0).T),
        "qk_bias": np.ascontiguousarray(np.stack([bq, bq[swap], bk, bk[swap]], 1)),
        "rotary": rotary(),
        "wv": np.ascontiguousarray(g("Wv").T),
        "wo": np.ascontiguousarray(g("Wo").T),
        "bv": rows(g("bv")),
        "bo": rows(g("bo")),
    }


def moe_weights(inputs):
    g = lambda name: np.asarray(inputs[f"L0_ffn_{name}"])
    return {
        "w1": np.ascontiguousarray(g("W1").transpose(2, 0, 1).reshape(P, NE * DFF)),
        "w2": np.ascontiguousarray(g("W2").reshape(NE, D, FT, P).transpose(3, 0, 2, 1).reshape(P, NE * DFF)),
        "wr": np.ascontiguousarray(g("Wr").T),
    }


def whole(nc, x_dram, out_dram, pads, consts, att, ssm_w, moe_w):
    whole_of = lambda t: t[tuple([slice(None)] * len(t.shape))]
    with ExitStack() as ctx:
        ps = ctx.enter_context(nc.psum_tensor("ps", [P, 8, S], F32))
        x = ctx.enter_context(nc.sbuf_tensor("x", [P, NT, D], F32))
        mw = {k: ctx.enter_context(nc.sbuf_tensor(f"moe_{k}", list(v.shape), F32)) for k, v in moe_w.items()}
        c, load = place_constants(nc, ctx, consts)
        s_x = ctx.enter_context(nc.semaphore("x_loaded"))
        s_mw = ctx.enter_context(nc.semaphore("moe_weights_loaded"))
        s_out = ctx.enter_context(nc.semaphore("out_stored"))
        xs = nc.dram_tensor("expert_rows", [NE * (REGION + P), ROW], F32, kind="Internal").ap()
        ys = nc.dram_tensor("expert_results", [2 * (NT + NE) * P, D], F32, kind="Internal").ap()
        parts = nc.dram_tensor("parts", [B, 2, 3, P, S], BF16, kind="Internal").ap()
        x_rows = x_dram.rearrange("b (t p) d -> p (b t) d", p=P)
        out_rows = out_dram.rearrange("b (t p) d -> p (b t) d", p=P)

        with ExitStack() as actx:
            w = {k: actx.enter_context(nc.sbuf_tensor(f"w_{k}", list(v.shape), F32)) for k, v in att.items()}
            hatq = actx.enter_context(nc.sbuf_tensor("hatq", [KROWS, 2, NH, S], BF16))
            hatk = actx.enter_context(nc.sbuf_tensor("hatk", [KROWS, 2, NH, S], BF16))
            vall = actx.enter_context(nc.sbuf_tensor("vall", [P, NT, D], F32))
            s_hat = {k: actx.enter_context(nc.semaphore(f"hat_{k}")) for k in (0, 1, "fill")}
            with nc.Block() as block:
                @block.sync
                def _(sp):
                    sp.dma_start(x[:, :, :], x_rows).then_inc(s_x, 16)
                    for k, v in w.items():
                        sp.dma_start(whole_of(v), att[k]).then_inc(s_x, 16)
                    for k, v in mw.items():
                        sp.dma_start(whole_of(v), moe_w[k]).then_inc(s_mw, 16)
                    sp.wait_ge(s_x, 16 * (1 + len(w)))

                load(block)
            attention_prepare(nc, ps, x, c, w, parts, hatq, hatk, vall, s_hat)
            attention(nc, ps, x, c, w, parts, hatq, hatk, vall, s_hat)
        moe(nc, "moe0", ps, x, c, mw, pads, xs, ys, s_mw)
        ssm(nc, ps, x, c, ssm_w)
        moe(nc, "moe1", ps, x, c, mw, pads, xs, ys, s_mw)
        with nc.Block() as block:
            @block.sync
            def _(sp):
                sp.dma_start(out_rows, x[:, :, :]).then_inc(s_out, 16)
                sp.wait_ge(s_out, 16)


def kernel(**inputs):
    import concourse.bacc as bacc
    from concourse.bass_utils import run_bass_kernel_spmd

    nc = bacc.Bacc("TRN2", target_bir_lowering=False, num_devices=1)
    groups = {"c": constants(), "att": attention_weights(inputs), "ssm": ssm_weights(inputs), "moe": moe_weights(inputs)}
    arrays, aps = {}, {}
    for g, members in groups.items():
        aps[g] = {}
        for k, a in members.items():
            arrays[f"{g}_{k}_dram"] = a
            aps[g][k] = nc.dram_tensor(f"{g}_{k}_dram", a.shape, F32, kind="ExternalInput").ap()
    arrays["x_dram"] = np.ascontiguousarray(inputs["L0_attn_a_x"])
    x = nc.dram_tensor("x_dram", [B, S, D], F32, kind="ExternalInput").ap()
    out = nc.dram_tensor("out_dram", [B, S, D], F32, kind="ExternalOutput").ap()
    arrays["pad_rows_dram"] = pad_rows()
    pads = nc.dram_tensor("pad_rows_dram", [2 * NE * P, ROW], F32, kind="ExternalInput").ap()
    whole(nc, x, out, pads, aps["c"], aps["att"], aps["ssm"], aps["moe"])
    r = run_bass_kernel_spmd(nc, [arrays], core_ids=[0])
    return r.results[0]["out_dram"]
```

```python
from contextlib import ExitStack

import concourse.bass as bass
import numpy as np
from concourse import mybir

ALU = mybir.AluOpType
ACT = mybir.ActivationFunctionType
AX = mybir.AxisListType
F32 = mybir.dt.float32
BF16 = mybir.dt.bfloat16
I32 = mybir.dt.int32
U32 = mybir.dt.uint32

P = 128
B, S, D = 4, 512, 128
NT = B * S // P
TPB = S // P
EPS = 1e-5
ROUND = 12582912.0

NE, DFF = 8, 512
FT = DFF // P
NSLOT = (2 * NT * P + NE * (P - 1)) // P
GT = TPB
NG = NT // GT
REGION = B * S + P
ROW = D + 1


class Chain:

    def __init__(self, engine, semaphore, base=0):
        self.engine, self.semaphore, self.count, self.base = engine, semaphore, 0, base

    def did(self, instruction):
        instruction.then_inc(self.semaphore, 1)
        self.count += 1
        return instruction

    def settle(self):
        self.engine.wait_ge(self.semaphore, self.base + self.count)

    def link(self, instruction):
        self.did(instruction)
        self.settle()


def phase_semaphores(nc, ctx, tag):
    made = []

    def clear():
        nc.clear_and_free_semaphores(made)
        nc.all_engine_barrier()

    def sem(name):
        made.append(nc.alloc_semaphore(f"{tag}_{name}"))
        return made[-1]

    ctx.callback(clear)
    return sem


def bc(ap, n, at):
    shape = list(ap.shape)
    return ap.unsqueeze(at).to_broadcast(shape[:at] + [n] + shape[at:])


def active(tile):
    return not isinstance(tile, int) or 0 <= tile < NSLOT


def later(tile, n):
    return not isinstance(tile, int) or tile >= n


def over_slot_tiles(engine, step, steps=NSLOT + 3):
    for i in range(8):
        step(i, i % 4)
    with engine.Fori(8, 36, 4) as i:
        for u in range(4):
            step(i + u, u)
    for i in range(36, steps):
        step(i, i % 4)


class Router:

    def __init__(self, nc, ctx, c, mw, pads, xs_dram, s_weights):
        def sb(name, shape, dt=F32):
            return ctx.enter_context(nc.sbuf_tensor(f"r_{name}", shape, dt))

        self.c, self.mw, self.pad_rows, self.xs_dram, self.s_weights = c, mw, pads, xs_dram, s_weights
        self.stats = sb("stats", [P, NT, 6])
        self.mv = sb("mv", [P, NT, 2])
        self.std = sb("std", [P, NT])
        self.rstd = sb("rstd", [P, NT])
        self.rows = sb("rows", [P, 2, NT, ROW])
        self.xnT = sb("xnT", [P, GT * P])
        self.lg = sb("lg", [P, NT, NE])
        self.rest = sb("rest", [P, NT, NE])
        self.work = sb("work", [P, NT, NE])
        self.first = sb("first", [P, NT])
        self.oh = sb("oh", [P, 2, NT, NE])
        self.top = sb("top", [P, 2, NT])
        self.chosen = sb("chosen", [P, NT, NE], BF16)
        self.before = sb("before", [P, NT + 1, NE], BF16)
        self.pos = sb("pos", [P, NT, NE])
        self.mine = sb("mine", [P, NT, 2, NE])
        self.slot = sb("slot", [P, NT, 2])
        self.sloti = sb("sloti", [P, NT, 2], U32)
        self.tiles = sb("tiles", [1, NE])
        self.tiles_upto = sb("tiles_upto", [1, NE])
        self.pad_start = sb("pad_start", [1, NE], I32)
        self.passed = sb("passed", [1, NSLOT, NE])
        self.passed_tiles = sb("passed_tiles", [1, NSLOT, NE])
        self.eid = sb("eid", [1, NSLOT])
        self.first_tile = sb("first_tile", [1, NSLOT])
        self.eoff = sb("eoff", [1, NSLOT], I32)
        self.roff = sb("roff", [1, NSLOT], I32)
        self.gap = sb("gap", [P, NT])
        self.egap = sb("egap", [P, NT])
        self.gate = sb("gate", [P, 2, NT])

    def begin(self, sem, x, bank_t, bank_r):
        self.x, self.bank_t = x, bank_t
        self.logit_sums, self.rank_sums = bank_r[:, 0:GT * NE], bank_r[:, GT * NE:2 * GT * NE]
        self.total_sums = bank_r[:, 2 * GT * NE:2 * GT * NE + NE]
        self.s_chain = sem("router_chain")
        self.s_mv = sem("router_moments")
        self.s_std = sem("router_std")
        self.s_number = sem("row_numbers")
        self.s_xn = sem("router_rows")
        self.s_copy = sem("second_rows")
        self.s_t = sem("router_T_psum")
        self.s_tc = sem("router_T_copied")
        self.s_lg = sem("logits")
        self.s_ch = sem("chosen")
        self.s_rank = sem("ranks")
        self.s_total = sem("totals")
        self.s_gap = sem("gap")
        self.s_egap = sem("exp_gap")
        self.s_slot = sem("slots")
        self.s_off = sem("expert_offsets")
        self.s_pad = sem("pad_rows_written")
        self.s_scat = sem("scattered")
        self.chain = None

    def start(self, dve):
        self.chain = Chain(dve, self.s_chain)
        self.chain.link(dve.memset(self.before[:, 0, :], 0.0))

    def moments(self, dve, g):
        ch = self.chain
        for t in range(g * GT, (g + 1) * GT):
            ch.did(dve.bn_stats(self.stats[:, t, :], self.x[:, t, :]))
        ch.settle()
        for t in range(g * GT, (g + 1) * GT):
            dve.bn_aggr(self.mv[:, t, :], self.stats[:, t, :]).then_inc(self.s_mv, 1)

    def normalize(self, dve, g):
        ts = slice(g * GT, (g + 1) * GT)
        dve.wait_ge(self.s_std, g + 1)
        self.chain.link(dve.reciprocal(self.rstd[:, ts], self.std[:, ts]))
        for t in range(g * GT, (g + 1) * GT):
            dve.tensor_scalar(self.rows[:, 0, t, 0:D], self.x[:, t, :], self.mv[:, t, 0:1], self.rstd[:, t:t + 1],
                              ALU.subtract, ALU.mult).then_inc(self.s_xn, 1)

    def first_max(self, dve, g, src, k):
        ch, ts = self.chain, slice(g * GT, (g + 1) * GT)
        work, top, first = self.work[:, ts, :], self.top[:, k, ts], self.first[:, ts]
        ch.link(dve.tensor_reduce(top, src[:, ts, :], AX.X, ALU.max))
        ch.link(dve.tensor_tensor(work, src[:, ts, :], bc(top, NE, 2), ALU.is_equal))
        ch.link(dve.tensor_tensor(work, work, bc(self.c["falling"][:, :], GT, 1), ALU.mult))
        ch.link(dve.tensor_reduce(first, work, AX.X, ALU.max))
        ch.link(dve.tensor_tensor(self.oh[:, k, ts, :], work, bc(first, NE, 2), ALU.is_equal))

    def choose(self, dve, g):
        ch, ts = self.chain, slice(g * GT, (g + 1) * GT)
        if g:
            dve.wait_ge(self.s_ch, g)
        dve.wait_ge(self.s_lg, g + 1)
        ch.link(dve.tensor_copy(self.lg[:, ts, :], self.logit_sums.rearrange("p (t e) -> p t e", e=NE)))
        self.first_max(dve, g, self.lg, 0)
        ch.link(dve.scalar_tensor_tensor(self.rest[:, ts, :], self.oh[:, 0, ts, :], -3e38, self.lg[:, ts, :],
                                         ALU.mult, ALU.add))
        self.first_max(dve, g, self.rest, 1)
        ch.link(dve.tensor_tensor(self.chosen[:, ts, :], self.oh[:, 0, ts, :], self.oh[:, 1, ts, :], ALU.add))
        for t in range(g * GT, (g + 1) * GT):
            m = dve.tensor_tensor(self.before[:, t + 1, :], self.before[:, t, :], self.chosen[:, t, :], ALU.add)
            if t + 1 < (g + 1) * GT:
                ch.link(m)
        m.then_inc(self.s_ch, 1)

    def slots(self, dve, g):
        ch, ts = self.chain, slice(g * GT, (g + 1) * GT)
        dve.wait_ge(self.s_rank, g + 1)
        ch.link(dve.tensor_tensor(self.pos[:, ts, :], self.rank_sums.rearrange("p (t e) -> p t e", e=NE),
                                  bc(self.c["region"][:, :], GT, 1), ALU.add))
        for k in range(2):
            ch.did(dve.tensor_tensor(self.mine[:, ts, k, :], self.oh[:, k, ts, :], self.pos[:, ts, :], ALU.mult))
        ch.settle()
        ch.link(dve.tensor_reduce(self.slot[:, ts, :], self.mine[:, ts, :, :], AX.X, ALU.add))
        dve.tensor_copy(self.sloti[:, ts, :], self.slot[:, ts, :]).then_inc(self.s_slot, 1)

    def plan(self, dve):
        ch, c, tiles, first_tile, eid = self.chain, self.c, self.tiles, self.first_tile, self.eid
        dve.wait_ge(self.s_total, 1)
        total = self.total_sums[0:1, :]
        dve.tensor_tensor(self.pad_start[:, :], total, c["region"][0:1, :], ALU.add).then_inc(self.s_off, 1)
        ch.link(dve.tensor_scalar(tiles[:, :], total, 1.0 / P, 0.49609375, ALU.mult, ALU.add))
        ch.link(dve.tensor_scalar(tiles[:, :], tiles[:, :], ROUND, ROUND, ALU.add, ALU.subtract))
        ch.link(dve.tensor_tensor_scan(self.tiles_upto[:, :], c["one"][0:1, 0:NE], tiles[:, :], 0.0,
                                       ALU.mult, ALU.add))
        ch.link(dve.tensor_tensor(self.passed[:, :, :], bc(self.tiles_upto[:, :], NSLOT, 1),
                                  bc(c["slot_tile"][0:1, :], NE, 2), ALU.is_le))
        ch.did(dve.tensor_reduce(eid[:, :], self.passed[:, :, :], AX.X, ALU.add))
        ch.link(dve.tensor_tensor(self.passed_tiles[:, :, :], self.passed[:, :, :], bc(tiles[:, :], NSLOT, 1),
                                  ALU.mult))
        dve.tensor_scalar(self.eoff[:, :], eid[:, :], float(NE - 1), float(DFF), ALU.min,
                          ALU.mult).then_inc(self.s_off, 1)
        ch.link(dve.tensor_reduce(first_tile[:, :], self.passed_tiles[:, :, :], AX.X, ALU.add))
        ch.link(dve.tensor_tensor(first_tile[:, :], c["slot_tile"][0:1, :], first_tile[:, :], ALU.subtract))
        dve.wait_ge(self.s_off, 2)
        ch.link(dve.tensor_scalar(eid[:, :], eid[:, :], float(REGION), None, ALU.mult))
        dve.scalar_tensor_tensor(self.roff[:, :], first_tile[:, :], float(P), eid[:, :],
                                 ALU.mult, ALU.add).then_inc(self.s_off, 1)
        gap, gate = self.gap, self.gate
        dve.tensor_tensor(gap[:, :], self.top[:, 1, :], self.top[:, 0, :], ALU.subtract).then_inc(self.s_gap, 1)
        dve.wait_ge(self.s_egap, 1)
        ch.link(dve.tensor_scalar(gap[:, :], self.egap[:, :], 1.0, None, ALU.add))
        ch.link(dve.reciprocal(gate[:, 0, :], gap[:, :]))
        ch.link(dve.tensor_tensor(gate[:, 1, :], gate[:, 0, :], self.egap[:, :], ALU.mult))

    def deviation(self, act, g):
        act.wait_ge(self.s_mv, (g + 1) * GT)
        act.activation(self.std[:, g * GT:(g + 1) * GT], self.mv[:, g * GT:(g + 1) * GT, 1], ACT.Sqrt,
                       bias=self.c["eps"][:, 0:1]).then_inc(self.s_std, 1)

    def copies(self, act, g):
        act.wait_ge(self.s_t, g + 1)
        if g:
            act.wait_ge(self.s_lg, g)
        act.activation(self.xnT[:, :], self.bank_t, ACT.Copy).then_inc(self.s_tc, 1)
        act.activation(self.rows[:, 1, g * GT:(g + 1) * GT, 0:D], self.rows[:, 0, g * GT:(g + 1) * GT, 0:D],
                       ACT.Copy).then_inc(self.s_copy, 1)

    def gap_exponentials(self, act):
        act.wait_ge(self.s_gap, 1)
        act.activation(self.egap[:, :], self.gap[:, :], ACT.Exp).then_inc(self.s_egap, 1)

    def transposes(self, pe, g):
        pe.wait_ge(self.s_xn, GT * g + GT)
        if g:
            pe.wait_ge(self.s_tc, g)
        for t in range(GT):
            mm = pe.transpose(self.bank_t[:, t * P:(t + 1) * P], self.rows[:, 0, GT * g + t, 0:D],
                              self.c["ident"][:, :])
        mm.then_inc(self.s_t, 1)

    def logits(self, pe, g):
        pe.wait_ge(self.s_weights, 48)
        pe.wait_ge(self.s_tc, g + 1)
        if g:
            pe.wait_ge(self.s_slot, g)
        for t in range(GT):
            mm = pe.matmul(self.logit_sums[:, t * NE:(t + 1) * NE], self.xnT[:, t * P:(t + 1) * P],
                           self.mw["wr"][:, :], start=True, stop=True)
        mm.then_inc(self.s_lg, 1)

    def ranks(self, pe, g):
        flat = lambda a: a.rearrange("p a b -> p (a b)")
        pe.wait_ge(self.s_ch, g + 1)
        pe.matmul(self.rank_sums, self.c["before_bf"][:, :], flat(self.chosen[:, g * GT:(g + 1) * GT, :]),
                  start=True, stop=False)
        pe.matmul(self.rank_sums, self.c["ones_bf"][:, :], flat(self.before[:, g * GT:(g + 1) * GT, :]),
                  start=False, stop=True).then_inc(self.s_rank, 1)

    def totals(self, pe):
        pe.wait_ge(self.s_slot, NG)
        pe.matmul(self.total_sums, self.c["ones_bf"][:, :], self.before[:, NT, :], start=True,
                  stop=True).then_inc(self.s_total, 1)

    def pads(self, sp):
        sp.dma_start(self.xs_dram[NE * REGION:NE * REGION + NE * P, :],
                     self.pad_rows[NE * P:2 * NE * P, :]).then_inc(self.s_pad, 16)
        sp.wait_ge(self.s_off, 1)
        for e in range(NE):
            r = sp.value_load(self.pad_start[0:1, e:e + 1], min_val=e * REGION, max_val=(e + 1) * REGION - P)
            sp.dma_start(self.xs_dram[bass.ds(r, P), :], self.pad_rows[e * P:(e + 1) * P, :]).then_inc(self.s_pad, 16)
        sp.wait_ge(self.s_pad, 16 * (NE + 1))
        sp.wait_ge(self.s_scat, 16 * 2 * NT)

    def numbers(self, pool):
        pool.tensor_copy(self.rows[:, :, :, D:ROW].rearrange("p k t o -> p (k t o)"),
                         self.c["row_number"][:, :]).then_inc(self.s_number, 1)
        pool.wait_ge(self.s_number, 1)

    def scatter(self, pool, g, k):
        pool.wait_ge(self.s_slot, g + 1)
        if k:
            pool.wait_ge(self.s_copy, g + 1)
        else:
            pool.wait_ge(self.s_xn, (g + 1) * GT)
        for t in range(g * GT, (g + 1) * GT):
            pool.indirect_dma_start(self.xs_dram[:, :], bass.IndirectOffsetOnAxis(self.sloti[:, t, k:k + 1], 0),
                                    self.rows[:, k, t, :], None).then_inc(self.s_scat, 16)


def moe(nc, tag, ps, x, c, mw, router, xs_dram, ys_dram, prefetch=None, out=None):
    w1t, w2t, eoff, roff, gate = mw["w1"], mw["w2"], router.eoff, router.roff, router.gate
    with ExitStack() as ctx:
        def sb(name, shape, dt=F32):
            return ctx.enter_context(nc.sbuf_tensor(f"{tag}_{name}", shape, dt))

        sem = phase_semaphores(nc, ctx, tag)

        xg = sb("xg", [P, 4, ROW])
        xgT = sb("xgT", [P, 2, P])
        w1 = sb("w1", [P, 2, DFF])
        hT = sb("hT", [P, 2, DFF])
        y = sb("y", [P, 4, D])
        target = sb("target", [P, 4])
        targeti = sb("targeti", [P, 4], U32)
        warm = sb("warm", [P, 1])
        ytok = sb("ytok", [P, 2, NT, D])

        s_xg = [sem(f"xtloaded{i}") for i in range(4)]
        s_tgt = sem("targets_copied")
        s_x = sem("xgT_psum")
        s_xc = sem("xgT_copied")
        s_m1 = sem("hidden_psum")
        s_h = sem("hidden")
        s_w1 = sem("w1_of_tile")
        s_m2 = sem("y_psum")
        s_y = sem("y_copied")
        s_st = [sem(f"y_scattered{i}") for i in range(4)]
        s_go = sem("scatter_may_start")
        s_res = [[sem(f"results_loaded{k}_{g}") for g in range(NG)] for k in range(2)]
        s_gated, s_sum = sem("first_results_scaled"), sem("first_results_added")
        s_out = sem("combined")
        s_stored = sem("x_stored")

        psX = lambda i: ps[:, i % 2, 0:P]
        psH = lambda i: ps[:, 2 + i % 2, :]
        psY = lambda i: ps[:, 6 + i % 2, 0:D]

        block = ctx.enter_context(nc.Block())

        @block.vector
        def _(dve):
            def step(i, u):
                j = i
                if active(j):
                    w = dve.value_load(eoff[0:1, bass.ds(j, 1)], min_val=0, max_val=(NE - 1) * DFF)
                    if later(j, 2):
                        dve.wait_ge(s_m1, j - 1)
                    dve.tensor_copy(w1[:, u % 2, :], w1t[:, bass.ds(w, DFF)]).then_inc(s_w1, 1)
                j = i - 1
                if active(j):
                    q = (u - 1) % 4
                    if later(j, 4):
                        dve.wait_ge(s_y, (j - 3) * 2)
                    dve.wait_ge(s_x, j + 1)
                    dve.tensor_copy(target[:, q:q + 1], xg[:, q, D:ROW]).then_inc(s_tgt, 1)
                j = i - 3
                if active(j):
                    q = (u - 3) % 4
                    if later(j, 4):
                        dve.wait_ge(s_st[q], (j - q) * 4)
                    dve.wait_ge(s_tgt, j + 1)
                    dve.tensor_copy(targeti[:, q:q + 1], target[:, q:q + 1]).then_inc(s_y, 1)
                    dve.wait_ge(s_m2, j + 1)
                    dve.tensor_copy(y[:, q, :], psY(u + 1)).then_inc(s_y, 1)

            over_slot_tiles(dve, step)
            for g in range(NG):
                dve.wait_ge(s_res[1][g], 16)
                dve.wait_ge(s_sum, g + 1)
                for t in range(g * GT, (g + 1) * GT):
                    dve.scalar_tensor_tensor(x[:, t, :], ytok[:, 1, t, :], gate[:, 1, t:t + 1], x[:, t, :],
                                             ALU.mult, ALU.add).then_inc(s_out, 1)

        @block.scalar
        def _(act):
            act.activation(warm[:, :], gate[:, 0, 0:1], ACT.Silu)

            def step(i, u):
                j = i
                if active(j):
                    act.wait_ge(s_x, j + 1)
                    if later(j, 2):
                        act.wait_ge(s_m1, j - 1)
                    act.activation(xgT[:, u % 2, :], psX(u), ACT.Copy).then_inc(s_xc, 1)
                j = i - 1
                if active(j):
                    act.wait_ge(s_m1, j + 1)
                    if later(j, 2):
                        act.wait_ge(s_m2, j - 1)
                    act.activation(hT[:, (u + 1) % 2, :], psH(u + 1), ACT.Silu).then_inc(s_h, 1)

            over_slot_tiles(act, step)
            for t in range(NT):
                act.wait_ge(s_res[0][t // GT], 16)
                act.activation(ytok[:, 0, t, :], ytok[:, 0, t, :], ACT.Copy, scale=gate[:, 0, t:t + 1]).then_inc(s_gated, 1)

        @block.tensor
        def _(pe):
            def step(i, u):
                j = i
                if active(j):
                    pe.wait_ge(s_xg[u], (j - u) * 4 + 16)
                    if later(j, 2):
                        pe.wait_ge(s_xc, j - 1)
                    pe.transpose(psX(u), xg[:, u, 0:D], c["ident"][:, :]).then_inc(s_x, 1)
                j = i - 1
                if active(j):
                    pe.wait_ge(s_xc, j + 1)
                    pe.wait_ge(s_w1, j + 1)
                    if later(j, 2):
                        pe.wait_ge(s_h, j - 1)
                    for f in range(FT):
                        mm = pe.matmul(psH(u + 1)[:, f * P:(f + 1) * P], w1[:, (u + 1) % 2, f * P:(f + 1) * P],
                                       xgT[:, (u + 1) % 2, :], start=True, stop=True)
                    mm.then_inc(s_m1, 1)
                j = i - 2
                if active(j):
                    w = pe.value_load(eoff[0:1, bass.ds(j, 1)], min_val=0, max_val=(NE - 1) * DFF)
                    pe.wait_ge(s_h, j + 1)
                    if later(j, 2):
                        pe.wait_ge(s_y, (j - 1) * 2)
                    for f in range(FT):
                        mm = pe.matmul(psY(u), hT[:, u % 2, f * P:(f + 1) * P],
                                       w2t[:, bass.ds(w + f * P, P)], start=(f == 0), stop=(f == FT - 1))
                    mm.then_inc(s_m2, 1)

            over_slot_tiles(pe, step)

        @block.sync
        def _(sp):
            def step(i, u):
                if not active(i):
                    return
                r = sp.value_load(roff[0:1, bass.ds(i, 1)], min_val=0, max_val=NE * REGION + (NE - 1) * P)
                if later(i, 4):
                    sp.wait_ge(s_tgt, i - 3)
                sp.dma_start(xg[:, u, :], xs_dram[bass.ds(r, P), :]).then_inc(s_xg[u], 16)
                if prefetch is not None:
                    prefetch(sp, i)

            over_slot_tiles(sp, step)
            for q in range(4):
                sp.wait_ge(s_st[q], 16 * ((NSLOT - q + 3) // 4))
            for g in range(NG):
                for k in range(2):
                    r0 = k * NT * P + g * GT * P
                    sp.dma_start(ytok[:, k, g * GT:(g + 1) * GT, :],
                                 ys_dram[r0:r0 + GT * P, :].rearrange("(t p) d -> p t d", p=P)).then_inc(s_res[k][g], 16)
            if out is not None:
                for g in range(NG):
                    sp.wait_ge(s_out, (g + 1) * GT)
                    sp.dma_start(out[:, g * GT:(g + 1) * GT, :], x[:, g * GT:(g + 1) * GT, :]).then_inc(s_stored, 16)
                sp.wait_ge(s_stored, 16 * NG)

        @block.gpsimd
        def _(pool):
            def step(i, u):
                j = i - 4
                if active(j):
                    pool.wait_ge(s_y, (j + 1) * 2)
                    pool.sem_inc(s_go, 1)
                    pool.indirect_dma_start(ys_dram[:, :], bass.IndirectOffsetOnAxis(targeti[:, u:u + 1], 0),
                                            y[:, u, :], None).then_inc(s_st[u], 16)

            over_slot_tiles(pool, step, NSLOT + 4)
            for g in range(NG):
                pool.wait_ge(s_gated, (g + 1) * GT)
                xt, yg = x[:, g * GT:(g + 1) * GT, :], ytok[:, 0, g * GT:(g + 1) * GT, :]
                pool.tensor_tensor(xt, xt, yg, ALU.add).then_inc(s_sum, 1)


NH, DH = 16, 8
HG = 4
UNITS = B * NH // HG
GROUPS = NH // HG
KROWS = 128
MROW = 9 * DH
MASKED = -1e30
WIDTH = [S - P * k for k in range(TPB)]


def attention_prepare(nc, ps, x, c, w, parts_dram, hatq, hatk, vall, s_hat, x_loaded, weights_loaded):
    with ExitStack() as ctx:
        def sb(name, shape, dt=F32):
            return ctx.enter_context(nc.sbuf_tensor(f"ap_{name}", shape, dt))

        sem = phase_semaphores(nc, ctx, "ap")

        stats = sb("stats", [P, NT, 6])
        mv = sb("mv", [P, NT, 2])
        std = sb("std", [P, NT])
        rstd = sb("rstd", [P, NT])
        xn = sb("xn", [P, 2, TPB, D])
        xnT = sb("xnT", [P, 2, S])
        rot = sb("rot", [P, 2, 2, S])
        full = sb("full", [P, 2, 2, S])
        rest = sb("rest", [P, 2, S])
        part = sb("part", [P, 2, 2, 3, S], BF16)
        s_chain = sem("dve_chain")
        s_mv, s_std, s_xn, s_t, s_tc = sem("moments"), sem("std"), sem("xn"), sem("xnT_psum"), sem("xnT_copied")
        s_pr, s_rot, s_v = sem("projected"), sem("rotated"), sem("values")
        s_full, s_p0, s_r1, s_p1, s_p2 = (sem(f"split{k}") for k in range(5))
        s_store = [sem("parts_stored0"), sem("parts_stored1")]
        block = ctx.enter_context(nc.Block())

        @block.vector
        def _(dve):
            ch = Chain(dve, s_chain)
            dve.wait_ge(x_loaded, 16)

            def moments(b):
                for t in range(b * TPB, (b + 1) * TPB):
                    ch.did(dve.bn_stats(stats[:, t, :], x[:, t, :]))
                ch.settle()
                for t in range(b * TPB, (b + 1) * TPB):
                    dve.bn_aggr(mv[:, t, :], stats[:, t, :]).then_inc(s_mv, 1)

            def normalize(b):
                ts = slice(b * TPB, (b + 1) * TPB)
                dve.wait_ge(s_std, b + 1)
                ch.link(dve.reciprocal(rstd[:, ts], std[:, ts]))
                if b >= 2:
                    dve.wait_ge(s_t, b - 1)
                for t in range(TPB):
                    n = b * TPB + t
                    dve.tensor_scalar(xn[:, b % 2, t, :], x[:, n, :], mv[:, n, 0:1], rstd[:, n:n + 1],
                                      ALU.subtract, ALU.mult).then_inc(s_xn, 1)

            moments(0)
            moments(1)
            normalize(0)
            moments(2)
            moments(3)
            normalize(1)
            dve.wait_ge(weights_loaded, 16 * len(w))

            def rotate(b):
                for m in range(4):
                    dve.wait_ge(s_pr, 5 * b + m + 1)
                    if m % 2 == 0 and b:
                        dve.wait_ge(s_full, 2 * (b - 1) + m // 2 + 1)
                    dve.scalar_tensor_tensor(rot[:, m // 2, m % 2, :], ps[:, 2 + m, :], w["qk_bias"][:, m:m + 1],
                                             w["rotary"][:, m, :], ALU.add, ALU.mult).then_inc(s_rot, 1)
                dve.wait_ge(s_pr, 5 * b + 5)
                dve.tensor_tensor(vall[:, b * TPB:(b + 1) * TPB, :],
                                  ps[:, 6 + b % 2, :].rearrange("p (t d) -> p t d", d=D),
                                  bc(w["bv"][:, :], TPB, 1), ALU.add).then_inc(s_v, 1)

            def rests(b):
                for k in range(2):
                    dve.wait_ge(s_full, 2 * b + k + 1)
                    dve.wait_ge(s_p0, 2 * b + k + 1)
                    if b:
                        dve.wait_ge(s_p2, 2 * (b - 1) + k + 1)
                    dve.tensor_tensor(rest[:, k, :], full[:, b % 2, k, :], part[:, b % 2, k, 0, :],
                                      ALU.subtract).then_inc(s_r1, 1)

            for b in range(B):
                if b and b + 1 < B:
                    normalize(b + 1)
                rotate(b)
                if b:
                    rests(b - 1)
            rests(B - 1)

        @block.scalar
        def _(act):
            for b in range(B):
                act.wait_ge(s_mv, (b + 1) * TPB)
                act.activation(std[:, b * TPB:(b + 1) * TPB], mv[:, b * TPB:(b + 1) * TPB, 1], ACT.Sqrt,
                               bias=c["eps"][:, 0:1]).then_inc(s_std, 1)

            def copy_xnT(b):
                act.wait_ge(s_t, b + 1)
                if b >= 2:
                    act.wait_ge(s_pr, 5 * (b - 1))
                act.activation(xnT[:, b % 2, :], ps[:, b % 2, :], ACT.Copy).then_inc(s_tc, 1)

            def first_parts(b):
                if b >= 2:
                    act.wait_ge(s_store[b % 2], 32 * (b // 2))
                for k in range(2):
                    act.wait_ge(s_full, 2 * b + k + 1)
                    act.activation(part[:, b % 2, k, 0, :], full[:, b % 2, k, :], ACT.Copy).then_inc(s_p0, 1)

            def second_parts(b):
                for k in range(2):
                    act.wait_ge(s_r1, 2 * b + k + 1)
                    act.activation(part[:, b % 2, k, 1, :], rest[:, k, :], ACT.Copy).then_inc(s_p1, 1)

            def store(b):
                for k in range(2):
                    act.wait_ge(s_p2, 2 * b + k + 1)
                    act.dma_start(parts_dram[b, k].rearrange("i p t -> p i t"),
                                  part[:, b % 2, k, :, :]).then_inc(s_store[b % 2], 16)

            copy_xnT(0)
            for b in range(B):
                if b + 1 < B:
                    copy_xnT(b + 1)
                if b:
                    second_parts(b - 1)
                first_parts(b)
                if b and b + 1 < B:
                    store(b - 1)
            second_parts(B - 1)
            store(B - 2)
            store(B - 1)

        @block.gpsimd
        def _(pool):
            def sums(b):
                for k in range(2):
                    pool.wait_ge(s_rot, 4 * b + 2 * k + 2)
                    if b >= 2:
                        pool.wait_ge(s_p0, 2 * (b - 2) + k + 1)
                        pool.wait_ge(s_r1, 2 * (b - 2) + k + 1)
                    pool.tensor_tensor(full[:, b % 2, k, :], rot[:, k, 0, :], rot[:, k, 1, :], ALU.add).then_inc(s_full, 1)

            def third_parts(b):
                if b >= 2:
                    pool.wait_ge(s_store[b % 2], 32 * (b // 2))
                for k in range(2):
                    pool.wait_ge(s_p1, 2 * b + k + 1)
                    pool.wait_ge(s_r1, 2 * b + k + 1)
                    pool.tensor_tensor(part[:, b % 2, k, 2, :], rest[:, k, :], part[:, b % 2, k, 1, :],
                                       ALU.subtract).then_inc(s_p2, 1)

            pool.wait_ge(weights_loaded, 16 * len(w))
            for b in range(B):
                sums(b)
                if b:
                    third_parts(b - 1)
            third_parts(B - 1)

        @block.tensor
        def _(pe):
            def transposed(b):
                pe.wait_ge(s_xn, TPB * (b + 1))
                if b >= 2:
                    pe.wait_ge(s_tc, b - 1)
                for t in range(TPB):
                    mm = pe.transpose(ps[:, b % 2, t * P:(t + 1) * P], xn[:, b % 2, t, :], c["ident"][:, :])
                mm.then_inc(s_t, 1)

            transposed(0)
            pe.wait_ge(weights_loaded, 16 * len(w))
            for b in range(B):
                if b + 1 < B:
                    transposed(b + 1)
                pe.wait_ge(s_tc, b + 1)
                for m in range(4):
                    if b:
                        pe.wait_ge(s_rot, 4 * (b - 1) + m + 1)
                    pe.matmul(ps[:, 2 + m, :], w["wqk"][:, m * P:(m + 1) * P], xnT[:, b % 2, :],
                              start=True, stop=True).then_inc(s_pr, 1)
                if b >= 2:
                    pe.wait_ge(s_v, b - 1)
                for t in range(TPB):
                    mm = pe.matmul(ps[:, 6 + b % 2, t * P:(t + 1) * P], xnT[:, b % 2, t * P:(t + 1) * P],
                                   w["wv"][:, :], start=True, stop=True)
                mm.then_inc(s_pr, 1)

        @block.sync
        def _(sp):
            for par in range(2):
                for hat, name in ((hatq, "zero_rows"), (hatk, "one_rows")):
                    sp.dma_start(hat[MROW:KROWS, par, :, :], bc(c[name][:, :], NH, 1)).then_inc(s_hat["fill"], 16)
            sp.wait_ge(s_store[0], 32)
            load_hats(sp, 0, parts_dram, hatq, hatk, s_hat)
            for stored in s_store:
                sp.wait_ge(stored, 32 * (B // 2))


def load_hats(sp, b, parts_dram, hatq, hatk, s_hat):
    for i in range(3):
        for j in range(3):
            rows = slice((3 * i + j) * DH, (3 * i + j + 1) * DH)
            for hat, k, p in ((hatq, 0, i), (hatk, 1, j)):
                sp.dma_start(hat[rows, b % 2, :, :],
                             parts_dram[b, k, p].rearrange("(h d) t -> d h t", d=DH)).then_inc(s_hat[b % 2], 16)


def attention(nc, ps, x, c, w, parts_dram, hatq, hatk, vall, s_hat, router, load_moe_weights):
    with ExitStack() as ctx:
        def sb(name, shape, dt=F32):
            return ctx.enter_context(nc.sbuf_tensor(f"at_{name}", shape, dt))

        sem = phase_semaphores(nc, ctx, "at")

        pt = sb("pt", [P, 2, 5, 2 * S])
        vext = sb("vext", [P, TPB, NH, 32])
        mx = sb("mx", [P, 2, TPB, HG])
        mh = sb("mh", [P, TPB, 2, HG], BF16)
        mT = sb("mT", [2 * HG, S], BF16)
        oT = w["rotary"]
        rden = sb("rden", [P, NH])
        on = sb("on", [P, TPB, D])
        onT = w["wqk"]
        s_a, s_ar, s_b, s_e = sem("a_psum"), sem("a_max"), sem("b_psum"), sem("b_exp")
        s_pv, s_oc, s_vx, s_fill = sem("pv"), sem("o_copied"), sem("values_placed"), sem("fill")
        s_mh, s_mt, s_mc, s_md = sem("max_negated"), sem("maxT_psum"), sem("maxT_copied"), sem("max_rows")
        s_tt, s_tc, s_rd = sem("tail_psum"), sem("tail_read"), sem("denominator")
        s_causal, s_bo = sem("causal"), sem("bo_added")
        s_zr = [sem("rows_zeroed0"), sem("rows_zeroed1")]
        bankA = lambda k: ps[:, k % 2, :]
        chunkB = lambda k: ps[:, 2 + 2 * (k % 2):4 + 2 * (k % 2), :]
        bankO, bankM = ps[:, 6, :], ps[:, 7, :]
        tail_bank = lambda b, r: ps[:, 2 + r % 4, :] if b == B - 1 else bankM
        router.begin(sem, x, bankA(0), bankA(1))
        block = ctx.enter_context(nc.Block())

        A_CHUNKS = [[(h, 3, 0)] for h in range(4)] + [[(h, 2, 0), (h, 0, 384)] for h in range(4)] \
            + [[(h, 1, 0), (h + 1, 1, 256)] for h in (0, 2)]
        B_CHUNKS = [[(h, 0, 0, 0), (h, 1, 1, 0), (h, 3, 1, 384)] for h in range(4)] \
            + [[(h, 2, h // 2, 256 * (h % 2)) for h in range(4)]]
        PLACE = {(h, k): (n, S * bank + col) for n, ch in enumerate(B_CHUNKS) for h, k, bank, col in ch}

        def tail_rounds_before(u):
            b, g = (u - 1) // GROUPS, (u - 1) % GROUPS
            return max(0, 6 * (b - 1) + (0, 0, 4, 6)[g])

        TAIL = {(1, 1): 0, (1, 2): 1, (1, 3): 2, (1, 4): 3, (2, 1): 4, (2, 2): 5}

        v, z = UNITS - 2, UNITS - 1
        ROUTE_DVE = {(v - 4, 4): [("moments", 0)], (v - 3, 0): [("moments", 1)],
                     (v - 3, 3): [("normalize", 0)], (v - 2, 0): [("normalize", 1)],
                     (v, 0): [("choose", 0)], (v, 3): [("moments", 2)], (v, 4): [("slots", 0)],
                     (z, 0): [("normalize", 2), ("choose", 1)], (z, 3): [("slots", 1)], (z, 4): [("choose", 2), ("slots", 2)]}
        ROUTE_PE = {(v - 1, 4): [("transposes", 0)], (v, 0): [("logits", 0)], (v, 1): [("transposes", 1)],
                    (v, 4): [("ranks", 0)], (z, 0): [("logits", 1)], (z, 1): [("transposes", 2)],
                    (z, 3): [("ranks", 1)], (z, 4): [("logits", 2)]}
        ROUTE_ACT = {(v - 3, 1): [("deviation", 0), ("deviation", 1)], (v - 1, 4): [("copies", 0)],
                     (v, 2): [("copies", 1)], (v, 4): [("deviation", 2)], (z, 2): [("copies", 2)]}

        @block.tensor
        def _(pe):
            def a_chunk(u, k):
                b, g, n = u // GROUPS, u % GROUPS, 10 * u + k
                if u % GROUPS == 0 and k == 0:
                    pe.wait_ge(s_hat[b % 2], 288 * (b // 2 + 1))
                    if b >= 2:
                        pe.wait_ge(s_zr[b % 2], 16 * (b // 2))
                if n >= 2:
                    pe.wait_ge(s_ar, n - 1)
                for h, t, col in A_CHUNKS[k]:
                    hh = HG * g + h
                    pe.matmul(bankA(n)[:, col:col + (t + 1) * P], hatq[0:KROWS, b % 2, hh, t * P:(t + 1) * P],
                              hatk[0:KROWS, b % 2, hh, 0:(t + 1) * P], start=True, stop=True)
                    mm = pe.matmul(bankA(n)[:, col + t * P:col + (t + 1) * P], c["ident_bf"][:, :],
                                   c["mask_q_bf"][:, :], start=False, stop=True, skip_group_check=True)
                mm.then_inc(s_a, 1)

            def b_chunk(u, k):
                b, g, n = u // GROUPS, u % GROUPS, 5 * u + k
                if k == 0:
                    pe.wait_ge(s_md, 32 * (u + 1))
                if n >= 2:
                    pe.wait_ge(s_e, n - 1)
                for h, t, bank, col in B_CHUNKS[k]:
                    hh = HG * g + h
                    mm = pe.matmul(chunkB(n)[:, bank, col:col + WIDTH[t]], hatk[0:KROWS, b % 2, hh, t * P:(t + 1) * P],
                              hatq[0:KROWS, b % 2, hh, t * P:S], start=True, stop=True)
                mm.then_inc(s_b, 1)

            def pv(u, t):
                b, g = u // GROUPS, u % GROUPS
                pe.wait_ge(s_e, 5 * u + (4 if t < 2 else 5))
                pe.wait_ge(s_causal, 4 * u + t + 1)
                if t == 0:
                    if u:
                        pe.wait_ge(s_oc, u)
                    if g == 0:
                        pe.wait_ge(s_vx, b + 1)
                for h in range(HG):
                    chunk, col = PLACE[h, t]
                    mm = pe.matmul(bankO[32 * h:32 * h + 32, t * P:S], vext[:, t, HG * g + h, :],
                                   pt[:, u % 2, chunk, col:col + WIDTH[t]],
                                   start=(t == 0), stop=(t == TPB - 1), skip_group_check=True)
                if t == TPB - 1:
                    mm.then_inc(s_pv, 1)

            def max_rows(u):
                pe.wait_ge(s_mh, 2 * (u + 1))
                if u:
                    pe.wait_ge(s_mc, u)
                if u > GROUPS + 1 and tail_rounds_before(u):
                    pe.wait_ge(s_tc, tail_rounds_before(u))
                out = bankM.bitcast(BF16)
                for t in range(TPB):
                    mm = pe.transpose(out[0:2 * HG, t * P:(t + 1) * P],
                                      mh[:, t, :, :].rearrange("p i h -> p (i h)"), c["ident_bf"][:, :])
                mm.then_inc(s_mt, 1)

            def tail(b, r):
                last, dst = b == B - 1, tail_bank(b, r)
                if r == 0:
                    pe.wait_ge(s_oc, GROUPS * (b + 1))
                if r in (0, 4) and not last:
                    pe.wait_ge(s_mc, min(GROUPS * (b + 1) + 3 + r // 4, UNITS))
                if (b or r) and (not last or r >= 4):
                    pe.wait_ge(s_tc, 6 * b + r)
                for t in range(TPB):
                    to = dst[:, t * P:(t + 1) * P]
                    if r < 4:
                        mm = pe.transpose(to, oT[:, t, r * P:(r + 1) * P], c["ident"][:, :])
                    elif r == 4:
                        mm = pe.transpose(to, on[:, t, :], c["ident"][:, :])
                    else:
                        mm = pe.matmul(to, onT[:, t * P:(t + 1) * P], w["wo"][:, :], start=True, stop=True)
                mm.then_inc(s_tt, 1)

            def route(part, group):
                {"transposes": router.transposes, "logits": router.logits, "ranks": router.ranks}[part](pe, group)

            pe.wait_ge(s_hat["fill"], 64)
            for u in range(2):
                for k in range(10):
                    a_chunk(u, k)
                    if (u, k) == (1, 1):
                        max_rows(0)
            for u in range(UNITS):
                b, g = u // GROUPS, u % GROUPS
                for k in range(5):
                    if u + 2 < UNITS:
                        a_chunk(u + 2, 2 * k)
                    b_chunk(u, k)
                    if u + 2 < UNITS:
                        a_chunk(u + 2, 2 * k + 1)
                    if u and k:
                        pv(u - 1, k - 1)
                    if k == 0 and u + 1 < UNITS:
                        max_rows(u + 1)
                    if b and (g, k) in TAIL:
                        tail(b - 1, TAIL[g, k])
                    for part, group in ROUTE_PE.get((u, k), ()):
                        if (part, group) == ("transposes", 0):
                            pe.wait_ge(s_ar, 10 * UNITS)
                        route(part, group)
            for t in range(TPB):
                pv(UNITS - 1, t)
            route("ranks", 2)
            for r in range(6):
                tail(B - 1, r)
            for part in ("transposes", "logits", "ranks"):
                route(part, B - 1)
            router.totals(pe)

        @block.vector
        def _(dve):
            def a_max(u, k):
                n = 10 * u + k
                dve.wait_ge(s_a, n + 1)
                if k == 0 and u >= 2:
                    dve.wait_ge(s_mh, 2 * (u - 1))
                chunk = A_CHUNKS[k]
                if len(chunk) == 2 and chunk[0][1] == chunk[1][1]:
                    h, t, _ = chunk[0]
                    m = dve.tensor_reduce(mx[:, u % 2, t, h:h + 2], bankA(n).rearrange("p (h c) -> p h c", h=2),
                                          AX.X, ALU.max)
                else:
                    for h, t, col in chunk:
                        m = dve.tensor_reduce(mx[:, u % 2, t, h:h + 1], bankA(n)[:, col:col + (t + 1) * P],
                                              AX.X, ALU.max)
                m.then_inc(s_ar, 1)

            def negate(u):
                dve.wait_ge(s_ar, 10 * (u + 1))
                if u:
                    dve.wait_ge(s_mt, u)
                dve.tensor_scalar(mh[:, :, 0, :], mx[:, u % 2, :, :], -1.0, None, ALU.mult).then_inc(s_mh, 1)
                dve.wait_ge(s_mh, 2 * u + 1)
                dve.scalar_tensor_tensor(mh[:, :, 1, :], mx[:, u % 2, :, :], -1.0, mh[:, :, 0, :],
                                         ALU.mult, ALU.subtract).then_inc(s_mh, 1)

            def rows_copy(u):
                dve.wait_ge(s_mt, u + 1)
                if u:
                    dve.wait_ge(s_md, 32 * u)
                dve.tensor_copy(mT[:, :], bankM.bitcast(BF16)[0:2 * HG, 0:S]).then_inc(s_mc, 1)

            def place_values(b):
                if b:
                    dve.wait_ge(s_pv, GROUPS * b)
                else:
                    dve.wait_ge(s_fill, 2)
                src = vall[:, b * TPB:(b + 1) * TPB, :].rearrange("p t (h d) -> p (t h) d", d=DH)
                dve.tensor_copy(vext[:, :, :, 0:DH].rearrange("p t h d -> p (t h) d"), src).then_inc(s_vx, 1)

            def tail(b, r):
                bank = tail_bank(b, r)
                dve.wait_ge(s_tt, 6 * b + r + 1)
                if r < 4:
                    o = bank.rearrange("p (h c) -> p h c", c=32)
                    if b or r:
                        dve.wait_ge(s_tc, 6 * b + r)
                    dve.reciprocal(rden[:, :], o[:, :, DH]).then_inc(s_rd, 1)
                    dve.wait_ge(s_rd, 4 * b + r + 1)
                    dve.tensor_tensor(on[:, r, :].rearrange("p (h d) -> p h d", d=DH), o[:, :, 0:DH],
                                      bc(rden[:, :], DH, 2), ALU.mult).then_inc(s_tc, 1)
                elif r == 4:
                    dve.tensor_copy(onT[:, :], bank).then_inc(s_tc, 1)
                else:
                    dve.wait_ge(s_bo, b + 1)
                    xb = x[:, b * TPB:(b + 1) * TPB, :]
                    dve.tensor_tensor(xb, bank.rearrange("p (t d) -> p t d", d=D), xb, ALU.add).then_inc(s_tc, 1)

            def route(part, group):
                if part == "moments":
                    dve.wait_ge(s_tc, 6 * (group + 1))
                {"moments": router.moments, "normalize": router.normalize, "choose": router.choose,
                 "slots": router.slots}[part](dve, group)

            router.start(dve)
            for u in range(2):
                for k in range(10):
                    a_max(u, k)
                negate(u)
                if u == 0:
                    rows_copy(u)
            place_values(0)
            for u in range(UNITS):
                b, g = u // GROUPS, u % GROUPS
                for k in range(5):
                    if u + 2 < UNITS:
                        a_max(u + 2, 2 * k)
                        a_max(u + 2, 2 * k + 1)
                    if k == 0 and u + 1 < UNITS:
                        rows_copy(u + 1)
                    if g == 0 and b and k == 3:
                        place_values(b)
                    if b and (g, k) in TAIL:
                        tail(b - 1, TAIL[g, k])
                    for part, group in ROUTE_DVE.get((u, k), ()):
                        route(part, group)
                if u + 2 < UNITS:
                    negate(u + 2)
            for r in range(6):
                tail(B - 1, r)
            for part in ("moments", "normalize", "choose", "slots"):
                route(part, B - 1)
            router.plan(dve)

        @block.scalar
        def _(act):
            def o_copy(u):
                b, g = u // GROUPS, u % GROUPS
                act.wait_ge(s_pv, u + 1)
                if g == 0 and b:
                    act.wait_ge(s_tt, 6 * (b - 1) + 4)
                act.activation(oT[:, g, :], bankO, ACT.Copy).then_inc(s_oc, 1)

            for u in range(UNITS):
                for k in range(5):
                    n = 5 * u + k
                    act.wait_ge(s_b, n + 1)
                    if k == 0 and u >= 2:
                        act.wait_ge(s_pv, u - 1)
                    act.activation(pt[:, u % 2, k, :], chunkB(n).rearrange("p a b -> p (a b)"), ACT.Exp).then_inc(s_e, 1)
                    if k == 4 and u:
                        o_copy(u - 1)
                    for part, group in ROUTE_ACT.get((u, k), ()):
                        (router.deviation if part == "deviation" else router.copies)(act, group)
            o_copy(UNITS - 1)
            router.deviation(act, B - 1)
            router.copies(act, B - 1)
            router.gap_exponentials(act)

        @block.gpsimd
        def _(pool):
            pool.memset(vext[:, :, :, :], 0.0).then_inc(s_fill, 1)
            pool.wait_ge(s_fill, 1)
            pool.memset(vext[:, :, :, DH:DH + 1], 1.0).then_inc(s_fill, 1)
            for b in range(B):
                xb = x[:, b * TPB:(b + 1) * TPB, :]
                pool.tensor_tensor(xb, xb, bc(w["bo"][:, :], TPB, 1), ALU.add).then_inc(s_bo, 1)
            router.numbers(pool)
            for u in range(UNITS):
                if u == UNITS - 1:
                    router.scatter(pool, 0, 0)
                for t in range(TPB):
                    pool.wait_ge(s_e, 5 * u + (4 if t < 2 else 5))
                    chunk, col = PLACE[0, t]
                    if t == 2:
                        own = pt[:, u % 2, chunk, :].rearrange("p (h q) -> p h q", h=HG)[:, :, 0:P]
                    else:
                        own = pt[:, u % 2, 0:HG, col:col + P]
                    pool.affine_select(out=own, in_=own, compare_op=ALU.is_ge, fill=0.0, base=0,
                                       pattern=[[0, HG], [1, P]], channel_multiplier=-1).then_inc(s_causal, 1)
            router.scatter(pool, 0, 1)
            for group in range(1, B):
                router.scatter(pool, group, 0)
                router.scatter(pool, group, 1)

        @block.sync
        def _(sp):
            load_hats(sp, 1, parts_dram, hatq, hatk, s_hat)
            for u in range(UNITS):
                b, g = u // GROUPS, u % GROUPS
                if g == 2 and b + 1 in range(2, B):
                    sp.wait_ge(s_b, 5 * GROUPS * b)
                    sp.dma_start(hatq[MROW:MROW + 2, (b + 1) % 2, :, :],
                                 bc(c["zero_rows"][0:2, :], NH, 1)).then_inc(s_zr[(b + 1) % 2], 16)
                    load_hats(sp, b + 1, parts_dram, hatq, hatk, s_hat)
                if u == 1:
                    load_moe_weights(sp)
                sp.wait_ge(s_mc, u + 1)
                for i in range(2):
                    sp.dma_start(hatq[MROW + i:MROW + i + 1, b % 2, HG * g:HG * (g + 1), :],
                                 mT[HG * i:HG * (i + 1), :]).then_inc(s_md, 16)
            router.pads(sp)


NF, NB = 64, 4
NFFT = 2 * S
R4 = 4
HALF = S // 2
KT = HALF // P
COLS = 2 * B * NF
TABLE_PIECES = NSLOT - 4
TWO_PI = 2 * np.pi
TWO_PI_HI = 6.28125
PI_BELOW = 3.1415925


class Moments:

    def __init__(self, sb, sem, tag):
        self.stats = sb(f"{tag}_stats", [P, NT, 6])
        self.mv = sb(f"{tag}_mv", [P, NT, 2])
        self.std = sb(f"{tag}_std", [P, NT])
        self.rstd = sb(f"{tag}_rstd", [P, NT])
        self.s_st, self.s_mv, self.s_std = sem(f"{tag}_stats"), sem(f"{tag}_moments"), sem(f"{tag}_std")
        self.s_rstd, self.s_done = sem(f"{tag}_rstd"), sem(f"{tag}_normalized")

    def moments(self, dve, src, g):
        for t in range(g * TPB, (g + 1) * TPB):
            dve.bn_stats(self.stats[:, t, :], src[:, t, :]).then_inc(self.s_st, 1)
        dve.wait_ge(self.s_st, (g + 1) * TPB)
        for t in range(g * TPB, (g + 1) * TPB):
            dve.bn_aggr(self.mv[:, t, :], self.stats[:, t, :]).then_inc(self.s_mv, 1)

    def root(self, act, eps, g):
        ts = slice(g * TPB, (g + 1) * TPB)
        act.wait_ge(self.s_mv, (g + 1) * TPB)
        act.activation(self.std[:, ts], self.mv[:, ts, 1], ACT.Sqrt, bias=eps[:, 0:1]).then_inc(self.s_std, 1)

    def normalize(self, dve, dst, src, g):
        ts = slice(g * TPB, (g + 1) * TPB)
        dve.wait_ge(self.s_std, g + 1)
        dve.reciprocal(self.rstd[:, ts], self.std[:, ts]).then_inc(self.s_rstd, 1)
        dve.wait_ge(self.s_rstd, g + 1)
        for t in range(g * TPB, (g + 1) * TPB):
            dve.tensor_scalar(dst[:, t, :], src[:, t, :], self.mv[:, t, 0:1], self.rstd[:, t:t + 1],
                              ALU.subtract, ALU.mult).then_inc(self.s_done, 1)


def ssm_project(nc, ps, x, c, w, xi, xh, cp, gate, U, K, weights_loaded):
    with ExitStack() as ctx:
        def sb(name, shape, dt=F32):
            return ctx.enter_context(nc.sbuf_tensor(f"sp_{name}", shape, dt))

        sem = phase_semaphores(nc, ctx, "sp")

        outer, inner = Moments(sb, sem, "outer"), Moments(sb, sem, "inner")
        xnT = sb("xnT", [P, 2, S])
        sig = sb("sig", [P, 4, S])
        uT = sb("uT", [P, 2, S])
        pw = sb("pw", [P, S + 1])
        k1 = sb("k1", [P, S])
        kT = sb("kT", [P, 2, S])
        turn, turned, angle = (K[:, n:n + 1, :, :, :].rearrange("p t c b n -> p (t c b n)") for n in range(3))
        wave = sb("wave", [P, S])
        col = sb("col", [P, 12])
        erow = sb("erow", [P, NF])
        s_ch, s_a = sem("dve_chain"), sem("act_setup")
        s_dv, s_red, s_wave = sem("dve_setup"), sem("angles"), sem("wave")
        s_pool, s_decay = sem("pool_chain"), sem("decay")
        s_t, s_tc = sem("xnT_psum"), sem("xnT_copied")
        s_pr = sem("projected")
        s_sig = sem("sigmoids")
        s_u, s_cp, s_k1, s_k = sem("inputs"), sem("concept"), sem("kernel_size"), sem("kernel")
        s_ut, s_kt, s_uc, s_kc = sem("inputs_psum"), sem("kernel_psum"), sem("inputs_copied"), sem("kernel_copied")
        PROJ = [("fg", 2), ("band", 3), ("tg", 4), ("sp", 5), ("concept", 6), ("cg", 7), ("gate", 2)]
        block = ctx.enter_context(nc.Block())

        @block.vector
        def _(dve):
            ch = Chain(dve, s_ch)
            dve.wait_ge(weights_loaded, 16 * (len(w) - 1))

            def affine(b):
                dve.wait_ge(s_t, b + 1)
                if b >= 2:
                    dve.wait_ge(s_pr, 7 * (b - 1))
                dve.tensor_scalar(xnT[:, b % 2, :], ps[:, b % 2, :], w["norm_gb"][:, 0:1], w["norm_gb"][:, 1:2],
                                  ALU.mult, ALU.add).then_inc(s_tc, 1)

            def inner_moments(b):
                dve.wait_ge(outer.s_done, TPB * (b + 1))
                inner.moments(dve, xi, b)

            outer.moments(dve, x, 0)
            outer.moments(dve, x, 1)
            outer.normalize(dve, xi, x, 0)
            ch.link(dve.tensor_reduce(col[:, 0:1], w["fi_row"][:, :], AX.X, ALU.max))
            dve.tensor_scalar(col[:, 1:2], col[:, 0:1], -1.0, None, ALU.mult).then_inc(s_dv, 1)
            inner_moments(0)
            outer.normalize(dve, xi, x, 1)
            inner.normalize(dve, xh, xi, 0)
            inner_moments(1)
            outer.moments(dve, x, 2)
            inner.normalize(dve, xh, xi, 1)
            affine(0)
            outer.normalize(dve, xi, x, 2)
            outer.moments(dve, x, 3)
            inner_moments(2)
            affine(1)
            dve.wait_ge(s_a, 1)
            dve.reciprocal(col[:, 6:7], col[:, 2:3]).then_inc(s_dv, 1)
            outer.normalize(dve, xi, x, 3)
            inner.normalize(dve, xh, xi, 2)
            inner_moments(3)
            inner.normalize(dve, xh, xi, 3)
            ch.link(dve.memset(pw[:, 0:1], 1.0))

            def copies(b):
                for bank, s, done, dst in ((3, s_ut, s_uc, U), (4, s_kt, s_kc, K)):
                    dve.wait_ge(s, b + 1)
                    for cc in range(2):
                        m = dve.tensor_copy(dst[:, :, cc, b, :],
                                            ps[:, bank, :].rearrange("p (t c n) -> p t c n", c=2, n=NF)[:, :, cc, :])
                    m.then_inc(done, 1)

            for b in range(B):
                dve.wait_ge(s_pr, 7 * b + 4)
                dve.wait_ge(s_sig, 5 * b + 1)
                dve.tensor_tensor(uT[:, b % 2, :], ps[:, 5, :], sig[:, 0, :], ALU.mult).then_inc(s_u, 1)
                dve.wait_ge(s_sig, 5 * b + 2)
                if b:
                    dve.wait_ge(s_k1, b)
                else:
                    dve.wait_ge(s_decay, 1)
                ch.link(dve.tensor_tensor_scan(pw[:, 1:S + 1], sig[:, 1, :], col[:, 8:9].to_broadcast([P, S]), 1.0,
                                               ALU.mult, ALU.mult))
                dve.wait_ge(s_sig, 5 * b + 3)
                if b:
                    dve.wait_ge(s_k, b)
                dve.tensor_tensor(k1[:, :], pw[:, 0:S], sig[:, 2, :], ALU.mult).then_inc(s_k1, 1)
                dve.wait_ge(s_pr, 7 * b + 5)
                dve.wait_ge(s_sig, 5 * b + 4)
                dve.scalar_tensor_tensor(cp[:, b, :], ps[:, 6, :], w["bias"][:, 4:5], sig[:, 3, :],
                                         ALU.add, ALU.mult).then_inc(s_cp, 1)
                if b + 2 < B:
                    affine(b + 2)
                copies(b)

        @block.scalar
        def _(act):
            act.wait_ge(weights_loaded, 16 * (len(w) - 1))
            eps = c["eps"]
            outer.root(act, eps, 0)
            outer.root(act, eps, 1)
            inner.root(act, eps, 0)
            inner.root(act, eps, 1)
            act.wait_ge(s_dv, 1)
            act.activation(erow[:, :], w["fi_row"][:, :], ACT.Exp, bias=col[:, 1:2], accum_out=col[:, 2:3]).then_inc(s_a, 1)
            act.activation(col[:, 3:4], w["fi_col"][:, 0:1], ACT.Exp, bias=col[:, 1:2]).then_inc(s_a, 1)
            act.activation(col[:, 4:5], w["log_decay"][:, 0:1], ACT.Sigmoid).then_inc(s_a, 1)
            act.activation(col[:, 5:6], w["dt"][:, 0:1], ACT.Sigmoid).then_inc(s_a, 1)
            outer.root(act, eps, 2)
            outer.root(act, eps, 3)
            inner.root(act, eps, 2)
            inner.root(act, eps, 3)
            for b in range(B):
                for k, (m, bias) in enumerate(((1, 0), (2, 1), (3, 2), (6, 3), (7, 5))):
                    act.wait_ge(s_pr, 7 * b + m)
                    if b:
                        if k == 0:
                            act.wait_ge(s_u, b)
                        elif k == 1:
                            act.wait_ge(s_k1, b)
                        elif k == 3:
                            act.wait_ge(s_cp, b)
                    dst = sig[:, k, :] if k < 4 else gate[:, b, :]
                    act.activation(dst, ps[:, PROJ[m - 1][1], :], ACT.Sigmoid,
                                   bias=w["bias"][:, bias:bias + 1]).then_inc(s_sig, 1)
                if b == 0:
                    act.wait_ge(s_red, 1)
                    act.activation(wave[:, :], angle, ACT.Sin).then_inc(s_wave, 1)

        @block.gpsimd
        def _(pool):
            ch = Chain(pool, s_pool)
            pool.wait_ge(weights_loaded, 16 * (len(w) - 1))
            pool.wait_ge(s_a, 4)
            pool.wait_ge(s_dv, 2)
            ch.link(pool.tensor_scalar(col[:, 7:8], col[:, 3:4], col[:, 6:7], float(NF), ALU.mult, ALU.mult))
            pool.tensor_tensor(col[:, 8:9], col[:, 7:8], col[:, 4:5], ALU.mult).then_inc(s_decay, 1)
            ch.link(pool.tensor_scalar(col[:, 9:10], w["freq"][:, 0:1], 0.1, None, ALU.mult))
            ch.link(pool.tensor_scalar(col[:, 10:11], col[:, 5:6], col[:, 9:10], 2.0, ALU.mult, ALU.mult))
            ch.link(pool.tensor_scalar(angle, w["steps"][:, :], col[:, 10:11], w["quarter"][:, 0:1],
                                       ALU.mult, ALU.add))
            ch.link(pool.tensor_scalar(turn, angle, 1 / TWO_PI, ROUND, ALU.mult, ALU.add))
            ch.link(pool.tensor_scalar(turn, turn, ROUND, None, ALU.subtract))
            for whole_turn in (TWO_PI_HI, TWO_PI - TWO_PI_HI):
                ch.link(pool.tensor_scalar(turned, turn, whole_turn, None, ALU.mult))
                ch.link(pool.tensor_tensor(angle, angle, turned, ALU.subtract))
            pool.tensor_scalar(angle, angle, PI_BELOW, -PI_BELOW, ALU.min, ALU.max).then_inc(s_red, 1)
            pool.wait_ge(s_wave, 1)
            for b in range(B):
                pool.wait_ge(s_k1, b + 1)
                if b >= 2:
                    pool.wait_ge(s_kt, b - 1)
                pool.tensor_tensor(kT[:, b % 2, :], k1[:, :], wave[:, :], ALU.mult).then_inc(s_k, 1)

        @block.tensor
        def _(pe):
            pe.wait_ge(weights_loaded, 16 * (len(w) - 1))
            def transposed(b):
                pe.wait_ge(inner.s_done, TPB * (b + 1))
                if b >= 2:
                    pe.wait_ge(s_tc, b - 1)
                for t in range(TPB):
                    mm = pe.transpose(ps[:, b % 2, t * P:(t + 1) * P], xh[:, b * TPB + t, :], c["ident"][:, :])
                mm.then_inc(s_t, 1)

            def by_token(b):
                for bank, s, ready, src in ((3, s_ut, s_u, uT), (4, s_kt, s_k, kT)):
                    pe.wait_ge(ready, b + 1)
                    pe.wait_ge(s_sig, 5 * b + 3)
                    for t in range(TPB):
                        mm = pe.transpose(ps[:, bank, t * P:(t + 1) * P], src[:, b % 2, t * P:(t + 1) * P],
                                          c["ident"][:, :])
                    mm.then_inc(s, 1)

            transposed(0)
            transposed(1)
            for b in range(B):
                pe.wait_ge(s_tc, b + 1)
                for m, (_, bank) in enumerate(PROJ):
                    if b and m == 0:
                        pe.wait_ge(s_sig, 5 * b)
                    elif b and m == 1:
                        pe.wait_ge(s_uc, b)
                    elif b and m == 2:
                        pe.wait_ge(s_kc, b)
                    elif b and m == 3:
                        pe.wait_ge(s_u, b)
                    elif b and m == 4:
                        pe.wait_ge(s_cp, b)
                    elif m == 6:
                        pe.wait_ge(s_sig, 5 * b + 1)
                    pe.matmul(ps[:, bank, :], w["wproj"][:, m * P:(m + 1) * P], xnT[:, b % 2, :],
                              start=True, stop=True).then_inc(s_pr, 1)
                if b + 2 < B:
                    transposed(b + 2)
                by_token(b)


def ssm_convolve(nc, ps, w, U, K, spec, tables_loaded, router):
    with ExitStack() as ctx:
        def sb(name, shape, dt=F32):
            return ctx.enter_context(nc.sbuf_tensor(f"cv_{name}", shape, dt))

        sem = phase_semaphores(nc, ctx, "cv")

        H = COLS // 2
        forward, inverse_table = (
            w["tables"][:, n * R4 * KT * KT * 3 * P:(n + 1) * R4 * KT * KT * 3 * P].rearrange(
                "p (k r g j c) -> p k r g j c", k=KT, r=R4, g=KT, j=3) for n in range(2))
        fold = [sb(f"fold{k}", [P, KT, 2, COLS]) for k in range(2)]
        uf = sb("uf", [P, 2, COLS])
        prod = sb("prod", [P, 2, 2, COLS])
        free = router.rows[:, :, :, :].rearrange("p k t o -> p (k t o)")
        Y = free[:, 0:4 * COLS].rearrange("p (n c) -> p n c", c=COLS)
        even = free[:, 4 * COLS:6 * COLS].rearrange("p (k c) -> p k c", c=COLS)
        odd = free[:, 6 * COLS:8 * COLS].rearrange("p (k c) -> p k c", c=COLS)
        sums = U[:, :, :, :, :].rearrange("p (s k) c b n -> p s k (c b n)", s=2)
        s_fold = [sem("folded0"), sem("folded1")]
        s_f = sem("transformed")
        s_uf, s_pr, s_y = sem("uf_copied"), sem("products"), sem("Y")
        s_z, s_zc, s_cb, s_sp = sem("inverse"), sem("inverse_copied"), sem("combined"), sem("spectral")
        ORDER = (0, 2, 1, 3)
        flat = lambda a, t: a[:, t, :, :, :].rearrange("p c b n -> p (c b n)")
        part = lambda a, mt, cc: a[:, mt, cc * H:(cc + 1) * H].rearrange("p (b n) -> p b n", n=NF)
        to = lambda t, cc: spec[:, t, :, cc, :]
        bankU = lambda n: ps[:, n % 2, :]
        bankK = lambda n: ps[:, 2 + n % 2, :]
        bankZ = lambda q, mt: ps[:, 4 + 2 * (q % 2) + mt, :]
        block = ctx.enter_context(nc.Block())

        def folds(eng, k, src):
            for q, r in enumerate(ORDER):
                if q >= 2:
                    eng.wait_ge(s_f, 4 * (q - 1))
                for kt in range(KT):
                    a, z, o = flat(src, kt), flat(src, KT + kt), fold[k][:, kt, q % 2, :]
                    if r % 2 == 0:
                        m = eng.tensor_tensor(o, a, z, ALU.subtract if r else ALU.add)
                    else:
                        ops = (ALU.add, ALU.subtract) if r == 1 else (ALU.subtract, ALU.add)
                        eng.tensor_tensor(o[:, 0:H], a[:, 0:H], z[:, H:COLS], ops[0])
                        m = eng.tensor_tensor(o[:, H:COLS], a[:, H:COLS], z[:, 0:H], ops[1])
                m.then_inc(s_fold[k], 1)
                yield

        @block.vector
        def _(dve):
            step = folds(dve, 0, U)
            next(step)
            next(step)

            def multiply(n):
                dve.wait_ge(s_f, 2 * n + 2)
                dve.wait_ge(s_uf, n + 1)
                if n >= 2:
                    dve.wait_ge(s_y, 2 * (n - 1))
                u, k, p = uf[:, n % 2, :], bankK(n), prod[:, n % 2, :, :]
                for half in range(2):
                    dve.tensor_tensor(p[:, 0, half * H:(half + 1) * H], u[:, half * H:(half + 1) * H], k[:, 0:H], ALU.mult)
                    m = dve.tensor_tensor(p[:, 1, half * H:(half + 1) * H], u[:, (1 - half) * H:(2 - half) * H],
                                          k[:, H:COLS], ALU.mult)
                m.then_inc(s_pr, 1)

            def combine(q):
                for mt in range(KT):
                    dve.wait_ge(s_z, KT * q + mt + 1)
                    if mt == 0:
                        dve.wait_ge(s_zc, KT * (q // 2 + 1))
                    z, e = bankZ(q, mt), (even if q == 1 else odd)[:, mt, :]
                    dve.tensor_tensor(sums[:, q // 2, mt, :], e, z, ALU.add).then_inc(s_cb, 1)
                    dve.tensor_tensor(e, e, z, ALU.subtract).then_inc(s_cb, 1)

            for q in range(R4):
                for gt in range(KT):
                    multiply(KT * q + gt)
                if q < 2:
                    next(step)
                if q == 2:
                    dve.wait_ge(s_fold[0], R4)
                    combine(1)
            combine(3)
            dve.wait_ge(s_cb, 8)
            for mt in range(KT):
                dve.tensor_tensor(to(KT + mt, 0), part(even, mt, 0), part(odd, mt, 1), ALU.subtract)
                m = dve.tensor_tensor(to(KT + mt, 1), part(even, mt, 1), part(odd, mt, 0), ALU.add)
            m.then_inc(s_sp, 1)

        @block.gpsimd
        def _(pool):
            step = folds(pool, 1, K)
            next(step)
            next(step)
            for n in range(R4 * KT):
                pool.wait_ge(s_pr, n + 1)
                if n >= 4:
                    pool.wait_ge(s_z, KT * ((n - 4) // KT + 1))
                p, y = prod[:, n % 2, :, :], Y[:, n % 4, :]
                pool.tensor_tensor(y[:, 0:H], p[:, 0, 0:H], p[:, 1, 0:H], ALU.subtract).then_inc(s_y, 1)
                pool.tensor_tensor(y[:, H:COLS], p[:, 0, H:COLS], p[:, 1, H:COLS], ALU.add).then_inc(s_y, 1)
                if n in (1, 3):
                    next(step)
            pool.wait_ge(s_cb, 8)
            for mt in range(KT):
                for cc in range(2):
                    m = pool.tensor_tensor(to(mt, cc), part(sums[:, 0], mt, cc), part(sums[:, 1], mt, cc), ALU.add)
            m.then_inc(s_sp, 1)

        @block.scalar
        def _(act):
            def z_copy(q, dst):
                for mt in range(KT):
                    act.wait_ge(s_z, KT * q + mt + 1)
                    act.activation(dst[:, mt, :], bankZ(q, mt), ACT.Copy).then_inc(s_zc, 1)

            for n in range(R4 * KT):
                act.wait_ge(s_f, 2 * n + 1)
                if n >= 2:
                    act.wait_ge(s_pr, n - 1)
                act.activation(uf[:, n % 2, :], bankU(n), ACT.Copy).then_inc(s_uf, 1)
                if n == 3:
                    z_copy(0, even)
                if n == 7:
                    z_copy(2, odd)

        @block.tensor
        def _(pe):
            pe.wait_ge(tables_loaded, 16 * TABLE_PIECES)

            def transform(q, gt, k):
                r, n = ORDER[q], KT * q + gt
                bank = (bankU if k == 0 else bankK)(n)
                pe.wait_ge(s_fold[k], q + 1)
                if n >= 2:
                    if k == 0:
                        pe.wait_ge(s_uf, n - 1)
                    else:
                        pe.wait_ge(s_pr, n - 1)
                v = fold[k][:, :, q % 2, :]
                tab = lambda kt, j: forward[:, kt, r, gt, j, :]
                pe.matmul(bank, tab(0, 0), v[:, 0, :], start=True, stop=False)
                for kt in range(KT):
                    pe.matmul(bank[:, 0:H], tab(kt, 1), v[:, kt, H:COLS], start=False, stop=False,
                              skip_group_check=True)
                    pe.matmul(bank[:, H:COLS], tab(kt, 2), v[:, kt, 0:H], start=False, stop=False,
                              skip_group_check=True)
                pe.matmul(bank, tab(1, 0), v[:, 1, :], start=False, stop=True).then_inc(s_f, 1)

            def inverse(q):
                r = ORDER[q]
                pe.wait_ge(s_y, 2 * KT * (q + 1))
                if q == 2:
                    pe.wait_ge(s_zc, KT)
                if q == 3:
                    pe.wait_ge(s_cb, 4)
                for mt in range(KT):
                    bank = bankZ(q, mt)
                    tab = lambda gt, j: inverse_table[:, gt, r, mt, j, :]
                    y = lambda gt: Y[:, (KT * q + gt) % 4, :]
                    pe.matmul(bank, tab(0, 0), y(0), start=True, stop=False)
                    for gt in range(KT):
                        pe.matmul(bank[:, 0:H], tab(gt, 2), y(gt)[:, H:COLS], start=False, stop=False,
                                  skip_group_check=True)
                        pe.matmul(bank[:, H:COLS], tab(gt, 1), y(gt)[:, 0:H], start=False, stop=False,
                                  skip_group_check=True)
                    pe.matmul(bank, tab(1, 0), y(1), start=False, stop=True).then_inc(s_z, 1)

            for q in range(R4):
                for gt in range(KT):
                    transform(q, gt, 0)
                    transform(q, gt, 1)
                if q:
                    inverse(q - 1)
            inverse(R4 - 1)


def ssm_output(nc, ps, x, c, w, xi, cp, gate, spec, U, K, router):
    with ExitStack() as ctx:
        def sb(name, shape, dt=F32):
            return ctx.enter_context(nc.sbuf_tensor(f"so_{name}", shape, dt))

        sem = phase_semaphores(nc, ctx, "so")

        ln = Moments(sb, sem, "ln")
        xh = U[:, :, :, :, :].rearrange("p t c (b h) n -> p (t c b) (h n)", h=2)
        free = K[:, :, :, :, :].rearrange("p t c b n -> p t (c b n)")
        specT, gated = free[:, 0:2, :], free[:, 2:4, :]
        scale = sb("scale", [P, 1])
        xnT = sb("xnT", [P, 2, S])
        hid = sb("hid", [P, 2, FT, S])
        s_ch = sem("dve_chain")
        s_st, s_sc, s_yp = sem("specT_psum"), sem("specT_copied"), sem("y_psum")
        s_ga, s_gt, s_xi = sem("gated"), sem("gated_psum"), sem("xi")
        s_t, s_tc, s_h, s_hg = sem("xnT_psum"), sem("xnT"), sem("hidden_psum"), sem("hidden")
        s_o, s_x, s_xs = sem("out_psum"), sem("x"), sem("x_xi")
        router.begin(sem, x, ps[:, 1, :], ps[:, 7, :])
        block = ctx.enter_context(nc.Block())

        @block.vector
        def _(dve):
            ch = Chain(dve, s_ch)
            ch.link(dve.tensor_scalar(scale[:, :], w["output_scale"][:, 0:1], 0.5, None, ALU.mult))
            for b in range(B):
                dve.wait_ge(s_yp, b + 1)
                if b >= 2:
                    dve.wait_ge(s_gt, b - 1)
                ch.link(dve.scalar_tensor_tensor(gated[:, b % 2, :], ps[:, 2 + b % 2, :], scale[:, 0:1], gate[:, b, :],
                                                 ALU.mult, ALU.mult))
                dve.scalar_tensor_tensor(gated[:, b % 2, :], cp[:, b, :], 0.5, gated[:, b % 2, :],
                                         ALU.mult, ALU.add).then_inc(s_ga, 1)
                dve.wait_ge(s_gt, b + 1)
                xb = xi[:, b * TPB:(b + 1) * TPB, :]
                dve.tensor_tensor(xb, ps[:, 4 + b % 2, :].rearrange("p (t d) -> p t d", d=D), xb, ALU.add).then_inc(s_xi, 1)
                dve.wait_ge(s_xi, b + 1)
                ln.moments(dve, xi, b)
                if b:
                    ln.normalize(dve, xh, xi, b - 1)
            ln.normalize(dve, xh, xi, B - 1)

            def affine(b):
                dve.wait_ge(s_t, b + 1)
                if b >= 2:
                    dve.wait_ge(s_h, FT * (b - 1))
                dve.tensor_scalar(xnT[:, b % 2, :], ps[:, 0, :], w["norm2_gb"][:, 0:1], w["norm2_gb"][:, 1:2],
                                  ALU.mult, ALU.add).then_inc(s_tc, 1)

            def add(b):
                dve.wait_ge(s_o, b + 1)
                dve.wait_ge(s_xs, 2 * (b + 1))
                xb = x[:, b * TPB:(b + 1) * TPB, :]
                dve.tensor_tensor(xb, ps[:, 6, :].rearrange("p (t d) -> p t d", d=D), xb, ALU.add).then_inc(s_x, 1)
                dve.wait_ge(s_x, b + 1)
                router.moments(dve, b)

            router.start(dve)
            affine(0)
            affine(1)
            affine(2)
            add(0)
            router.normalize(dve, 0)
            affine(3)
            add(1)
            router.choose(dve, 0)
            router.normalize(dve, 1)
            add(2)
            router.slots(dve, 0)
            router.normalize(dve, 2)
            router.choose(dve, 1)
            add(3)
            router.slots(dve, 1)
            router.normalize(dve, 3)
            router.choose(dve, 2)
            router.slots(dve, 2)
            router.choose(dve, 3)
            router.slots(dve, 3)
            router.plan(dve)

        @block.sync
        def _(sp):
            router.pads(sp)

        @block.gpsimd
        def _(pool):
            router.numbers(pool)
            for b in range(B):
                xb = x[:, b * TPB:(b + 1) * TPB, :]
                pool.wait_ge(s_xi, b + 1)
                pool.tensor_tensor(xb, xb, xi[:, b * TPB:(b + 1) * TPB, :], ALU.add).then_inc(s_xs, 1)
                pool.wait_ge(s_xs, 2 * b + 1)
                pool.tensor_tensor(xb, xb, bc(w["b2"][:, :], TPB, 1), ALU.add).then_inc(s_xs, 1)
            for group in range(B):
                router.scatter(pool, group, 0)
                router.scatter(pool, group, 1)

        @block.scalar
        def _(act):
            for b in range(B):
                act.wait_ge(s_st, b + 1)
                if b >= 2:
                    act.wait_ge(s_yp, b - 1)
                act.activation(specT[:, b % 2, :], ps[:, b % 2, :], ACT.Copy).then_inc(s_sc, 1)
                if b:
                    ln.root(act, c["eps"], b - 1)
            ln.root(act, c["eps"], B - 1)
            def gelu(b):
                for f in range(FT):
                    act.wait_ge(s_h, FT * b + f + 1)
                    if b >= 2 and f == 0:
                        act.wait_ge(s_o, b - 1)
                    act.activation(hid[:, b % 2, f, :], ps[:, 2 + f, :], ACT.Gelu,
                                   bias=w["b1"][:, f:f + 1]).then_inc(s_hg, 1)

            gelu(0)
            gelu(1)
            router.deviation(act, 0)
            gelu(2)
            router.copies(act, 0)
            router.deviation(act, 1)
            gelu(3)
            router.copies(act, 1)
            router.deviation(act, 2)
            router.deviation(act, 3)
            router.copies(act, 2)
            router.copies(act, 3)
            router.gap_exponentials(act)

        @block.tensor
        def _(pe):
            def spectral(b):
                if b >= 2:
                    pe.wait_ge(s_sc, b - 1)
                for t in range(TPB):
                    mm = pe.transpose(ps[:, b % 2, t * P:(t + 1) * P],
                                      spec[:, t, b, :, :].rearrange("p c n -> p (c n)"), c["ident"][:, :])
                mm.then_inc(s_st, 1)

            def project(b):
                pe.wait_ge(s_sc, b + 1)
                if b >= 2:
                    pe.wait_ge(s_ga, b - 1)
                pe.matmul(ps[:, 2 + b % 2, :], w["wfs"][:, :], specT[:, b % 2, :], start=True, stop=True).then_inc(s_yp, 1)

            def by_token(b):
                pe.wait_ge(s_ga, b + 1)
                if b >= 2:
                    pe.wait_ge(s_xi, b - 1)
                for t in range(TPB):
                    mm = pe.transpose(ps[:, 4 + b % 2, t * P:(t + 1) * P], gated[:, b % 2, t * P:(t + 1) * P],
                                      c["ident"][:, :])
                mm.then_inc(s_gt, 1)

            spectral(0)
            for b in range(B):
                if b + 1 < B:
                    spectral(b + 1)
                project(b)
                by_token(b)

            def transposed(b):
                pe.wait_ge(ln.s_done, TPB * (b + 1))
                if b:
                    pe.wait_ge(s_tc, b)
                for t in range(TPB):
                    mm = pe.transpose(ps[:, 0, t * P:(t + 1) * P], xh[:, b * TPB + t, :], c["ident"][:, :])
                mm.then_inc(s_t, 1)

            def hidden(b):
                pe.wait_ge(s_tc, b + 1)
                for f in range(FT):
                    if b:
                        pe.wait_ge(s_hg, FT * (b - 1) + f + 1)
                    pe.matmul(ps[:, 2 + f, :], w["w1"][:, f * P:(f + 1) * P], xnT[:, b % 2, :],
                              start=True, stop=True).then_inc(s_h, 1)

            def out(b):
                pe.wait_ge(s_hg, FT * (b + 1))
                if b:
                    pe.wait_ge(s_x, b)
                for t in range(TPB):
                    for f in range(FT):
                        mm = pe.matmul(ps[:, 6, t * P:(t + 1) * P], hid[:, b % 2, f, t * P:(t + 1) * P],
                                       w["w2"][:, f, :], start=(f == 0), stop=(f == FT - 1))
                mm.then_inc(s_o, 1)

            transposed(0)
            transposed(1)
            hidden(0)
            transposed(2)
            hidden(1)
            out(0)
            transposed(3)
            hidden(2)
            pe.wait_ge(s_sc, B)
            router.transposes(pe, 0)
            out(1)
            router.logits(pe, 0)
            hidden(3)
            out(2)
            router.transposes(pe, 1)
            router.ranks(pe, 0)
            out(3)
            router.logits(pe, 1)
            router.transposes(pe, 2)
            router.ranks(pe, 1)
            router.logits(pe, 2)
            router.transposes(pe, 3)
            router.ranks(pe, 2)
            router.logits(pe, 3)
            router.ranks(pe, 3)
            router.totals(pe)


def constants():
    f = np.float32
    k = np.arange(P)
    rows = lambda a: np.ascontiguousarray(np.broadcast_to(np.asarray(a, f).reshape(1, -1), (P, np.size(a))))
    return {
        "ident": np.eye(P, dtype=f),
        "before": (k[:, None] < k[None, :]).astype(f),
        "falling": rows(np.arange(NE, 0, -1)),
        "region": rows(np.arange(NE) * REGION),
        "row_number": np.ascontiguousarray((np.arange(2 * NT)[None, :] * P + k[:, None]).astype(f)),
        "slot_tile": rows(np.arange(NSLOT)),
        "mask_q": np.where(k[None, :] > k[:, None], MASKED, 0).astype(f),
    }


def pad_rows():
    rows = np.zeros((2 * NE * P, ROW), np.float32)
    rows[:, D] = 2 * NT * P + np.arange(len(rows))
    return rows


def place_constants(nc, ctx, dram):
    c = {k: ctx.enter_context(nc.sbuf_tensor(f"c_{k}", list(v.shape), F32)) for k, v in dram.items()}
    for name, shape, dt in (("eps", [P, 1], F32), ("one", [P, NE], F32),
                            ("ones_bf", [P, P], BF16), ("before_bf", [P, P], BF16), ("ident_bf", [P, P], BF16),
                            ("mask_q_bf", [P, P], BF16), ("zero_rows", [KROWS - MROW, S], BF16),
                            ("one_rows", [KROWS - MROW, S], BF16)):
        c[name] = ctx.enter_context(nc.sbuf_tensor(f"c_{name}", shape, dt))
    s_const = ctx.enter_context(nc.semaphore("constants_loaded"))

    def load(block):
        @block.gpsimd
        def _(pool):
            pool.memset(c["zero_rows"][:, :], 0.0)
            pool.memset(c["one_rows"][:, :], 1.0)

        @block.vector
        def _(dve):
            dve.memset(c["eps"][:, :], EPS)
            dve.memset(c["one"][:, :], 1.0)
            dve.memset(c["ones_bf"][:, :], 1.0)
            dve.wait_ge(s_const, 16 * len(dram))
            dve.tensor_copy(c["before_bf"][:, :], c["before"][:, :])
            for k in ("ident", "mask_q"):
                dve.tensor_copy(c[k + "_bf"][:, :], c[k][:, :])

    return c, load, s_const


def rotary():
    f = np.float32
    half = DH // 2
    inv = (1.0 / f(10000.0) ** (np.arange(half, dtype=f) / half)).astype(f)
    angle = (np.arange(S, dtype=f)[:, None] * inv[None, :]).astype(f)
    row = np.arange(P) % DH
    cos, sin = np.cos(angle)[:, row // 2].T, np.sin(angle)[:, row // 2].T
    sin = sin * np.where(row % 2, 1, -1)[:, None]
    r = 1 / np.sqrt(f(DH))
    return np.ascontiguousarray(np.stack([cos * r, sin * r, cos, sin], 1).astype(f))


def transform_tables():
    k = np.arange(HALF)
    out = []
    for inverse in range(2):
        tab = np.empty((P, KT, R4, KT, 3, P), np.float64)
        for r in range(R4):
            turns = np.outer(k, R4 * k + r)
            turns = (turns.T if inverse else turns) % NFFT
            a = turns * (TWO_PI / NFFT)
            for j, m in enumerate((np.cos(a), np.sin(a), -np.sin(a))):
                tab[:, :, r, :, j, :] = m.reshape(KT, P, KT, P).transpose(1, 0, 2, 3)
        out.append((tab / (NFFT if inverse else 1)).astype(np.float32))
    return out


def padded(a, n):
    return np.ascontiguousarray(np.pad(a, ((0, 0), (0, -a.shape[1] % n))))


def ssm_weights(inputs):
    g = lambda name: np.asarray(inputs[f"L0_attn_b_{name}"])
    twice = lambda a: np.concatenate([a, a], 0)
    col = lambda a: np.ascontiguousarray(a.reshape(-1, 1))
    band = lambda a: twice(np.repeat(a, NF // NB, 0))
    every = lambda a: np.repeat(a, P, 0)
    f = np.float32
    proj = [twice(g("Wfg")), band(g("Wband")), every(g("Wtg")), g("Wsp"), g("Wconcept"), g("Wcg"), g("Wgate")]
    bias = [twice(g("bfg")), band(g("bband")), every(g("btg")), g("bcg"), g("bconcept"), g("bgate")]
    return {
        "wproj": np.ascontiguousarray(np.concatenate(proj, 0).T),
        "bias": np.ascontiguousarray(np.stack(bias, 1)),
        "norm_gb": np.ascontiguousarray(np.stack([g("norm_g"), g("norm_b")], 1)),
        "norm2_gb": np.ascontiguousarray(np.stack([g("norm2_g"), g("norm2_b")], 1)),
        "fi_row": np.ascontiguousarray(np.broadcast_to(g("freq_importance")[None, :], (P, NF))),
        "fi_col": col(twice(g("freq_importance"))),
        "log_decay": col(twice(g("log_decay"))),
        "dt": col(twice(g("dt"))),
        "freq": col(twice(g("frequencies"))),
        "steps": np.ascontiguousarray(np.broadcast_to(np.arange(1, S + 1, dtype=f)[None, :], (P, S))),
        "quarter": col(np.repeat(np.array([np.pi / 2, 0], f), NF)),
        "output_scale": col(every(g("output_scale"))),
        "wfs": np.ascontiguousarray(g("Wfs").T),
        "w1": np.ascontiguousarray(g("W1").T),
        "b1": np.ascontiguousarray(g("b1").reshape(FT, P).T),
        "w2": np.ascontiguousarray(g("W2").reshape(D, FT, P).transpose(2, 1, 0)),
        "b2": np.ascontiguousarray(np.broadcast_to(g("b2")[None, :], (P, D))),
        "tables": padded(np.concatenate([t.reshape(P, -1) for t in transform_tables()], 1), TABLE_PIECES),
    }


def ssm(nc, ps, x, c, w, s_w, s_tab, router):
    with ExitStack() as ctx:
        def sb(name, shape, dt=F32):
            return ctx.enter_context(nc.sbuf_tensor(f"sm_{name}", shape, dt))

        xi, xh = sb("xi", [P, NT, D]), sb("xh", [P, NT, D])
        cp, gate = sb("cp", [P, B, S]), sb("gate", [P, B, S])
        U, K = sb("U", [P, TPB, 2, B, NF]), sb("K", [P, TPB, 2, B, NF])
        spec = xh[:, :, :].rearrange("p (t b) (c n) -> p t b c n", b=B, n=NF)
        ssm_project(nc, ps, x, c, w, xi, xh, cp, gate, U, K, s_w)
        ssm_convolve(nc, ps, w, U, K, spec, s_tab, router)
        ssm_output(nc, ps, x, c, w, xi, cp, gate, spec, U, K, router)


def attention_weights(inputs):
    g = lambda name: np.asarray(inputs[f"L0_attn_a_{name}"])
    swap = np.arange(P) ^ 1
    rows = lambda a: np.ascontiguousarray(np.broadcast_to(a[None, :], (P, P)))
    wq, wk, bq, bk = g("Wq"), g("Wk"), g("bq"), g("bk")
    return {
        "wqk": np.ascontiguousarray(np.concatenate([wq, wq[swap], wk, wk[swap]], 0).T),
        "qk_bias": np.ascontiguousarray(np.stack([bq, bq[swap], bk, bk[swap]], 1)),
        "rotary": rotary(),
        "wv": np.ascontiguousarray(g("Wv").T),
        "wo": np.ascontiguousarray(g("Wo").T),
        "bv": rows(g("bv")),
        "bo": rows(g("bo")),
    }


def moe_weights(inputs):
    g = lambda name: np.asarray(inputs[f"L0_ffn_{name}"])
    return {
        "w1": np.ascontiguousarray(g("W1").transpose(2, 0, 1).reshape(P, NE * DFF)),
        "w2": np.ascontiguousarray(g("W2").reshape(NE, D, FT, P).transpose(3, 0, 2, 1).reshape(P, NE * DFF)),
        "wr": np.ascontiguousarray(g("Wr").T),
    }


def whole(nc, x_dram, out_dram, pads, consts, att, ssm_w, moe_w):
    whole_of = lambda t: t[tuple([slice(None)] * len(t.shape))]
    with ExitStack() as ctx:
        ps = ctx.enter_context(nc.psum_tensor("ps", [P, 8, S], F32))
        x = ctx.enter_context(nc.sbuf_tensor("x", [P, NT, D], F32))
        mw = {k: ctx.enter_context(nc.sbuf_tensor(f"moe_{k}", list(v.shape), F32)) for k, v in moe_w.items()}
        c, load, s_const = place_constants(nc, ctx, consts)
        s_x = ctx.enter_context(nc.semaphore("x_loaded"))
        s_aw = ctx.enter_context(nc.semaphore("attention_weights_loaded"))
        s_mw = ctx.enter_context(nc.semaphore("moe_weights_loaded"))
        s_sw = ctx.enter_context(nc.semaphore("ssm_weights_loaded"))
        s_tab = ctx.enter_context(nc.semaphore("ssm_tables_loaded"))
        xs = nc.dram_tensor("expert_rows", [NE * (REGION + P), ROW], F32, kind="Internal").ap()
        ys = nc.dram_tensor("expert_results", [2 * (NT + NE) * P, D], F32, kind="Internal").ap()
        parts = nc.dram_tensor("parts", [B, 2, 3, P, S], BF16, kind="Internal").ap()
        router = Router(nc, ctx, c, mw, pads, xs, s_mw)
        x_rows = x_dram.rearrange("b (t p) d -> p (b t) d", p=P)
        out_rows = out_dram.rearrange("b (t p) d -> p (b t) d", p=P)

        with ExitStack() as actx:
            w = {k: actx.enter_context(nc.sbuf_tensor(f"w_{k}", list(v.shape), F32)) for k, v in att.items()}
            hatq = actx.enter_context(nc.sbuf_tensor("hatq", [KROWS, 2, NH, S], BF16))
            hatk = actx.enter_context(nc.sbuf_tensor("hatk", [KROWS, 2, NH, S], BF16))
            vall = actx.enter_context(nc.sbuf_tensor("vall", [P, NT, D], F32))
            s_hat = {k: actx.enter_context(nc.semaphore(f"hat_{k}")) for k in (0, 1, "fill")}
            with nc.Block() as block:
                @block.sync
                def _(sp):
                    sp.dma_start(x[:, :, :], x_rows).then_inc(s_x, 16)
                    for k, v in consts.items():
                        sp.dma_start(c[k][:, :], v).then_inc(s_const, 16)
                    for k, v in w.items():
                        sp.dma_start(whole_of(v), att[k]).then_inc(s_aw, 16)

                load(block)
            def load_moe_weights(sp):
                for k, v in mw.items():
                    sp.dma_start(whole_of(v), moe_w[k]).then_inc(s_mw, 16)

            attention_prepare(nc, ps, x, c, w, parts, hatq, hatk, vall, s_hat, s_x, s_aw)
            attention(nc, ps, x, c, w, parts, hatq, hatk, vall, s_hat, router, load_moe_weights)
        sw = {k: ctx.enter_context(nc.sbuf_tensor(f"ssm_{k}", list(v.shape), F32)) for k, v in ssm_w.items()}

        def load_ssm_weights(sp, i):
            small = [k for k in sw if k != "tables"]
            if isinstance(i, int) and i < 4:
                return
            if isinstance(i, int) and i < 8:
                for k in small[i - 4::4]:
                    sp.dma_start(whole_of(sw[k]), ssm_w[k]).then_inc(s_sw, 16)
            n = ssm_w["tables"].shape[1] // TABLE_PIECES
            at = bass.ds((i - 4) * n, n)
            sp.dma_start(sw["tables"][:, at], ssm_w["tables"][:, at]).then_inc(s_tab, 16)

        moe(nc, "moe0", ps, x, c, mw, router, xs, ys, prefetch=load_ssm_weights)
        ssm(nc, ps, x, c, sw, s_sw, s_tab, router)
        moe(nc, "moe1", ps, x, c, mw, router, xs, ys, out=out_rows)


def kernel(**inputs):
    import concourse.bacc as bacc
    from concourse.bass_utils import run_bass_kernel_spmd

    nc = bacc.Bacc("TRN2", target_bir_lowering=False, num_devices=1)
    groups = {"c": constants(), "att": attention_weights(inputs), "ssm": ssm_weights(inputs), "moe": moe_weights(inputs)}
    arrays, aps = {}, {}
    for g, members in groups.items():
        aps[g] = {}
        for k, a in members.items():
            arrays[f"{g}_{k}_dram"] = a
            aps[g][k] = nc.dram_tensor(f"{g}_{k}_dram", a.shape, F32, kind="ExternalInput").ap()
    arrays["x_dram"] = np.ascontiguousarray(inputs["L0_attn_a_x"])
    x = nc.dram_tensor("x_dram", [B, S, D], F32, kind="ExternalInput").ap()
    out = nc.dram_tensor("out_dram", [B, S, D], F32, kind="ExternalOutput").ap()
    arrays["pad_rows_dram"] = pad_rows()
    pads = nc.dram_tensor("pad_rows_dram", [2 * NE * P, ROW], F32, kind="ExternalInput").ap()
    whole(nc, x, out, pads, aps["c"], aps["att"], aps["ssm"], aps["moe"])
    r = run_bass_kernel_spmd(nc, [arrays], core_ids=[0])
    return r.results[0]["out_dram"]
```
